# Optimizing a Trainium2 kernel written in Bass

```python
import numpy as np
import jax
import jax.numpy as jnp

def _softmax(x, axis=-1):
    return jax.nn.softmax(x, axis=axis)

def _gelu(x):
    return jax.nn.gelu(x, approximate=True)

def _silu(x):
    return jax.nn.silu(x)

def _sigmoid(x):
    return jax.nn.sigmoid(x)

def _layernorm(x, axis=-1, eps=1e-05):
    m = jnp.mean(x, axis=axis, keepdims=True)
    v = jnp.var(x, axis=axis, keepdims=True)
    return (x - m) / jnp.sqrt(v + eps)

def _scatter_add(tgt, idx, src, axis=0):
    return tgt.at[idx].add(src)

def _segment_sum(src, seg, n):
    return jax.ops.segment_sum(src, seg, n)
kernel_name = 'mk_conv_seq_d4_conv_nchw16_r4_045031'

def setup_inputs(seed: int=0):
    np.random.seed(seed)
    _w = jnp.asarray

    def _rec_inputs():
        import jax
        import jax.numpy as jnp
        _gk = jax.random.key(seed)
        x = -0.0003929 + 0.9999 * jax.random.normal(jax.random.fold_in(_gk, 1), (16, 16, 32, 32), jnp.float32)
        return x
    x = _rec_inputs()

    def _L0_conv_setup():
        import jax, jax.numpy as jnp
        import numpy as np
        B, C, SZ, WS, PS, H = (16, 16, 32, 32, 8, 8)
        WN = SZ // WS
        PPW = WS // PS
        NWIN = WN * WN
        NPAT = PPW * PPW
        PD = PS * PS * C
        PDH = PD // H
        POOLED = PS * WN
        PLD = (POOLED // WN) ** 2 * C
        WDH = PLD // H
        WIN_INNER = WDH * H
        WD = WS * WS * C
        EPS = 1e-05

        def _ln(t, g, b):
            m = t.mean(-1, keepdims=True)
            v = jnp.mean((t - m) ** 2, -1, keepdims=True)
            return (t - m) * jax.lax.rsqrt(v + EPS) * g + b

        def _heads(t):
            return t.reshape(*t.shape[:-1], H, -1).swapaxes(-2, -3)

        def _merge(t):
            t = t.swapaxes(-2, -3)
            return t.reshape(*t.shape[:-2], -1)

        def _attn(xn, Wqk, dph):
            q, k = jnp.split(xn @ Wqk, 2, -1)
            q, k = (_heads(q), _heads(k))
            return jax.nn.softmax(jnp.einsum('...hqd,...hkd->...hqk', q, k) * dph ** (-0.5), -1)

        def _dwconv(t, w, b, res):
            lead, c = (t.shape[:-2], t.shape[-1])
            img = t.reshape(-1, res * res, c).transpose(0, 2, 1).reshape(-1, c, res, res)
            y = jax.lax.conv_general_dilated(img, w, (1, 1), 'SAME', feature_group_count=c, dimension_numbers=('NCHW', 'OIHW', 'NCHW'))
            y = y + b[None, :, None, None]
            return y.reshape(-1, c, res * res).transpose(0, 2, 1).reshape(*lead, res * res, c)
        k = jax.random.split(jax.random.key(seed), 12)
        p = lambda i, shape: jax.random.normal(k[i], shape, jnp.float32) * 0.02
        return dict(x=jax.random.normal(k[0], (B, C, SZ, SZ), jnp.float32), pn_g=jnp.ones((PD,), jnp.float32), pn_b=jnp.zeros((PD,), jnp.float32), Wqk_p=p(1, (PD, 2 * PD)), Wv_p=p(2, (PD, PD)), conv_p_w=p(3, (PDH, 1, 3, 3)), conv_p_b=jnp.zeros((PDH,), jnp.float32), Wout_p=p(4, (PD, PD)), pln_g=jnp.ones((PLD,), jnp.float32), pln_b=jnp.zeros((PLD,), jnp.float32), Wqk_w=p(5, (PLD, 2 * WIN_INNER)), wn_g=jnp.ones((WD,), jnp.float32), wn_b=jnp.zeros((WD,), jnp.float32), Wv_w=p(6, (WD, WIN_INNER)), conv_w_w=p(7, (WDH, 1, 3, 3)), conv_w_b=jnp.zeros((WDH,), jnp.float32), Wout_w=p(8, (WIN_INNER, WD)))
    _L0_conv_all = _L0_conv_setup()
    _L0_conv_in = {k: v for k, v in _L0_conv_all.items() if k in ('pn_g', 'pn_b', 'Wqk_p', 'Wv_p', 'conv_p_w', 'conv_p_b', 'Wout_p', 'pln_g', 'pln_b', 'Wqk_w', 'wn_g', 'wn_b', 'Wv_w', 'conv_w_w', 'conv_w_b', 'Wout_w')}
    del _L0_conv_all

    def _L1_conv_setup():
        import jax, jax.numpy as jnp
        import numpy as np

        def _conv2d_same(x, w, b):
            y = jax.lax.conv_general_dilated(x, w, window_strides=(1, 1), padding=((1, 1), (1, 1)), dimension_numbers=('NCHW', 'OIHW', 'NCHW'))
            return y + b[None, :, None, None]
        key = jax.random.key(seed)
        ks = jax.random.split(key, 5)
        B, C, H, W = (16, 16, 128, 128)
        K = 3
        bound = float(np.sqrt(1.0 / (C * K * K)))
        x = jax.random.normal(ks[0], (B, C, H, W), dtype=jnp.float32)
        w1 = jax.random.uniform(ks[1], (C, C, K, K), minval=-bound, maxval=bound, dtype=jnp.float32)
        b1 = jax.random.uniform(ks[2], (C,), minval=-bound, maxval=bound, dtype=jnp.float32)
        w2 = jax.random.uniform(ks[3], (C, C, K, K), minval=-bound, maxval=bound, dtype=jnp.float32)
        b2 = jax.random.uniform(ks[4], (C,), minval=-bound, maxval=bound, dtype=jnp.float32)
        return {'x': x, 'w1': w1, 'b1': b1, 'w2': w2, 'b2': b2}
    _L1_conv_all = _L1_conv_setup()
    _L1_conv_in = {k: v for k, v in _L1_conv_all.items() if k in ('w1', 'b1', 'w2', 'b2')}
    del _L1_conv_all

    def _L2_conv_setup():
        import jax, jax.numpy as jnp
        import numpy as np

        def _conv2d_same(x, w, b):
            y = jax.lax.conv_general_dilated(x, w, window_strides=(1, 1), padding=((1, 1), (1, 1)), dimension_numbers=('NCHW', 'OIHW', 'NCHW'))
            return y + b[None, :, None, None]
        key = jax.random.key(seed)
        ks = jax.random.split(key, 5)
        B, C, H, W = (16, 16, 128, 128)
        K = 3
        bound = float(np.sqrt(1.0 / (C * K * K)))
        x = jax.random.normal(ks[0], (B, C, H, W), dtype=jnp.float32)
        w1 = jax.random.uniform(ks[1], (C, C, K, K), minval=-bound, maxval=bound, dtype=jnp.float32)
        b1 = jax.random.uniform(ks[2], (C,), minval=-bound, maxval=bound, dtype=jnp.float32)
        w2 = jax.random.uniform(ks[3], (C, C, K, K), minval=-bound, maxval=bound, dtype=jnp.float32)
        b2 = jax.random.uniform(ks[4], (C,), minval=-bound, maxval=bound, dtype=jnp.float32)
        return {'x': x, 'w1': w1, 'b1': b1, 'w2': w2, 'b2': b2}
    _L2_conv_all = _L2_conv_setup()
    _L2_conv_in = {k: v for k, v in _L2_conv_all.items() if k in ('w1', 'b1', 'w2', 'b2')}
    del _L2_conv_all

    def _L3_conv_setup():
        import jax, jax.numpy as jnp
        import numpy as np
        SOBEL_X = jnp.array([[-1.0, 0.0, 1.0], [-2.0, 0.0, 2.0], [-1.0, 0.0, 1.0]], dtype=jnp.float32) / 8.0
        SOBEL_Y = jnp.array([[-1.0, -2.0, -1.0], [0.0, 0.0, 0.0], [1.0, 2.0, 1.0]], dtype=jnp.float32) / 8.0
        TIME_STEPS = 10
        DT = 0.01
        EPS = 1e-06

        def _dwconv(u, k2d):
            C = u.shape[1]
            k = jnp.broadcast_to(k2d[None, None], (C, 1, 3, 3))
            return jax.lax.conv_general_dilated(u, k, window_strides=(1, 1), padding=((1, 1), (1, 1)), dimension_numbers=('NCHW', 'OIHW', 'NCHW'), feature_group_count=C)

        def _derivs(u):
            ux = _dwconv(u, SOBEL_X)
            uy = _dwconv(u, SOBEL_Y)
            uxx = _dwconv(ux, SOBEL_X)
            uxy = _dwconv(ux, SOBEL_Y)
            uyy = _dwconv(uy, SOBEL_Y)
            c = lambda t: jnp.clip(t, -10.0, 10.0)
            return (c(ux), c(uy), c(uxx), c(uxy), c(uyy))
        key = jax.random.key(seed)
        x = jax.random.normal(key, (8, 16, 128, 128), dtype=jnp.float32)
        return {'x': x, 'alpha_param': jnp.float32(0.1), 'beta_param': jnp.float32(0.01)}
    _L3_conv_all = _L3_conv_setup()
    _L3_conv_in = {k: v for k, v in _L3_conv_all.items() if k in ('alpha_param', 'beta_param')}
    del _L3_conv_all
    return {'x': x, 'L0_conv_pn_g': _L0_conv_in['pn_g'], 'L0_conv_pn_b': _L0_conv_in['pn_b'], 'L0_conv_Wqk_p': _L0_conv_in['Wqk_p'], 'L0_conv_Wv_p': _L0_conv_in['Wv_p'], 'L0_conv_conv_p_w': _L0_conv_in['conv_p_w'], 'L0_conv_conv_p_b': _L0_conv_in['conv_p_b'], 'L0_conv_Wout_p': _L0_conv_in['Wout_p'], 'L0_conv_pln_g': _L0_conv_in['pln_g'], 'L0_conv_pln_b': _L0_conv_in['pln_b'], 'L0_conv_Wqk_w': _L0_conv_in['Wqk_w'], 'L0_conv_wn_g': _L0_conv_in['wn_g'], 'L0_conv_wn_b': _L0_conv_in['wn_b'], 'L0_conv_Wv_w': _L0_conv_in['Wv_w'], 'L0_conv_conv_w_w': _L0_conv_in['conv_w_w'], 'L0_conv_conv_w_b': _L0_conv_in['conv_w_b'], 'L0_conv_Wout_w': _L0_conv_in['Wout_w'], 'L1_conv_w1': _L1_conv_in['w1'], 'L1_conv_b1': _L1_conv_in['b1'], 'L1_conv_w2': _L1_conv_in['w2'], 'L1_conv_b2': _L1_conv_in['b2'], 'L2_conv_w1': _L2_conv_in['w1'], 'L2_conv_b1': _L2_conv_in['b1'], 'L2_conv_w2': _L2_conv_in['w2'], 'L2_conv_b2': _L2_conv_in['b2'], 'L3_conv_alpha_param': _L3_conv_in['alpha_param'], 'L3_conv_beta_param': _L3_conv_in['beta_param']}

def reference(x, L0_conv_pn_g, L0_conv_pn_b, L0_conv_Wqk_p, L0_conv_Wv_p, L0_conv_conv_p_w, L0_conv_conv_p_b, L0_conv_Wout_p, L0_conv_pln_g, L0_conv_pln_b, L0_conv_Wqk_w, L0_conv_wn_g, L0_conv_wn_b, L0_conv_Wv_w, L0_conv_conv_w_w, L0_conv_conv_w_b, L0_conv_Wout_w, L1_conv_w1, L1_conv_b1, L1_conv_w2, L1_conv_b2, L2_conv_w1, L2_conv_b1, L2_conv_w2, L2_conv_b2, L3_conv_alpha_param, L3_conv_beta_param):
    import jax
    import jax.numpy as jnp

    def _L0_conv_ref(x, pn_g, pn_b, Wqk_p, Wv_p, conv_p_w, conv_p_b, Wout_p, pln_g, pln_b, Wqk_w, wn_g, wn_b, Wv_w, conv_w_w, conv_w_b, Wout_w):
        import jax, jax.numpy as jnp
        import numpy as np
        B, C, SZ, WS, PS, H = (16, 16, 32, 32, 8, 8)
        WN = SZ // WS
        PPW = WS // PS
        NWIN = WN * WN
        NPAT = PPW * PPW
        PD = PS * PS * C
        PDH = PD // H
        POOLED = PS * WN
        PLD = (POOLED // WN) ** 2 * C
        WDH = PLD // H
        WIN_INNER = WDH * H
        WD = WS * WS * C
        EPS = 1e-05

        def _ln(t, g, b):
            m = t.mean(-1, keepdims=True)
            v = jnp.mean((t - m) ** 2, -1, keepdims=True)
            return (t - m) * jax.lax.rsqrt(v + EPS) * g + b

        def _heads(t):
            return t.reshape(*t.shape[:-1], H, -1).swapaxes(-2, -3)

        def _merge(t):
            t = t.swapaxes(-2, -3)
            return t.reshape(*t.shape[:-2], -1)

        def _attn(xn, Wqk, dph):
            q, k = jnp.split(xn @ Wqk, 2, -1)
            q, k = (_heads(q), _heads(k))
            return jax.nn.softmax(jnp.einsum('...hqd,...hkd->...hqk', q, k) * dph ** (-0.5), -1)

        def _dwconv(t, w, b, res):
            lead, c = (t.shape[:-2], t.shape[-1])
            img = t.reshape(-1, res * res, c).transpose(0, 2, 1).reshape(-1, c, res, res)
            y = jax.lax.conv_general_dilated(img, w, (1, 1), 'SAME', feature_group_count=c, dimension_numbers=('NCHW', 'OIHW', 'NCHW'))
            y = y + b[None, :, None, None]
            return y.reshape(-1, c, res * res).transpose(0, 2, 1).reshape(*lead, res * res, c)
        b = x.shape[0]
        xf = x.reshape(b, C, WN, PPW, PS, WN, PPW, PS)
        xf = xf.transpose(0, 2, 5, 3, 6, 4, 7, 1).reshape(b, NWIN, NPAT, PD)
        fl = _ln(xf, pn_g, pn_b)
        pw = _attn(fl, Wqk_p, PDH)
        pv = _heads(fl @ Wv_p)
        pf = jnp.einsum('...hnv,...hvd->...hnd', pw, pv)
        pf = pf + _dwconv(pv, conv_p_w, conv_p_b, PPW)
        pf = _merge(pf) @ Wout_p
        pf = pf.reshape(b, NWIN, NPAT * PD)
        pooled = x.reshape(b, C, POOLED, SZ // POOLED, POOLED, SZ // POOLED).mean((3, 5))
        pl = pooled.reshape(b, C, WN, POOLED // WN, WN, POOLED // WN)
        pl = pl.transpose(0, 2, 4, 3, 5, 1).reshape(b, NWIN, PLD)
        ww = _attn(_ln(pl, pln_g, pln_b), Wqk_w, WDH)
        diag = jnp.diagonal(ww, axis1=-2, axis2=-1)
        eye = jnp.eye(NWIN, dtype=ww.dtype)
        non_diag = ww - diag[..., None] * eye
        line = diag < 0.5
        diag_scaled = jnp.where(line, 0.5, diag)[..., None] * eye
        nds = jnp.where(line[..., None], 0.5 / (1.0 - diag[..., None]) * non_diag, non_diag)
        pfh = _heads(pf)
        wfeat = _merge(jnp.einsum('...hnv,...hvd->...hnd', diag_scaled, pfh))
        xw = x.reshape(b, C, WN, WS, WN, WS).transpose(0, 2, 4, 3, 5, 1).reshape(b, NWIN, WD)
        wv = _heads(_ln(xw, wn_g, wn_b) @ Wv_w)
        wf = jnp.einsum('...hnv,...hvd->...hnd', nds, wv)
        wf = wf + _dwconv(wv, conv_w_w, conv_w_b, WN)
        wf = _merge(wf) @ Wout_w
        wfeat = wfeat + wf
        out = wfeat.reshape(b, WN, WN, WS, WS, C).transpose(0, 5, 1, 3, 2, 4).reshape(b, C, SZ, SZ)
        return out + x

    def _L1_conv_ref(x, w1, b1, w2, b2):
        import jax, jax.numpy as jnp
        import numpy as np

        def _conv2d_same(x, w, b):
            y = jax.lax.conv_general_dilated(x, w, window_strides=(1, 1), padding=((1, 1), (1, 1)), dimension_numbers=('NCHW', 'OIHW', 'NCHW'))
            return y + b[None, :, None, None]
        out = _conv2d_same(x, w1, b1)
        out = jax.nn.relu(out)
        out = _conv2d_same(out, w2, b2)
        return out + x

    def _L2_conv_ref(x, w1, b1, w2, b2):
        import jax, jax.numpy as jnp
        import numpy as np

        def _conv2d_same(x, w, b):
            y = jax.lax.conv_general_dilated(x, w, window_strides=(1, 1), padding=((1, 1), (1, 1)), dimension_numbers=('NCHW', 'OIHW', 'NCHW'))
            return y + b[None, :, None, None]
        out = _conv2d_same(x, w1, b1)
        out = jax.nn.relu(out)
        out = _conv2d_same(out, w2, b2)
        return out + x

    def _L3_conv_ref(x, alpha_param, beta_param):
        import jax, jax.numpy as jnp
        import numpy as np
        SOBEL_X = jnp.array([[-1.0, 0.0, 1.0], [-2.0, 0.0, 2.0], [-1.0, 0.0, 1.0]], dtype=jnp.float32) / 8.0
        SOBEL_Y = jnp.array([[-1.0, -2.0, -1.0], [0.0, 0.0, 0.0], [1.0, 2.0, 1.0]], dtype=jnp.float32) / 8.0
        TIME_STEPS = 10
        DT = 0.01
        EPS = 1e-06

        def _dwconv(u, k2d):
            C = u.shape[1]
            k = jnp.broadcast_to(k2d[None, None], (C, 1, 3, 3))
            return jax.lax.conv_general_dilated(u, k, window_strides=(1, 1), padding=((1, 1), (1, 1)), dimension_numbers=('NCHW', 'OIHW', 'NCHW'), feature_group_count=C)

        def _derivs(u):
            ux = _dwconv(u, SOBEL_X)
            uy = _dwconv(u, SOBEL_Y)
            uxx = _dwconv(ux, SOBEL_X)
            uxy = _dwconv(ux, SOBEL_Y)
            uyy = _dwconv(uy, SOBEL_Y)
            c = lambda t: jnp.clip(t, -10.0, 10.0)
            return (c(ux), c(uy), c(uxx), c(uxy), c(uyy))
        alpha = jnp.abs(alpha_param)
        beta = jnp.abs(beta_param)

        def step(u, _):
            ux, uy, uxx, uxy, uyy = _derivs(u)
            g2 = ux * ux + uy * uy
            denK = jnp.maximum(1.0 + g2, EPS)
            K = jnp.clip((uxx * uyy - uxy * uxy) / (denK * denK + EPS), -5.0, 5.0)
            denH = jnp.sqrt(1.0 + g2 + EPS)
            H = ((1.0 + uy * uy) * uxx - 2.0 * ux * uy * uxy + (1.0 + ux * ux) * uyy) / (2.0 * denH ** 3 + EPS)
            H = jnp.clip(H, -5.0, 5.0)
            diff = jnp.clip(alpha * K + beta * H, -1.0, 1.0)
            u = u + DT * diff
            u = jnp.pad(u[:, :, 1:-1, 1:-1], ((0, 0), (0, 0), (1, 1), (1, 1)), mode='edge')
            return (u, None)
        u, _ = jax.lax.scan(step, x, None, length=TIME_STEPS)
        return 0.7 * u + 0.3 * x

    def _gn(v, G=8, eps=1e-05):
        B_, C_, H_, W_ = v.shape
        g = v.reshape(B_, G, C_ // G, H_, W_)
        m = jnp.mean(g, axis=(2, 3, 4), keepdims=True)
        s = jnp.var(g, axis=(2, 3, 4), keepdims=True)
        return ((g - m) / jnp.sqrt(s + eps)).reshape(v.shape)

    def _ln_c(v, eps=1e-06):
        m = jnp.mean(v, axis=1, keepdims=True)
        s = jnp.var(v, axis=1, keepdims=True)
        return (v - m) / jnp.sqrt(s + eps)

    def _ln_t(v, eps=1e-05):
        m = jnp.mean(v, axis=-1, keepdims=True)
        s = jnp.var(v, axis=-1, keepdims=True)
        return (v - m) / jnp.sqrt(s + eps)

    def _to_tokens(v):
        B_, C_, H_, W_ = v.shape
        return v.reshape(B_, C_, H_ * W_).transpose(0, 2, 1)

    def _from_tokens(t, like):
        B_, C_, H_, W_ = like.shape
        return t.transpose(0, 2, 1).reshape(B_, C_, H_, W_)
    x = _L0_conv_ref(x, L0_conv_pn_g, L0_conv_pn_b, L0_conv_Wqk_p, L0_conv_Wv_p, L0_conv_conv_p_w, L0_conv_conv_p_b, L0_conv_Wout_p, L0_conv_pln_g, L0_conv_pln_b, L0_conv_Wqk_w, L0_conv_wn_g, L0_conv_wn_b, L0_conv_Wv_w, L0_conv_conv_w_w, L0_conv_conv_w_b, L0_conv_Wout_w)
    x = _L1_conv_ref(x, L1_conv_w1, L1_conv_b1, L1_conv_w2, L1_conv_b2)
    x = _L2_conv_ref(x, L2_conv_w1, L2_conv_b1, L2_conv_w2, L2_conv_b2)
    x = _L3_conv_ref(x, L3_conv_alpha_param, L3_conv_beta_param)
    return x

_drawn_inputs = setup_inputs


def setup_inputs(seed=0):
    import zlib

    import numpy as np

    out = dict(_drawn_inputs(seed))
    spreads = {'L0_conv_pn_g': (1.0, 0.57),
     'L0_conv_pn_b': (0.0, 0.1),
     'L0_conv_conv_p_b': (0.0, 0.1),
     'L0_conv_pln_g': (1.0, 0.2),
     'L0_conv_pln_b': (0.0, 0.1),
     'L0_conv_wn_g': (1.0, 0.6),
     'L0_conv_wn_b': (0.0, 2.0),
     'L0_conv_conv_w_b': (0.0, 0.1)}
    factors = {'L0_conv_conv_p_w': 2.706, 'L1_conv_b1': 3.369, 'L2_conv_b1': 3.431}
    for name, (base, spread) in spreads.items():
        noise = np.random.default_rng([zlib.crc32(name.encode()), seed]).standard_normal(out[name].shape)
        drawn = base * np.exp(spread * noise) if base else spread * noise
        out[name] = jnp.asarray(drawn.astype(out[name].dtype))
    for name, factor in factors.items():
        out[name] = (out[name] * factor).astype(out[name].dtype)
    return out
```

```python
from contextlib import ExitStack

import concourse.bass as bass
from concourse import mybir

F32 = mybir.dt.float32
ALU = mybir.AluOpType
ACT = mybir.ActivationFunctionType
AX = mybir.AxisListType

P = 128
B, C, S = 16, 16, 32
HEADS = 8
PS = 8
PPW = S // PS
TOK = B * PPW * PPW
PD = PS * PS * C
WD = S * S * C
DH = PD // HEADS
KC = PD // P
TT = TOK // P
NBLK = TT * HEADS
BL = B // TT
G = 4
RG = S // G
WP = S + 2
ROWF = WP * B
ROW = S * B
NSLOT = 4
SLOTF = KC * 1024
PREFIX = ["q", "k", "V0", "v", "V1", "V2", "V3", "o", "wq", "wk"]
NV = WD // P // KC
NO = WD // 1024
V_FIRST = 4
STEPS = 10
NCH = 4
SLOTS = STEPS * NCH
LN_EPS, D_EPS, DT = 1e-5, 1e-6, 0.01
NCONV = 4

PARAMS = [("pn_g", KC), ("pn_b", KC), ("pln_g", KC), ("pln_b", KC), ("wn_g", P), ("wn_b", P),
          ("cp_w", 9), ("cp_b", 1), ("cw_w", KC), ("cw_b", KC), ("conv_b", NCONV), ("alpha", 1), ("beta", 1),
          ("ident", P), ("mask", P), ("pool", P)]
COL, _at = {}, 0
for _n, _w in PARAMS:
    COL[_n] = (_at, _at + _w)
    _at += _w
NPARAM = _at
MATS = ["SV", "DV", "SS", "-SS", "DS", "2DS", "DD", "2DD"]


def build(nc, x_patch, x_window, x_conv, params, wqk_p, wv_p, wout_p, wqk_w, wv_w, wout_w,
          conv_band, conv_halo, vmats, edge, y_rows, out):
    with ExitStack() as ctx:
        def sb(name, cols):
            return ctx.enter_context(nc.sbuf_tensor(name, [P, cols], F32))

        def sem(name):
            return ctx.enter_context(nc.semaphore(name))

        ring = sb("ring", NSLOT * SLOTF)
        prm = sb("prm", NPARAM)
        ones = sb("ones", P)
        xw = sb("xw", P * B + B)
        xa = sb("xa", G * ROWF)
        reg_a = sb("reg_a", 2048)
        reg_b = sb("reg_b", 2048)
        reg_c = sb("reg_c", 2048)
        reg_d = sb("reg_d", G * ROWF)
        reg_e = sb("reg_e", 2048)
        reg_f = sb("reg_f", 2048)
        reg_g = sb("reg_g", 2048)
        small = sb("small", 896)
        bank = ctx.enter_context(nc.psum_tensor("bank", [P, 8, 512], F32))

        def par(name):
            a, b = COL[name]
            return prm[:, a:b]

        ident = par("ident")

        slot = [ring[:, r * SLOTF:(r + 1) * SLOTF].rearrange("p (k n) -> p k n", k=KC) for r in range(NSLOT)]
        fl = reg_a[:, :].rearrange("p (k t) -> p k t", k=KC)
        prob = reg_a[:, :].rearrange("p (i k) -> p i k", i=NBLK)
        sq = reg_b[:, :].rearrange("p (k t) -> p k t", k=KC)
        prob_t = reg_b[:, :].rearrange("p (i q) -> p i q", i=NBLK)
        q_t = reg_c[:, :].rearrange("p (h t) -> p h t", h=HEADS)
        rows = reg_c[:, :].rearrange("p (t e) -> p t e", t=TT)
        k_t = reg_d[:, 0:2048].rearrange("p (h t) -> p h t", h=HEADS)
        v_tok = reg_e[:, :].rearrange("p (t e) -> p t e", t=TT)
        v_t = reg_f[:, :].rearrange("p (i t) -> p i t", i=NBLK)
        wsq = reg_g[:, :].rearrange("p (k b) -> p k b", b=B)
        pf_t = reg_g[:, :].rearrange("p (i t) -> p i t", i=NBLK)
        xwk = xw[:, 0:P * B].rearrange("p (k b) -> p k b", b=B)
        xa4 = xa[:, :].rearrange("p (g w b) -> p g w b", g=G, b=B)
        xb4 = reg_d[:, :].rearrange("p (g w b) -> p g w b", g=G, b=B)

        at = [0]

        def sm(cols):
            at[0] += cols
            return small[:, at[0] - cols:at[0]]

        rstd_p = reg_c[:, TOK:2 * TOK]
        wsum, wsq_sum, wrstd, pl_sum, pl_sq_sum, pl_rstd = (sm(B) for _ in range(6))
        pl = sm(KC * B)
        pl_sq = reg_f[:, 0:KC * B]
        pln = sm(KC * 2 * B)
        negmax, psum_exp, pinv = sm(NBLK), sm(NBLK), sm(NBLK)
        logit, lmax, wexp, wwt, omd, fct, line, ds, nds = (sm(2) for _ in range(9))
        eps_ln = sm(1)
        dst = sm(TOK // 4)
        d_eps, ln2 = sm(1), sm(1)
        wft = sm(KC * 2 * B)

        ld_patch, ld_prm, ld_win, ld_img = sem("ld_patch"), sem("ld_prm"), sem("ld_win"), sem("ld_img")
        ld_slot = [sem(f"ld_slot{r}") for r in range(NSLOT)]
        ld_band, ld_vm = sem("ld_band"), sem("ld_vm")
        pe = {n: sem("pe_" + n) for n in (
            "slot_used", "patch_mean", "patch_var", "win_mean", "pool", "win_var", "pl_mean", "pl_var", "qkv",
            "scores", "vt", "pt", "attn", "out", "ds", "conv", "fld1", "fld2", "edge")}
        ve = {n: sem("ve_" + n) for n in (
            "order", "consts", "patch_centred", "fl", "win_sums", "win_centred", "win_sq_sums", "xw", "pl_sums",
            "pl_sq_sums", "pln", "negmax", "prob", "pf", "dsl", "stage", "conv", "bank_turn", "img",
            "clip1", "clip2", "slope", "cross", "hn", "kh", "cliph", "diff", "clipd", "u", "pad", "fin", "band0")}
        ac = {n: sem("ac_" + n) for n in (
            "order", "patch_sq", "patch_std", "win_sq", "win_std", "pl_std", "qkv", "vt", "exp", "pt", "rows",
            "wwk", "wv", "conv", "sqr", "lnw", "psq", "w15", "lnd", "inv", "beta", "x3")}
        po = {n: sem("po_" + n) for n in ("zero", "stat", "bandz", "padz", "a", "t", "s", "cxy", "m", "absum", "nk")}
        halo_x, halo_y = sem("halo_x"), sem("halo_y")
        st_rows, ld_u, st_out = sem("st_rows"), sem("ld_u"), sem("st_out")

        block = ctx.enter_context(nc.Block())

        stat = reg_e
        STATF = KC * B + B
        stat_v = [reg_e[:, 1024 + m * STATF:1024 + (m + 1) * STATF] for m in range(4)]

        CB = (RG + 2) * C
        bands = reg_c[:, 0:3 * NCONV * CB].rearrange("p (m n) -> p m n", n=CB)
        hmats = xw[:, 0:NCONV * P].rearrange("p (m n) -> p m n", n=P)
        halo_of = {0: reg_e[:, :].rearrange("p (g n) -> p g n", g=G), 1: reg_f[:, :].rearrange("p (g n) -> p g n", g=G)}

        la = [0]

        def arena(cols):
            la[0] += cols
            return ring[:, la[0] - cols:la[0]]

        u = arena(NCH * ROWF).rearrange("p (x w b) -> p x w b", x=NCH, b=B)
        x3 = arena(NCH * ROW).rearrange("p (x n) -> p x n", x=NCH)
        vm = arena(2 * len(MATS) * P).rearrange("p (m n) -> p m n", n=P)
        edge_m = arena(P)
        dual = lambda cols: [arena(cols) for _ in range(2)]
        h_a, h_s, h_t = dual(ROWF), dual(ROWF), dual(ROWF)
        fld = dual(5 * ROW)
        sqs = dual(3 * ROW)
        cxy, mxy, slope = dual(ROW), dual(ROW), dual(ROW)
        ab, abs_ = dual(2 * ROW), dual(ROW)
        num = dual(2 * ROW)
        lnw = [arena(ROW)] * 2
        den, inv = dual(2 * ROW), dual(2 * ROW)
        kh = num
        hb, dif = dual(ROW), dual(ROW)
        assert la[0] <= NSLOT * SLOTF

        def result(x):
            return kh[x // 2][:, (x % 2) * ROW:(x % 2 + 1) * ROW]

        def mat(name, first):
            return vm[:, MATS.index(name) + (0 if first else len(MATS)), :]

        def slot_ready(eng, k):
            eng.wait_ge(ld_slot[k % NSLOT], 16 * (k // NSLOT + 1))

        k0 = len(PREFIX)
        k1 = k0 + NV - V_FIRST
        U_PREFIX = V_FIRST + 2
        U_V = U_PREFIX + NV - V_FIRST
        U_ALL = U_V + NO
        released, n_v = [], 0
        for kind in PREFIX:
            if kind in ("q", "k", "v"):
                released.append((pe["qkv"], 4 * (("q", "k", "v").index(kind) + 1)))
            elif kind == "o":
                released.append((pe["out"], 4))
            else:
                n_v += 1
                released.append((pe["slot_used"], n_v))

        @block.sync
        def _(sp):
            sp.dma_start(reg_a[:, :], x_patch).then_inc(ld_patch, 16)
            vslot = 0
            for k, kind in enumerate(PREFIX + ["V"] * NSLOT):
                if k >= NSLOT:
                    sp.wait_ge(*released[k - NSLOT])
                if kind in ("q", "k"):
                    n0 = 0 if kind == "q" else PD
                    src = wqk_p.rearrange("(p k) n -> p k n", k=KC)[:, :, n0:n0 + PD]
                elif kind == "v":
                    src = wv_p.rearrange("(p k) n -> p k n", k=KC)
                elif kind == "o":
                    src = wout_p.rearrange("(h d) n -> d h n", d=DH)
                elif kind in ("wq", "wk"):
                    src = wqk_w[("wq", "wk").index(kind)].rearrange("p (k n) -> p k n", k=KC)
                else:
                    src = wv_w[vslot].rearrange("p (k n) -> p k n", k=KC)
                    vslot += 1
                sp.dma_start(slot[k % NSLOT], src).then_inc(ld_slot[k % NSLOT], 16)
            with sp.Fori(1, (NV - V_FIRST) // NSLOT) as i:
                for m in range(NSLOT):
                    sp.wait_ge(pe["slot_used"], i * NSLOT + (U_PREFIX + m - NSLOT + 1))
                    r = (k0 + m) % NSLOT
                    sp.dma_start(ring[:, r * SLOTF:(r + 1) * SLOTF], wv_w[i * NSLOT + (V_FIRST + m)]).then_inc(ld_slot[r], 16)
            with sp.Fori(0, NO // NSLOT) as i:
                for m in range(NSLOT):
                    sp.wait_ge(pe["slot_used"], i * NSLOT + (U_V + m - NSLOT + 1))
                    r = (k1 + m) % NSLOT
                    sp.dma_start(ring[:, r * SLOTF:(r + 1) * SLOTF], wout_w[i * NSLOT + m]).then_inc(ld_slot[r], 16)
            sp.wait_ge(pe["slot_used"], U_ALL)
            sp.dma_start(vm, vmats.rearrange("p (m n) -> p m n", n=P)).then_inc(ld_vm, 16)
            sp.dma_start(edge_m, edge).then_inc(ld_vm, 16)
            for layer in range(NCONV):
                src, halo, hs = (xa4, halo_of[0], halo_x) if layer % 2 == 0 else (xb4, halo_of[1], halo_y)
                if layer == 0:
                    sp.wait_ge(ve["stage"], NO)
                    sp.wait_ge(po["zero"], 4)
                elif layer % 2 == 0:
                    sp.wait_ge(ve["conv"], G * layer // 2)
                else:
                    sp.wait_ge(ac["conv"], G * (layer + 1) // 2)
                for dw in range(3):
                    sp.dma_start(halo[dw * C:(dw + 1) * C, 1:G, :],
                                 src[P - C:P, 0:G - 1, dw:dw + S, :].rearrange("p g w b -> p g (w b)")).then_inc(hs, 16)
                    sp.dma_start(halo[(3 + dw) * C:(4 + dw) * C, 0:G - 1, :],
                                 src[0:C, 1:G, dw:dw + S, :].rearrange("p g w b -> p g (w b)")).then_inc(hs, 16)
            sp.wait_ge(ve["conv"], G * NCONV // 2)
            for g in range(G):
                sp.dma_start(y_rows[:, g * RG:(g + 1) * RG, :].rearrange("c r n -> r c n"),
                             xa4[:, g, 1:S + 1, :].rearrange("p w b -> p (w b)")).then_inc(st_rows, 16)
            sp.wait_ge(st_rows, 16 * G)
            for x in range(NCH):
                sp.dma_start(x3[:, x, :], y_rows[x * 4:(x + 1) * 4].rearrange("c h n -> (c h) n")).then_inc(ld_u, 16)
            for x in range(NCH):
                sp.wait_ge(ve["fin"], x + 1)
                sp.dma_start(out[x * P:(x + 1) * P, :], result(x)).then_inc(st_out, 16)
            sp.wait_ge(st_out, 16 * NCH)

        @block.tensor
        def _(te):
            def used(ins):
                ins.then_inc(pe["slot_used"], 1)

            def all_sum(dst, src, ready, value, signal, chunks):
                te.wait_ge(ready, value)
                for k in range(chunks):
                    ins = te.matmul(dst, ones[:, :], src(k), start=(k == 0), stop=(k == chunks - 1))
                ins.then_inc(pe[signal], 1)

            def project_t(k, first):
                slot_ready(te, k)
                for h in range(HEADS):
                    n = first + h // 2
                    if h % 2 == 0 and n >= 2:
                        te.wait_ge(ac["qkv"], n - 1)
                    for c in range(KC):
                        ins = te.matmul(bank[:, 4 + n % 2, (h % 2) * TOK:(h % 2 + 1) * TOK],
                                        slot[k % NSLOT][:, c, h * DH:(h + 1) * DH], fl[:, c, :],
                                        start=(c == 0), stop=(c == KC - 1))
                    if h % 2 == 1:
                        ins.then_inc(pe["qkv"], 1)

            def thin(k, lhs, b_, n0, start, stop):
                for c in range(KC):
                    for j in range(4):
                        ins = te.matmul(bank[32 * j:32 * j + 32, b_, n0:n0 + 256], lhs(c),
                                        slot[k % NSLOT][:, c, 256 * j:256 * j + 256],
                                        start=start and c == 0, stop=stop and c == KC - 1, skip_group_check=True)
                return ins

            def v_slot(k, s):
                slot_ready(te, k)
                used(thin(k, lambda c: xw[:, (s * KC + c) * B:(s * KC + c) * B + 2 * B], 7, 0, s == 0, False))

            te.wait_ge(ve["consts"], 1)
            te.wait_ge(ld_prm, 16)
            all_sum(bank[:, 0, 0:TOK], lambda c: fl[:, c, :], ld_patch, 16, "patch_mean", KC)
            all_sum(bank[:, 1, 0:TOK], lambda c: sq[:, c, :], ac["patch_sq"], 1, "patch_var", KC)
            all_sum(bank[:, 2, 0:B], lambda c: wsum, ve["win_sums"], 1, "win_mean", 1)
            te.wait_ge(ve["win_sums"], 2)
            te.matmul(bank[:, 3, :], par("pool"), reg_g[:, 0:512], start=True, stop=True).then_inc(pe["pool"], 1)
            te.wait_ge(ve["fl"], 1)
            project_t(0, 0)
            te.wait_ge(ve["patch_centred"], 1)
            all_sum(bank[:, 0, 0:B], lambda c: wsq_sum, ve["win_sq_sums"], 1, "win_var", 1)
            all_sum(bank[:, 1, 0:B], lambda c: pl_sum, ve["pl_sums"], 1, "pl_mean", 1)
            project_t(1, 4)
            all_sum(bank[:, 2, 0:B], lambda c: pl_sq_sum, ve["pl_sq_sums"], 1, "pl_var", 1)
            te.wait_ge(ve["xw"], 1)
            v_slot(2, 0)
            slot_ready(te, 3)
            for n in range(4):
                t, half = n // 2, n % 2
                te.wait_ge(ac["qkv"], 8 + n - 1)
                for c in range(KC):
                    ins = te.matmul(bank[:, 4 + n % 2, :], fl[:, c, t * P:(t + 1) * P],
                                    slot[3][:, c, half * 512:(half + 1) * 512], start=(c == 0), stop=(c == KC - 1))
                ins.then_inc(pe["qkv"], 1)
            te.wait_ge(ac["pl_std"], 1)
            te.wait_ge(ve["pln"], 1)
            te.wait_ge(ac["qkv"], 8)
            for i in range(NBLK):
                t, h = i // HEADS, i % HEADS
                ins = te.matmul(bank[:, i // 4, (i % 4) * P:(i % 4 + 1) * P], q_t[:, h, t * P:(t + 1) * P],
                                k_t[:, h, t * P:(t + 1) * P], start=True, stop=True, skip_group_check=True)
                if i % 4 == 3:
                    ins.then_inc(pe["scores"], 1)
            te.wait_ge(ac["qkv"], 12)
            for i in range(NBLK):
                t, h = i // HEADS, i % HEADS
                if i % 4 == 0 and i >= 8:
                    te.wait_ge(ac["vt"], i // 4 - 1)
                ins = te.transpose(bank[:, 4 + i // 4 % 2, (i % 4) * P:(i % 4 + 1) * P],
                                   v_tok[:, t, h * DH:(h + 1) * DH], ident)
                if i % 4 == 3:
                    ins.then_inc(pe["vt"], 1)
            v_slot(4, 1)
            v_slot(5, 2)
            te.wait_ge(ve["prob"], 1)
            te.wait_ge(ac["vt"], 4)
            for i in range(NBLK):
                if i % 4 == 0 and i >= 8:
                    te.wait_ge(ac["pt"], i // 4 - 1)
                ins = te.transpose(bank[:, 4 + i // 4 % 2, (i % 4) * P:(i % 4 + 1) * P], prob[:, i, :], ident)
                if i % 4 == 3:
                    ins.then_inc(pe["pt"], 1)
            v_slot(6, 3)
            for i in range(NBLK):
                t, h = i // HEADS, i % HEADS
                if i % 4 == 0:
                    te.wait_ge(ac["pt"], i // 4 + 1)
                ins = te.matmul(bank[:, i // 4, (i % 4) * P:(i % 4 + 1) * P], v_tok[:, t, h * DH:(h + 1) * DH],
                                prob_t[:, i, :], start=True, stop=True, skip_group_check=True)
                if i % 4 == 3:
                    ins.then_inc(pe["attn"], 1)
            slot_ready(te, 7)
            te.wait_ge(ve["pf"], 4)
            for n in range(4):
                t, half = n // 2, n % 2
                if n >= 2:
                    te.wait_ge(ac["rows"], n - 1)
                for c in range(HEADS):
                    ins = te.matmul(bank[:, 4 + n % 2, :], pf_t[:, t * HEADS + c, :],
                                    slot[3][:, c, half * 512:(half + 1) * 512], start=(c == 0), stop=(c == HEADS - 1))
                ins.then_inc(pe["out"], 1)
            for k, n0 in ((8, 0), (9, 256)):
                slot_ready(te, k)
                used(thin(k, lambda c: pln[:, c * 2 * B:(c + 1) * 2 * B], 6, n0, True, True))
            te.wait_ge(ve["dsl"], 2)
            te.matmul(bank[:, 3, 0:64], reg_b[:, 0:P], ident.rearrange("p (g b) -> p g b", g=G)[:, :, 0:B],
                      start=True, stop=True).then_inc(pe["ds"], 1)
            with te.Fori(0, (NV - V_FIRST) // NSLOT) as i:
                for m in range(NSLOT):
                    te.wait_ge(ld_slot[(k0 + m) % NSLOT], i * 16 + 16 * ((k0 + m) // NSLOT + 1))
                    te.wait_ge(po["stat"], i * NSLOT + (m + 1))
                    used(thin(k0 + m, lambda c: stat_v[m][:, c * B:(c + 2) * B], 7, 0, False, False))
            with te.Fori(0, NO // NSLOT) as i:
                for m in range(NSLOT):
                    te.wait_ge(ld_slot[(k1 + m) % NSLOT], i * 16 + 16 * ((k1 + m) // NSLOT + 1))
                    te.wait_ge(ve["bank_turn"], i * NSLOT + (m + 1))
                    used(thin(k1 + m, lambda c: wft[:, c * 2 * B:(c + 1) * 2 * B], 4 + m, 0, True, True))
            te.wait_ge(ve["stage"], NO)
            te.wait_ge(ld_band, 16 * (RG + 2))
            for layer in range(NCONV):
                src, halo, hs = (xa4, halo_of[0], halo_x) if layer % 2 == 0 else (xb4, halo_of[1], halo_y)
                b0 = 4 * (layer % 2)
                for g in range(G):
                    if layer:
                        te.wait_ge(ve["conv"] if layer % 2 == 0 else ac["conv"],
                                   G * layer // 2 - G + g + 1 if layer % 2 == 0 else G * (layer // 2) + g + 1)
                    for dw in range(3):
                        te.matmul(bank[:, b0 + g, :], bands[:, layer * 3 + dw, C:C + P],
                                  src[:, g, dw:dw + S, :], start=(dw == 0), stop=False)
                te.wait_ge(hs, 96 * (layer // 2 + 1))
                for g in range(G):
                    te.matmul(bank[:, b0 + g, :], hmats[0:6 * C, layer, :], halo[0:6 * C, g, :],
                              start=False, stop=True).then_inc(pe["conv"], 1)

            def fields(k, c, par_, first, wait):
                a3 = h_a[par_].rearrange("p (w b) -> p w b", b=B)
                s3 = h_s[par_].rearrange("p (w b) -> p w b", b=B)
                b1 = 5 * par_
                te.wait_ge(po["a"], k + 1)
                if wait:
                    te.wait_ge(ve["clip1"], k - 1)
                te.matmul(bank[:, b1, :], mat("SV", first), a3[:, 1:S + 1], start=True, stop=True)
                for n, (m, sh) in enumerate((("DS", 0), ("2DS", 1), ("DS", 2))):
                    te.matmul(bank[:, b1 + 2, :], mat(m, first), a3[:, sh:sh + S], start=(n == 0), stop=(n == 2))
                te.wait_ge(po["s"], k + 1)
                te.matmul(bank[:, b1 + 1, :], mat("DV", first), s3[:, 1:S + 1],
                          start=True, stop=True).then_inc(pe["fld1"], 1)
                if wait or c:
                    te.wait_ge(ve["clip2"], k)
                for n, (m, sh) in enumerate((("DD", 0), ("2DD", 1), ("DD", 2))):
                    te.matmul(bank[:, 3, :], mat(m, first), s3[:, sh:sh + S], start=(n == 0), stop=(n == 2))
                te.matmul(bank[:, 4, :], mat("SS", first), a3[:, 2:S + 2], start=True, stop=False)
                te.matmul(bank[:, 4, :], mat("-SS", first), a3[:, 0:S], start=False, stop=True).then_inc(pe["fld2"], 1)

            te.wait_ge(ld_vm, 32)
            te.wait_ge(ve["conv"], G * NCONV // 2)
            for k in range(4):
                fields(k, k, k % 2, True, k >= 2)
            with te.Fori(1, STEPS) as i:
                for c in range(NCH):
                    fields(i * NCH + c, c, c % 2, False, True)
            te.wait_ge(ve["clip2"], SLOTS)
            for x in range(NCH):
                te.wait_ge(ve["pad"], SLOTS - NCH + x + 1)
                te.matmul(bank[:, x, :], edge_m, u[:, x, 1:S + 1, :], start=True, stop=True).then_inc(pe["edge"], 1)

        @block.vector
        def _(v):
            n_order = [0]

            def then(ins):
                n_order[0] += 1
                ins.then_inc(ve["order"], 1)
                v.wait_ge(ve["order"], n_order[0])

            def kb(row, k):
                return row.unsqueeze(1).to_broadcast([P, k, row.shape[1]])

            then(v.memset(ones[:, :], 1.0))
            then(v.memset(eps_ln, LN_EPS))
            then(v.memset(d_eps, D_EPS))
            then(v.memset(ln2, 0.6931471805599453))
            then(v.memset(xw[:, P * B:], 0.0))
            v.memset(pln, 0.0).then_inc(ve["consts"], 1)
            v.wait_ge(ve["consts"], 1)
            v.wait_ge(pe["patch_mean"], 1)
            v.wait_ge(ld_patch, 16)
            mean = reg_c[:, 0:TOK]
            then(v.tensor_scalar(mean, bank[:, 0, 0:TOK], 1.0 / PD, None, ALU.mult))
            v.tensor_tensor(fl, fl, kb(mean, KC), ALU.subtract).then_inc(ve["patch_centred"], 1)
            v.wait_ge(ld_win, 16)
            v.tensor_reduce(wsum, xwk.rearrange("p k b -> p b k"), AX.X, ALU.add).then_inc(ve["win_sums"], 1)
            for w2 in range(2):
                ins = v.tensor_reduce(reg_g[:, w2 * 256:(w2 + 1) * 256],
                                      xw[:, w2 * 1024:(w2 + 1) * 1024].rearrange("p (w n) -> p n w", w=4), AX.X, ALU.add)
                if w2 == 0:
                    then(ins)
            ins.then_inc(ve["win_sums"], 1)
            v.wait_ge(ac["patch_std"], 1)
            v.wait_ge(ld_prm, 16)
            v.wait_ge(ve["patch_centred"], 1)
            then(v.reciprocal(rstd_p, rstd_p))
            then(v.tensor_tensor(fl, fl, kb(rstd_p, KC), ALU.mult))
            for c in range(KC):
                ins = v.tensor_scalar(fl[:, c, :], fl[:, c, :], par("pn_g")[:, c:c + 1], par("pn_b")[:, c:c + 1],
                                      ALU.mult, ALU.add)
            ins.then_inc(ve["fl"], 1)
            v.wait_ge(pe["win_mean"], 1)
            v.wait_ge(ve["win_sums"], 2)
            then(v.tensor_scalar(wsum, bank[:, 2, 0:B], 1.0 / WD, None, ALU.mult))
            v.wait_ge(pe["pool"], 1)
            v.tensor_tensor(xwk, xwk, kb(wsum, P), ALU.subtract).then_inc(ve["win_centred"], 1)
            for q in range(4):
                then(v.tensor_copy(pl[32 * q:32 * q + 32, :], bank[32 * q:32 * q + 32, 3, q * P:(q + 1) * P]))
            pl3 = pl.rearrange("p (k b) -> p k b", b=B)
            plq3 = pl_sq.rearrange("p (k b) -> p k b", b=B)
            v.tensor_reduce(pl_sum, pl3.rearrange("p k b -> p b k"), AX.X, ALU.add).then_inc(ve["pl_sums"], 1)
            v.wait_ge(ac["win_sq"], 1)
            v.tensor_reduce(wsq_sum, wsq.rearrange("p k b -> p b k"), AX.X, ALU.add).then_inc(ve["win_sq_sums"], 1)
            v.wait_ge(pe["pl_mean"], 1)
            then(v.tensor_scalar(pl_sum, bank[:, 1, 0:B], 1.0 / PD, None, ALU.mult))
            then(v.tensor_tensor(pl3, pl3, kb(pl_sum, KC), ALU.subtract))
            then(v.tensor_tensor(pl_sq, pl, pl, ALU.mult))
            v.tensor_reduce(pl_sq_sum, plq3.rearrange("p k b -> p b k"), AX.X, ALU.add).then_inc(ve["pl_sq_sums"], 1)
            v.wait_ge(ac["win_std"], 1)
            v.wait_ge(ve["win_centred"], 1)
            then(v.reciprocal(wrstd, wrstd))
            then(v.tensor_tensor(xwk, xwk, kb(wrstd, P), ALU.mult))
            then(v.tensor_tensor(xwk, xwk, par("wn_g").unsqueeze(2).to_broadcast([P, P, B]), ALU.mult))
            v.tensor_tensor(xwk, xwk, par("wn_b").unsqueeze(2).to_broadcast([P, P, B]), ALU.add).then_inc(ve["xw"], 1)
            v.wait_ge(ac["pl_std"], 1)
            then(v.reciprocal(pl_rstd, pl_rstd))
            then(v.tensor_tensor(pl3, pl3, kb(pl_rstd, KC), ALU.mult))
            then(v.tensor_tensor(pl3, pl3, par("pln_g").unsqueeze(2).to_broadcast([P, KC, B]), ALU.mult))
            v.tensor_tensor(pln.rearrange("p (k b) -> p k b", b=2 * B)[:, :, 0:B], pl3,
                            par("pln_b").unsqueeze(2).to_broadcast([P, KC, B]), ALU.add).then_inc(ve["pln"], 1)
            for n in range(4):
                v.wait_ge(pe["scores"], n + 1)
                if n == 0:
                    v.wait_ge(ac["qkv"], 12)
                then(v.scalar_tensor_tensor(prob[:, 4 * n:4 * n + 4, :],
                                            bank[:, n, :].rearrange("p (i k) -> p i k", k=P), DH ** -0.5,
                                            kb(par("mask"), 4), ALU.mult, ALU.add))
            v.tensor_reduce(negmax, prob, AX.X, ALU.max, negate=True).then_inc(ve["negmax"], 1)
            v.wait_ge(ac["exp"], NBLK)
            then(v.reciprocal(pinv, psum_exp))
            v.tensor_tensor(prob, prob, pinv.unsqueeze(2).to_broadcast([P, NBLK, P]), ALU.mult).then_inc(ve["prob"], 1)
            v.wait_ge(ac["vt"], 4)
            then(v.tensor_scalar(reg_g[:, :], reg_f[:, :], par("cp_w")[:, 4:5], par("cp_b"), ALU.mult, ALU.add))

            def tap(kh_, kw_):
                w = par("cp_w")[:, kh_ * 3 + kw_:kh_ * 3 + kw_ + 1]
                dg, dj = kh_ - 1, kw_ - 1
                g0, g1 = max(0, -dg), G - max(0, dg)
                if dj == 0:
                    o = reg_g[:, :].rearrange("p (n r) -> p n r", r=G * BL)[:, :, g0 * BL:g1 * BL]
                    i_ = reg_f[:, :].rearrange("p (n r) -> p n r", r=G * BL)[:, :, (g0 + dg) * BL:(g1 + dg) * BL]
                    then(v.scalar_tensor_tensor(o, i_, w, o, ALU.mult, ALU.add))
                    return
                j0, j1 = max(0, -dj), PPW - max(0, dj)
                if dg == 0:
                    o, i_ = pf_t[:, :, j0 * 32:j1 * 32], v_t[:, :, (j0 + dj) * 32:(j1 + dj) * 32]
                    then(v.scalar_tensor_tensor(o, i_, w, o, ALU.mult, ALU.add))
                    return
                for j in range(j0, j1):
                    o = pf_t[:, :, j * 32 + g0 * BL:j * 32 + g1 * BL]
                    i_ = v_t[:, :, (j + dj) * 32 + (g0 + dg) * BL:(j + dj) * 32 + (g1 + dg) * BL]
                    ins = v.scalar_tensor_tensor(o, i_, w, o, ALU.mult, ALU.add)
                    if j < j1 - 1:
                        continue
                    then(ins)

            for kh_ in range(3):
                for kw_ in range(3):
                    if (kh_, kw_) != (1, 1):
                        tap(kh_, kw_)
            for n in range(4):
                v.wait_ge(pe["attn"], n + 1)
                v.tensor_tensor(pf_t[:, 4 * n:4 * n + 4, :], pf_t[:, 4 * n:4 * n + 4, :],
                                bank[:, n, :].rearrange("p (i k) -> p i k", k=P), ALU.add).then_inc(ve["pf"], 1)
            v.wait_ge(pe["slot_used"], U_PREFIX)
            v.wait_ge(ac["wwk"], 1)
            qk = reg_b[:, 256:512]
            then(v.tensor_tensor(qk, bank[:, 6, 0:256], reg_b[:, 0:256], ALU.mult))
            then(v.tensor_reduce(logit, qk.rearrange("p (h d) -> p h d", h=2), AX.X, ALU.add))
            then(v.tensor_scalar(logit, logit, DH ** -0.5, None, ALU.mult))
            then(v.tensor_reduce(lmax, logit.unsqueeze(2), AX.X, ALU.max))
            v.tensor_tensor(logit, logit, lmax, ALU.subtract).then_inc(ve["dsl"], 1)
            v.wait_ge(ac["wwk"], 2)
            then(v.tensor_reduce(lmax, wexp.unsqueeze(2), AX.X, ALU.add))
            then(v.reciprocal(lmax, lmax))
            then(v.tensor_tensor(wwt, wexp, lmax, ALU.mult))
            then(v.tensor_scalar(line, wwt, 0.5, None, ALU.is_lt))
            then(v.tensor_scalar(ds, wwt, 0.5, None, ALU.max))
            then(v.tensor_tensor(nds, wwt, wwt, ALU.subtract))
            then(v.tensor_scalar(omd, wwt, -1.0, 1.0, ALU.mult, ALU.add))
            then(v.tensor_scalar(omd, omd, 0.5, None, ALU.max))
            then(v.reciprocal(fct, omd))
            then(v.tensor_scalar(fct, fct, 0.5, -1.0, ALU.mult, ALU.add))
            then(v.tensor_tensor(fct, fct, line, ALU.mult))
            then(v.scalar_tensor_tensor(nds, fct, 1.0, nds, ALU.add, ALU.mult))
            then(v.tensor_scalar(reg_b[:, 0:64], ones[:, 0:64], ds[:, 0:1], None, ALU.mult))
            v.tensor_scalar(reg_b[:, 64:128], ones[:, 0:64], ds[:, 1:2], None, ALU.mult).then_inc(ve["dsl"], 1)
            v.wait_ge(pe["ds"], 1)
            for t in range(TT):
                then(v.tensor_copy(dst[:, t * 32:(t + 1) * 32].rearrange("p (g b) -> p g b", b=BL),
                                   bank[:, 3, 0:64].rearrange("p (g b) -> p g b", b=B)[:, :, t * BL:(t + 1) * BL]))
            v.wait_ge(ac["rows"], 4)
            v.wait_ge(ld_img, 16)
            v.wait_ge(po["zero"], 1)
            for t in range(TT):
                tr = reg_b[:, 1024 * (1 - t):1024 * (2 - t)].rearrange("p (w n) -> p w n", n=32)
                then(v.transpose(tr, rows[:, t, :].rearrange("p (r w c) -> p w r c", r=2, w=S)))
                then(v.tensor_tensor(tr, tr, kb(dst[:, t * 32:(t + 1) * 32], S), ALU.mult))
                xv = xa4[:, :, 1:S + 1, t * BL:(t + 1) * BL].rearrange("p g w b -> p w g b")
                v.tensor_tensor(xv, xv, tr.rearrange("p w (g b) -> p w g b", b=BL), ALU.add).then_inc(ve["img"], 1)
            v.wait_ge(ac["wv"], 1)
            wv_s, w0, t1, t2 = (reg_b[:, 256 * n:256 * n + 256] for n in range(4))
            for h in range(2):
                then(v.tensor_scalar(w0[:, h * P:(h + 1) * P], wv_s[:, h * P:(h + 1) * P], nds[:, h:h + 1], None, ALU.mult))
            then(v.transpose(t1, wv_s))
            then(v.transpose(t2, w0))
            r3 = lambda a: a.rearrange("p (k b) -> p k b", b=2 * B)
            cb = lambda n: par(n).unsqueeze(2).to_broadcast([P, KC, 2 * B])
            then(v.tensor_tensor(r3(t1), r3(t1), cb("cw_w"), ALU.mult))
            then(v.tensor_tensor(r3(t1), r3(t1), cb("cw_b"), ALU.add))
            v.wait_ge(ve["img"], TT)
            v.tensor_tensor(wft, t1, t2, ALU.add).then_inc(ve["bank_turn"], NSLOT)
            with v.Fori(0, NO // NSLOT) as i:
                for m in range(NSLOT):
                    v.wait_ge(pe["slot_used"], i * NSLOT + (U_V + m + 1))
                    tr = reg_b[:, 1024 + 256 * m:1024 + 256 * (m + 1)]
                    v.transpose(tr, bank[:, 4 + m, 0:256]).then_inc(ve["bank_turn"], 1)
                    v.wait_ge(ve["bank_turn"], i * NSLOT + (NSLOT + m + 1))
                    xv = xa4[:, bass.ds(i, 1), 1 + 8 * m:9 + 8 * m, :].rearrange("p g w b -> p (g w) b")
                    v.tensor_tensor(xv, xv, tr.rearrange("p (w b) -> p w b", b=2 * B)[:, :, 0:B],
                                    ALU.add).then_inc(ve["stage"], 1)
            for n in range(G * NCONV // 2):
                layer, g = 1 + 2 * (n // G), n % G
                v.wait_ge(pe["conv"], layer * G + g + 1)
                if n == 0:
                    v.wait_ge(ve["stage"], NO)
                    v.wait_ge(halo_x, 96)
                if n == G:
                    v.wait_ge(ve["conv"], G)
                    v.wait_ge(halo_x, 192)
                v.scalar_tensor_tensor(xa4[:, g, 1:S + 1, :], bank[:, 4 + g, :].rearrange("p (w b) -> p w b", b=B),
                                       par("conv_b")[:, layer:layer + 1], xa4[:, g, 1:S + 1, :],
                                       ALU.add, ALU.add).then_inc(ve["conv"], 1)

            def f(par_, n, m=1):
                return fld[par_][:, n * ROW:(n + m) * ROW]

            def first_part(k, q):
                v.wait_ge(po["nk"], k - 1)
                v.wait_ge(ac["inv"], k - 1)
                v.wait_ge(ve["hn"], k - 1)
                v.tensor_tensor(kh[q], num[q], inv[q], ALU.mult).then_inc(ve["kh"], 1)
                v.wait_ge(ve["kh"], k - 1)
                v.tensor_scalar(kh[q], kh[q], 5.0, -5.0, ALU.min, ALU.max).then_inc(ve["cliph"], 1)

            def clips(k, q):
                v.wait_ge(pe["fld1"], k)
                v.tensor_scalar(f(q, 0, 3), bank[:, 5 * q:5 * q + 3, :].rearrange("p x n -> p (x n)"),
                                10.0, -10.0, ALU.min, ALU.max).then_inc(ve["clip1"], 1)
                v.wait_ge(pe["fld2"], k)
                v.tensor_scalar(f(q, 3, 2), bank[:, 3:5, :].rearrange("p x n -> p (x n)"),
                                10.0, -10.0, ALU.min, ALU.max).then_inc(ve["clip2"], 1)

            def update(k, q, c):
                v.wait_ge(ve["cliph"], k - 1)
                v.wait_ge(ac["beta"], k - 1)
                v.scalar_tensor_tensor(dif[q], kh[q][:, 0:ROW], par("alpha"), hb[q], ALU.mult, ALU.add).then_inc(ve["diff"], 1)
                v.wait_ge(ve["diff"], k - 1)
                v.tensor_scalar(dif[q], dif[q], 1.0, -1.0, ALU.min, ALU.max).then_inc(ve["clipd"], 1)
                v.wait_ge(ve["clipd"], k - 1)
                uc = u[:, c, 1:S + 1, :]
                v.scalar_tensor_tensor(uc, dif[q].rearrange("p (w b) -> p w b", b=B), DT, uc,
                                       ALU.mult, ALU.add).then_inc(ve["u"], 1)
                v.wait_ge(ve["u"], k - 1)
                v.tensor_copy(u[:, c, 1:S + 1:S - 1, :], u[:, c, 2:S:S - 3, :]).then_inc(ve["pad"], 1)

            def second_part(k, q):
                v.wait_ge(ac["sqr"], k)
                v.scalar_tensor_tensor(slope[q], sqs[q][:, 0:ROW], 1.0, sqs[q][:, ROW:2 * ROW],
                                       ALU.add, ALU.add).then_inc(ve["slope"], 1)
                v.wait_ge(ve["clip2"], k)
                v.scalar_tensor_tensor(ab[q], sqs[q][:, 0:2 * ROW], 1.0, f(q, 3, 2), ALU.add, ALU.mult).then_inc(ve["cross"], 1)
                v.wait_ge(po["cxy"], k)
                v.scalar_tensor_tensor(cxy[q], cxy[q], -2.0, f(q, 2), ALU.mult, ALU.mult).then_inc(ve["cross"], 1)
                v.wait_ge(ve["cross"], 2 * k)
                v.wait_ge(po["absum"], k)
                v.tensor_tensor(num[q][:, ROW:2 * ROW], abs_[q], cxy[q], ALU.add).then_inc(ve["hn"], 1)

            v.wait_ge(pe["slot_used"], U_ALL)
            v.wait_ge(ld_u, 16 * NCH)
            v.wait_ge(po["padz"], 5)
            for n in ("alpha", "beta"):
                then(v.scalar_tensor_tensor(par(n), par(n), -1.0, par(n), ALU.mult, ALU.max))
            for x in range(NCH):
                ins = v.tensor_copy(u[:, x, 1:S + 1, :], x3[:, x, :].rearrange("p (w b) -> p w b", b=B))
                ins.then_inc(ve["band0"], 1)
            v.wait_ge(ve["band0"], NCH)
            clips(1, 0)
            second_part(1, 0)
            for k in range(2, 6):
                first_part(k, k % 2)
                clips(k, (k - 1) % 2)
                update(k, k % 2, (k - 2) % NCH)
                second_part(k, (k - 1) % 2)
            with v.Fori(1, (SLOTS - 2) // NCH) as i:
                for m in range(NCH):
                    k = i * NCH + (m + 2)
                    first_part(k, m % 2)
                    clips(k, (m + 1) % 2)
                    update(k, m % 2, m)
                    second_part(k, (m + 1) % 2)
            for k in range(NCH * ((SLOTS - 2) // NCH) + 2, SLOTS + 2):
                first_part(k, k % 2)
                if k <= SLOTS:
                    clips(k, (k - 1) % 2)
                update(k, k % 2, (k - 2) % NCH)
                if k <= SLOTS:
                    second_part(k, (k - 1) % 2)
            for x in range(NCH):
                v.wait_ge(pe["edge"], x + 1)
                v.wait_ge(ac["x3"], x + 1)
                if x == 0:
                    v.wait_ge(ve["diff"], SLOTS)
                v.scalar_tensor_tensor(result(x), bank[:, x, :], 0.7, x3[:, x, :], ALU.mult, ALU.add).then_inc(ve["fin"], 1)

        @block.scalar
        def _(a):
            a.dma_start(prm[:, :], params).then_inc(ld_prm, 16)
            a.dma_start(xw[:, 0:P * B], x_window).then_inc(ld_win, 16)
            a.wait_ge(po["zero"], 1)
            a.dma_start(xa4[:, :, 1:S + 1, :], x_conv.rearrange("p (g w b) -> p g w b", g=G, b=B)).then_inc(ld_img, 16)
            a.wait_ge(ve["consts"], 1)
            a.wait_ge(ve["patch_centred"], 1)
            a.activation(reg_b[:, :], reg_a[:, :], ACT.Square).then_inc(ac["patch_sq"], 1)
            a.wait_ge(pe["patch_var"], 1)
            a.activation(rstd_p, bank[:, 1, 0:TOK], ACT.Sqrt, bias=eps_ln, scale=1.0 / PD).then_inc(ac["patch_std"], 1)
            a.wait_ge(ve["win_centred"], 1)
            a.activation(reg_g[:, :], xw[:, 0:P * B], ACT.Square).then_inc(ac["win_sq"], 1)
            for n in range(4):
                a.wait_ge(pe["qkv"], n + 1)
                a.activation(reg_c[:, n * 512:(n + 1) * 512], bank[:, 4 + n % 2, :], ACT.Copy).then_inc(ac["qkv"], 1)
            a.wait_ge(pe["win_var"], 1)
            a.activation(wrstd, bank[:, 0, 0:B], ACT.Sqrt, bias=eps_ln, scale=1.0 / WD).then_inc(ac["win_std"], 1)
            for n in range(4):
                a.wait_ge(pe["qkv"], 4 + n + 1)
                a.activation(reg_d[:, n * 512:(n + 1) * 512], bank[:, 4 + n % 2, :], ACT.Copy).then_inc(ac["qkv"], 1)
            a.wait_ge(pe["pl_var"], 1)
            a.activation(pl_rstd, bank[:, 2, 0:B], ACT.Sqrt, bias=eps_ln, scale=1.0 / PD).then_inc(ac["pl_std"], 1)
            for n in range(4):
                a.wait_ge(pe["qkv"], 8 + n + 1)
                a.activation(reg_e[:, n * 512:(n + 1) * 512], bank[:, 4 + n % 2, :], ACT.Copy).then_inc(ac["qkv"], 1)
            for n in range(4):
                a.wait_ge(pe["vt"], n + 1)
                a.activation(reg_f[:, n * 512:(n + 1) * 512], bank[:, 4 + n % 2, :], ACT.Copy).then_inc(ac["vt"], 1)
            a.wait_ge(ve["negmax"], 1)
            for i in range(NBLK):
                a.activation(prob[:, i, :], prob[:, i, :], ACT.Exp, bias=negmax[:, i:i + 1],
                             accum_out=psum_exp[:, i:i + 1]).then_inc(ac["exp"], 1)
            for n in range(4):
                a.wait_ge(pe["pt"], n + 1)
                a.activation(reg_b[:, n * 512:(n + 1) * 512], bank[:, 4 + n % 2, :], ACT.Copy).then_inc(ac["pt"], 1)
            for n in range(4):
                a.wait_ge(pe["out"], n + 1)
                a.activation(reg_c[:, n * 512:(n + 1) * 512], bank[:, 4 + n % 2, :], ACT.Copy).then_inc(ac["rows"], 1)
            a.wait_ge(pe["slot_used"], U_PREFIX)
            a.activation(reg_b[:, 0:256], bank[:, 6, 256:512], ACT.Copy).then_inc(ac["wwk"], 1)
            a.wait_ge(ve["dsl"], 1)
            a.activation(wexp, logit, ACT.Exp).then_inc(ac["wwk"], 1)
            a.wait_ge(pe["slot_used"], U_V)
            a.wait_ge(ve["img"], TT)
            a.activation(reg_b[:, 0:256], bank[:, 7, 0:256], ACT.Copy).then_inc(ac["wv"], 1)
            for n in range(G * NCONV // 2):
                layer, g = 2 * (n // G), n % G
                a.wait_ge(pe["conv"], layer * G + g + 1)
                if n == 0:
                    a.wait_ge(po["zero"], 2)
                if n == G:
                    a.wait_ge(halo_y, 96)
                a.activation(xb4[:, g, 1:S + 1, :], bank[:, g, :].rearrange("p (w b) -> p w b", b=B), ACT.Relu,
                             bias=par("conv_b")[:, layer:layer + 1]).then_inc(ac["conv"], 1)

            def scale_h(k, q):
                a.wait_ge(ve["cliph"], k - 1)
                a.activation(hb[q], kh[q][:, ROW:2 * ROW], ACT.Copy, scale=par("beta")).then_inc(ac["beta"], 1)

            def inverses(k, q):
                a.wait_ge(ve["clip1"], k)
                a.activation(sqs[q], fld[q][:, 0:3 * ROW], ACT.Square).then_inc(ac["sqr"], 1)
                a.wait_ge(ve["slope"], k)
                a.activation(lnw[q], slope[q], ACT.Ln, bias=d_eps).then_inc(ac["lnw"], 1)
                a.activation(den[q][:, 0:ROW], slope[q], ACT.Square).then_inc(ac["psq"], 1)
                a.wait_ge(ac["lnw"], k)
                a.activation(den[q][:, ROW:2 * ROW], lnw[q], ACT.Exp, bias=ln2, scale=1.5).then_inc(ac["w15"], 1)
                a.wait_ge(ac["psq"], k)
                a.wait_ge(ac["w15"], k)
                a.activation(den[q], den[q], ACT.Ln, bias=d_eps).then_inc(ac["lnd"], 1)
                a.wait_ge(ac["lnd"], k)
                a.activation(inv[q], den[q], ACT.Exp, scale=-1.0).then_inc(ac["inv"], 1)

            a.wait_ge(ve["band0"], NCH)
            for x in range(NCH):
                a.activation(x3[:, x, :], x3[:, x, :], ACT.Copy, scale=0.3).then_inc(ac["x3"], 1)
            inverses(1, 0)
            for k in range(2, 6):
                scale_h(k, k % 2)
                inverses(k, (k - 1) % 2)
            with a.Fori(1, (SLOTS - 2) // NCH) as i:
                for m in range(NCH):
                    k = i * NCH + (m + 2)
                    scale_h(k, m % 2)
                    inverses(k, (m + 1) % 2)
            for k in range(NCH * ((SLOTS - 2) // NCH) + 2, SLOTS + 2):
                scale_h(k, k % 2)
                if k <= SLOTS:
                    inverses(k, (k - 1) % 2)

        @block.gpsimd
        def _(p):
            p.memset(xa[:, :], 0.0).then_inc(po["zero"], 1)
            p.wait_ge(pe["scores"], 4)
            p.memset(reg_d[:, :], 0.0).then_inc(po["zero"], 1)
            p.wait_ge(pe["attn"], 4)
            p.wait_ge(ve["xw"], 1)
            for m in range(NSLOT):
                n = V_FIRST + m
                p.tensor_copy(stat_v[m], xw[:, n * KC * B:n * KC * B + STATF]).then_inc(po["stat"], 1)
            with p.Fori(1, (NV - V_FIRST) // NSLOT) as i:
                for m in range(NSLOT):
                    p.wait_ge(pe["slot_used"], i * NSLOT + (U_PREFIX + m - NSLOT + 1))
                    p.tensor_copy(stat_v[m], xw[:, bass.ds(i * (NSLOT * KC * B) + (V_FIRST + m) * KC * B, STATF)])\
                        .then_inc(po["stat"], 1)
            p.wait_ge(ve["img"], TT)
            p.memset(bands, 0.0).then_inc(po["bandz"], 1)
            p.wait_ge(po["bandz"], 1)
            for r in range(RG):
                p.dma_start(bands[r * C:(r + 1) * C, :, r * C:(r + 3) * C],
                            conv_band.rearrange("c (m n) -> c m n", n=3 * C)).then_inc(ld_band, 16)
            p.wait_ge(pe["slot_used"], U_V)
            p.memset(hmats, 0.0).then_inc(po["bandz"], 1)
            p.wait_ge(po["bandz"], 2)
            halo_src = conv_halo.rearrange("c (s m n) -> c s m n", s=2, n=C)
            p.dma_start(hmats[0:3 * C, :, 0:C], halo_src[:, 0]).then_inc(ld_band, 16)
            p.dma_start(hmats[3 * C:6 * C, :, P - C:P], halo_src[:, 1]).then_inc(ld_band, 16)
            p.memset(reg_e[:, :], 0.0).then_inc(po["zero"], 1)
            p.wait_ge(ve["pf"], 4)
            p.memset(reg_f[:, :], 0.0).then_inc(po["zero"], 1)
            p.wait_ge(pe["slot_used"], U_ALL)
            p.memset(u, 0.0).then_inc(po["padz"], 1)
            for q in range(2):
                p.memset(h_a[q], 0.0).then_inc(po["padz"], 1)
                p.memset(h_s[q], 0.0).then_inc(po["padz"], 1)
            p.wait_ge(po["padz"], 5)
            p.wait_ge(ve["band0"], NCH)

            def horizontal(k, q, c, later, used):
                if later:
                    p.wait_ge(ve["pad"], k - (NCH - 1))
                if used:
                    p.wait_ge(pe["fld2"], k - 1)
                uc = u[:, c].rearrange("p w b -> p (w b)")
                p.tensor_tensor(h_a[q][:, B:(S + 1) * B], uc[:, 2 * B:], uc[:, 0:S * B], ALU.subtract).then_inc(po["a"], 1)
                p.tensor_tensor(h_t[q][:, 0:(S + 1) * B], uc[:, 0:(S + 1) * B], uc[:, B:], ALU.add).then_inc(po["t"], 1)
                p.wait_ge(po["t"], k + 1)
                p.tensor_tensor(h_s[q][:, B:(S + 1) * B], h_t[q][:, 0:S * B], h_t[q][:, B:(S + 1) * B],
                                ALU.add).then_inc(po["s"], 1)

            def products(k, q):
                p.wait_ge(ve["clip1"], k)
                p.tensor_tensor(cxy[q], fld[q][:, 0:ROW], fld[q][:, ROW:2 * ROW], ALU.mult).then_inc(po["cxy"], 1)
                p.wait_ge(ve["clip2"], k)
                p.tensor_tensor(mxy[q], fld[q][:, 3 * ROW:4 * ROW], fld[q][:, 4 * ROW:5 * ROW], ALU.mult).then_inc(po["m"], 1)
                p.wait_ge(ve["cross"], 2 * k - 1)
                p.tensor_tensor(abs_[q], ab[q][:, 0:ROW], ab[q][:, ROW:2 * ROW], ALU.add).then_inc(po["absum"], 1)
                p.wait_ge(po["m"], k)
                p.wait_ge(ac["sqr"], k)
                p.tensor_tensor(num[q][:, 0:ROW], mxy[q], sqs[q][:, 2 * ROW:3 * ROW], ALU.subtract).then_inc(po["nk"], 1)

            horizontal(0, 0, 0, False, False)
            for k in range(1, 6):
                horizontal(k, k % 2, k % NCH, k >= NCH, k >= 2)
                products(k, (k - 1) % 2)
            with p.Fori(1, (SLOTS - 2) // NCH) as i:
                for m in range(NCH):
                    k = i * NCH + (m + 2)
                    horizontal(k, m % 2, (m + 2) % NCH, True, True)
                    products(k, (m + 1) % 2)
            for k in range(NCH * ((SLOTS - 2) // NCH) + 2, SLOTS + 1):
                if k < SLOTS:
                    horizontal(k, k % 2, k % NCH, True, True)
                products(k, (k - 1) % 2)
    return nc


def vertical_operators(np):
    sv = np.eye(S) * 2 + np.eye(S, k=1) + np.eye(S, k=-1)
    dv = np.eye(S, k=1) - np.eye(S, k=-1)
    edge = np.eye(S)
    edge[0], edge[S - 1] = edge[1], edge[S - 2]
    ops = {"SV": sv / 8, "DV": dv / 8, "SS": sv @ sv / 64, "-SS": -sv @ sv / 64, "DS": dv @ sv / 64,
           "2DS": 2 * dv @ sv / 64, "DD": dv @ dv / 64, "2DD": 2 * dv @ dv / 64}
    four = lambda m: np.kron(np.eye(P // S), m.T)
    mats = [four(ops[n]) for n in MATS] + [four(ops[n] @ edge) for n in MATS]
    return (np.concatenate(mats, 1).astype(np.float32), four(edge).astype(np.float32))


def kernel(**inputs):
    import numpy as np
    import concourse.bacc as bacc
    from concourse.bass_utils import run_bass_kernel_spmd

    a = {k: np.asarray(v) for k, v in inputs.items()}
    x = a["x"]
    d = {}
    x8 = x.reshape(TT, BL, C, PPW, PS, PPW, PS)
    d["x_patch"] = x8.transpose(4, 6, 2, 0, 5, 3, 1).reshape(P, KC * TOK)
    d["x_window"] = x.transpose(2, 3, 1, 0).reshape(P, P * B)
    d["x_conv"] = x.reshape(B, C, G, RG, S).transpose(3, 1, 2, 4, 0).reshape(P, G * ROW)
    L0 = {k[len("L0_conv_"):]: v for k, v in a.items() if k.startswith("L0_conv_")}
    d["wqk_p"], d["wv_p"], d["wout_p"] = L0["Wqk_p"], L0["Wv_p"], L0["Wout_p"]
    d["wqk_w"] = L0["Wqk_w"].reshape(32, 4, KC, 2, PD).transpose(3, 1, 0, 2, 4).reshape(2, P, SLOTF)
    d["wv_w"] = L0["Wv_w"].reshape(P, NV, SLOTF).transpose(1, 0, 2)
    d["wout_w"] = L0["Wout_w"].reshape(4, KC, 32, G, 4, 2, 4, 8, C).transpose(3, 6, 0, 2, 1, 4, 7, 5, 8)\
        .reshape(NO, P, SLOTF)
    by_quadrant = lambda t: np.broadcast_to(t.reshape(1, 4, 32).transpose(0, 2, 1)[:, :, None, :], (4, 32, 2, 4)).reshape(P, KC)
    conv_w = np.stack([a[f"L{l}_conv_w{i}"] for l in (1, 2) for i in (1, 2)])
    conv_b = np.stack([a[f"L{l}_conv_b{i}"] for l in (1, 2) for i in (1, 2)])
    d["conv_band"] = conv_w[:, :, :, ::-1, :].transpose(2, 0, 4, 3, 1).reshape(C, 3 * NCONV * 3 * C)
    d["conv_halo"] = conv_w[:, :, :, 0::2, :].transpose(4, 2, 3, 0, 1).reshape(3 * C, 2 * NCONV * C)
    tok = np.arange(P)
    rows = tok // 4
    pooled_at = np.arange(P) % 32
    cols = {
        "pn_g": L0["pn_g"].reshape(P, KC), "pn_b": L0["pn_b"].reshape(P, KC),
        "pln_g": L0["pln_g"].reshape(32, 4, KC).transpose(1, 0, 2).reshape(P, KC),
        "pln_b": L0["pln_b"].reshape(32, 4, KC).transpose(1, 0, 2).reshape(P, KC),
        "wn_g": L0["wn_g"].reshape(P, P), "wn_b": L0["wn_b"].reshape(P, P),
        "cp_w": L0["conv_p_w"].reshape(DH, 9), "cp_b": L0["conv_p_b"].reshape(DH, 1),
        "cw_w": by_quadrant(L0["conv_w_w"][:, 0, 1, 1]), "cw_b": by_quadrant(L0["conv_w_b"]),
        "conv_b": np.tile(conv_b.T, (RG, 1)),
        "alpha": np.broadcast_to(a["L3_conv_alpha_param"].reshape(1, 1), (P, 1)),
        "beta": np.broadcast_to(a["L3_conv_beta_param"].reshape(1, 1), (P, 1)),
        "ident": np.eye(P, dtype=np.float32),
        "mask": np.where(tok[:, None] % BL == tok[None] % BL, 0.0, -1e30).astype(np.float32),
        "pool": (((rows // 4)[:, None] * 4 + (tok % 4)[:, None]) == pooled_at[None]).astype(np.float32) / 16,
    }
    d["params"] = np.concatenate([cols[n] for n, _ in PARAMS], 1)
    d["vmats"], d["edge"] = vertical_operators(np)

    nc = bacc.Bacc("TRN2", target_bir_lowering=False, num_devices=1)
    arrays, args = {}, []
    for n in ("x_patch", "x_window", "x_conv", "params", "wqk_p", "wv_p", "wout_p", "wqk_w", "wv_w", "wout_w",
              "conv_band", "conv_halo", "vmats", "edge"):
        arrays[n] = np.ascontiguousarray(d[n])
        assert arrays[n].dtype == np.float32, n
        args.append(nc.dram_tensor(n, arrays[n].shape, F32, kind="ExternalInput").ap())
    args.append(nc.dram_tensor("y_rows", (C, S, ROW), F32, kind="Internal").ap())
    args.append(nc.dram_tensor("out", (NCH * P, ROW), F32, kind="ExternalOutput").ap())
    build(nc, *args)
    r = run_bass_kernel_spmd(nc, [arrays], core_ids=[0])
    return r.results[0]["out"].reshape(C, S, S, B).transpose(3, 0, 1, 2)
```

```python
from contextlib import ExitStack

import concourse.bass as bass
from concourse import mybir

F32 = mybir.dt.float32
ALU = mybir.AluOpType
ACT = mybir.ActivationFunctionType
AX = mybir.AxisListType

P = 128
B, C, S = 16, 16, 32
HEADS = 8
PS = 8
PPW = S // PS
TOK = B * PPW * PPW
PD = PS * PS * C
WD = S * S * C
DH = PD // HEADS
KC = PD // P
TT = TOK // P
NBLK = TT * HEADS
BL = B // TT
G = 4
RG = S // G
WP = S + 2
ROWF = WP * B
ROW = S * B
NSLOT = 4
SLOTF = KC * 1024
PREFIX = ["q", "V0", "V1", "k", "V2", "V3", "V4", "v", "V5", "V6", "V7", "o", "wq", "wk"]
NV = WD // P // KC
NO = WD // 1024
V_FIRST = 8
STEPS = 10
NCH = 4
SLOTS = STEPS * NCH
LN_EPS, D_EPS, DT = 1e-5, 1e-6, 0.01
NCONV = 4

PARAMS = [("pn_g", KC), ("pn_b", KC), ("pln_g", KC), ("pln_b", KC), ("wn_g", P), ("wn_b", P),
          ("cp_w", 9), ("cp_b", 1), ("cw_w", KC), ("cw_b", KC), ("conv_b", NCONV), ("alpha", 1), ("beta", 1),
          ("ident", P), ("mask", P), ("pool", P)]
COL, _at = {}, 0
for _n, _w in PARAMS:
    COL[_n] = (_at, _at + _w)
    _at += _w
NPARAM = _at
MATS = ["SV", "DV", "SS", "-SS", "DS", "2DS", "DD", "2DD"]


def build(nc, x_patch, x_window, x_conv, params, wqk_p, wv_p, wout_p, wqk_w, wv_w, wout_w,
          conv_band, conv_halo, vmats, edge, y_rows, out):
    with ExitStack() as ctx:
        def sb(name, cols):
            return ctx.enter_context(nc.sbuf_tensor(name, [P, cols], F32))

        def sem(name):
            return ctx.enter_context(nc.semaphore(name))

        ring = sb("ring", NSLOT * SLOTF)
        prm = sb("prm", NPARAM)
        ones = sb("ones", P)
        xw = sb("xw", P * B + B)
        xa = sb("xa", G * ROWF)
        reg_a = sb("reg_a", 2048)
        reg_b = sb("reg_b", 2048)
        reg_c = sb("reg_c", 2048)
        reg_d = sb("reg_d", G * ROWF)
        reg_e = sb("reg_e", 2048)
        reg_f = sb("reg_f", 2048)
        reg_g = sb("reg_g", 2048)
        small = sb("small", 896)
        bank = ctx.enter_context(nc.psum_tensor("bank", [P, 8, 512], F32))

        def par(name):
            a, b = COL[name]
            return prm[:, a:b]

        ident = par("ident")

        slot = [ring[:, r * SLOTF:(r + 1) * SLOTF].rearrange("p (k n) -> p k n", k=KC) for r in range(NSLOT)]
        fl = reg_a[:, :].rearrange("p (k t) -> p k t", k=KC)
        prob = reg_a[:, :].rearrange("p (i k) -> p i k", i=NBLK)
        sq = reg_b[:, :].rearrange("p (k t) -> p k t", k=KC)
        prob_t = reg_b[:, :].rearrange("p (i q) -> p i q", i=NBLK)
        q_t = reg_c[:, :].rearrange("p (h t) -> p h t", h=HEADS)
        rows = reg_c[:, :].rearrange("p (t e) -> p t e", t=TT)
        k_t = reg_d[:, 0:2048].rearrange("p (h t) -> p h t", h=HEADS)
        v_tok = reg_e[:, :].rearrange("p (t e) -> p t e", t=TT)
        v_t = reg_f[:, :].rearrange("p (i t) -> p i t", i=NBLK)
        wsq = reg_g[:, :].rearrange("p (k b) -> p k b", b=B)
        pf_t = reg_g[:, :].rearrange("p (i t) -> p i t", i=NBLK)
        xwk = xw[:, 0:P * B].rearrange("p (k b) -> p k b", b=B)
        xa4 = xa[:, :].rearrange("p (g w b) -> p g w b", g=G, b=B)
        xb4 = reg_d[:, :].rearrange("p (g w b) -> p g w b", g=G, b=B)

        at = [0]

        def sm(cols):
            at[0] += cols
            return small[:, at[0] - cols:at[0]]

        rstd_p, patch_part, patch_part2 = (reg_c[:, n * TOK:(n + 1) * TOK] for n in range(1, 4))
        wsum, wsq_sum, wrstd, pl_sum, pl_sq_sum, pl_rstd = (sm(B) for _ in range(6))
        pl = sm(KC * B)
        pl_sq = reg_f[:, 0:KC * B]
        pln = sm(KC * 2 * B)
        negmax, psum_exp, pinv = sm(NBLK), sm(NBLK), sm(NBLK)
        logit, lmax, wexp, wwt, omd, fct, line, ds, nds = (sm(2) for _ in range(9))
        eps_ln = sm(1)
        dst = sm(TOK // 4)
        d_eps, ln2 = sm(1), sm(1)
        wft = sm(KC * 2 * B)

        ld_patch, ld_prm, ld_win, ld_img = sem("ld_patch"), sem("ld_prm"), sem("ld_win"), sem("ld_img")
        ld_slot = [sem(f"ld_slot{r}") for r in range(NSLOT)]
        ld_band, ld_vm = sem("ld_band"), sem("ld_vm")
        pe = {n: sem("pe_" + n) for n in (
            "slot_used", "patch_mean", "patch_var", "win_mean", "pool", "win_var", "pl_mean", "pl_var", "qkv",
            "scores", "vt", "pt", "attn", "out", "ds", "conv", "fld1", "fld2", "edge")}
        ve = {n: sem("ve_" + n) for n in (
            "order", "consts", "patch_part", "patch_centred", "fl", "win_sums", "win_centred", "win_sq_sums", "xw", "pl_sums",
            "pl_sq_sums", "pln", "negmax", "prob", "pf", "dsl", "stage", "conv", "bank_turn", "img",
            "clip1", "clip2", "slope", "outer", "cross", "hn", "kh", "cliph", "diff", "clipd", "u", "pad", "fin", "u0")}
        ac = {n: sem("ac_" + n) for n in (
            "order", "patch_sq", "patch_std", "fl", "win_sq", "win_std", "pl_std", "qkv", "vt", "exp", "pt", "rows",
            "wwk", "wv", "conv", "evac1", "evac2", "sqr", "lnw", "psq", "w15", "lnd", "inv", "beta", "x3")}
        po = {n: sem("po_" + n) for n in ("zero", "stat", "bandz", "padz", "a", "t", "s", "cxy", "m", "absum", "nk")}
        halo_x, halo_y = sem("halo_x"), sem("halo_y")
        st_rows, ld_u, st_out = sem("st_rows"), [sem(f"ld_u{x}") for x in range(NCH)], sem("st_out")

        block = ctx.enter_context(nc.Block())

        stat = reg_e
        STATF = KC * B + B
        stat_v = [reg_e[:, 1024 + m * STATF:1024 + (m + 1) * STATF] for m in range(4)]

        CB = (RG + 2) * C
        bands = reg_c[:, 0:3 * NCONV * CB].rearrange("p (m n) -> p m n", n=CB)
        hmats = xw[:, 0:NCONV * P].rearrange("p (m n) -> p m n", n=P)
        halo_of = {0: reg_e[:, :].rearrange("p (g n) -> p g n", g=G), 1: reg_f[:, :].rearrange("p (g n) -> p g n", g=G)}

        la = [0]

        def arena(cols):
            la[0] += cols
            return ring[:, la[0] - cols:la[0]]

        u = arena(NCH * ROWF).rearrange("p (x w b) -> p x w b", x=NCH, b=B)
        x3 = arena(NCH * ROW).rearrange("p (x n) -> p x n", x=NCH)
        vm = arena(2 * len(MATS) * P).rearrange("p (m n) -> p m n", n=P)
        edge_m = arena(P)
        dual = lambda cols: [arena(cols) for _ in range(2)]
        h_t = dual(ROWF)
        h_a = [reg_d[:, n * ROWF:(n + 1) * ROWF] for n in range(4)]
        h_s = [xa[:, n * ROWF:(n + 1) * ROWF] for n in range(4)]
        fld = dual(5 * ROW)
        sqs = dual(3 * ROW)
        cxy, mxy, slope = dual(ROW), dual(ROW), dual(ROW)
        ab, abs_ = dual(2 * ROW), dual(ROW)
        num = dual(2 * ROW)
        lnw = [arena(ROW)] * 2
        den, inv = dual(2 * ROW), dual(2 * ROW)
        kh = num
        hb, dif = dual(ROW), dual(ROW)
        assert la[0] <= NSLOT * SLOTF

        def result(x):
            return kh[x // 2][:, (x % 2) * ROW:(x % 2 + 1) * ROW]

        def mat(name, first):
            return vm[:, MATS.index(name) + (0 if first else len(MATS)), :]

        def slot_ready(eng, k):
            eng.wait_ge(ld_slot[k % NSLOT], 16 * (k // NSLOT + 1))

        k0 = len(PREFIX)
        k1 = k0 + NV - V_FIRST
        U_PREFIX = V_FIRST + 2
        U_V = U_PREFIX + NV - V_FIRST
        U_ALL = U_V + NO
        released, n_v = [], 0
        for kind in PREFIX:
            if kind in ("q", "k", "v"):
                released.append((pe["qkv"], 4 * (("q", "k", "v").index(kind) + 1)))
            elif kind == "o":
                released.append((pe["out"], 4))
            else:
                n_v += 1
                released.append((pe["slot_used"], n_v))

        @block.sync
        def _(sp):
            sp.dma_start(reg_a[:, :], x_patch).then_inc(ld_patch, 16)
            sp.dma_start(xw[:, 0:P * B], x_window).then_inc(ld_win, 16)
            vslot = 0
            for k, kind in enumerate(PREFIX + ["V"] * NSLOT):
                if k >= NSLOT:
                    sp.wait_ge(*released[k - NSLOT])
                if kind in ("q", "k"):
                    n0 = 0 if kind == "q" else PD
                    src = wqk_p.rearrange("(p k) n -> p k n", k=KC)[:, :, n0:n0 + PD]
                elif kind == "v":
                    src = wv_p.rearrange("(p k) n -> p k n", k=KC)
                elif kind == "o":
                    src = wout_p.rearrange("(h d) n -> d h n", d=DH)
                elif kind in ("wq", "wk"):
                    src = wqk_w[("wq", "wk").index(kind)].rearrange("p (k n) -> p k n", k=KC)
                else:
                    src = wv_w[vslot].rearrange("p (k n) -> p k n", k=KC)
                    vslot += 1
                sp.dma_start(slot[k % NSLOT], src).then_inc(ld_slot[k % NSLOT], 16)
            with sp.Fori(1, (NV - V_FIRST) // NSLOT) as i:
                for m in range(NSLOT):
                    sp.wait_ge(pe["slot_used"], i * NSLOT + (U_PREFIX + m - NSLOT + 1))
                    r = (k0 + m) % NSLOT
                    sp.dma_start(ring[:, r * SLOTF:(r + 1) * SLOTF], wv_w[i * NSLOT + (V_FIRST + m)]).then_inc(ld_slot[r], 16)
            with sp.Fori(0, NO // NSLOT) as i:
                for m in range(NSLOT):
                    sp.wait_ge(pe["slot_used"], i * NSLOT + (U_V + m - NSLOT + 1))
                    r = (k1 + m) % NSLOT
                    sp.dma_start(ring[:, r * SLOTF:(r + 1) * SLOTF], wout_w[i * NSLOT + m]).then_inc(ld_slot[r], 16)
            sp.wait_ge(pe["slot_used"], U_ALL)
            sp.dma_start(vm, vmats.rearrange("p (m n) -> p m n", n=P)).then_inc(ld_vm, 16)
            sp.dma_start(edge_m, edge).then_inc(ld_vm, 16)
            for layer in range(NCONV):
                src, halo, hs = (xa4, halo_of[0], halo_x) if layer % 2 == 0 else (xb4, halo_of[1], halo_y)
                if layer == 0:
                    sp.wait_ge(ve["stage"], NO)
                    sp.wait_ge(po["zero"], 4)
                elif layer % 2 == 0:
                    sp.wait_ge(ve["conv"], G * layer // 2)
                else:
                    sp.wait_ge(ac["conv"], G * (layer + 1) // 2)
                for dw in range(3):
                    sp.dma_start(halo[dw * C:(dw + 1) * C, 1:G, :],
                                 src[P - C:P, 0:G - 1, dw:dw + S, :].rearrange("p g w b -> p g (w b)")).then_inc(hs, 16)
                    sp.dma_start(halo[(3 + dw) * C:(4 + dw) * C, 0:G - 1, :],
                                 src[0:C, 1:G, dw:dw + S, :].rearrange("p g w b -> p g (w b)")).then_inc(hs, 16)
            for g in range(G):
                sp.wait_ge(ve["conv"], G * NCONV // 2 - G + g + 1)
                sp.dma_start(y_rows[:, g * RG:(g + 1) * RG, :].rearrange("c r n -> r c n"),
                             xa4[:, g, 1:S + 1, :].rearrange("p w b -> p (w b)")).then_inc(st_rows, 16)
            sp.wait_ge(st_rows, 16 * G)
            for x in range(NCH):
                sp.dma_start(x3[:, x, :], y_rows[x * 4:(x + 1) * 4].rearrange("c h n -> (c h) n")).then_inc(ld_u[x], 16)
            for x in range(NCH):
                sp.wait_ge(ve["fin"], x + 1)
                sp.dma_start(out[x * P:(x + 1) * P, :], result(x)).then_inc(st_out, 16)
            sp.wait_ge(st_out, 16 * NCH)

        @block.tensor
        def _(te):
            def used(ins):
                ins.then_inc(pe["slot_used"], 1)

            def all_sum(dst, src, ready, value, signal):
                te.wait_ge(ready, value)
                te.matmul(dst, ones[:, :], src, start=True, stop=True).then_inc(pe[signal], 1)

            def project_t(k, first):
                slot_ready(te, k)
                for h in range(HEADS):
                    n = first + h // 2
                    if h % 2 == 0 and n >= 2:
                        te.wait_ge(ac["qkv"], n - 1)
                    for c in range(KC):
                        if first == 0 and h == 0:
                            te.wait_ge(ac["fl"], c + 1)
                        ins = te.matmul(bank[:, 4 + n % 2, (h % 2) * TOK:(h % 2 + 1) * TOK],
                                        slot[k % NSLOT][:, c, h * DH:(h + 1) * DH], fl[:, c, :],
                                        start=(c == 0), stop=(c == KC - 1))
                    if h % 2 == 1:
                        ins.then_inc(pe["qkv"], 1)

            def thin(k, lhs, b_, n0, start, stop):
                for c in range(KC):
                    for j in range(4):
                        ins = te.matmul(bank[32 * j:32 * j + 32, b_, n0:n0 + 256], lhs(c),
                                        slot[k % NSLOT][:, c, 256 * j:256 * j + 256],
                                        start=start and c == 0, stop=stop and c == KC - 1, skip_group_check=True)
                return ins

            def v_slot(s):
                k = PREFIX.index(f"V{s}")
                slot_ready(te, k)
                used(thin(k, lambda c: xw[:, (s * KC + c) * B:(s * KC + c) * B + 2 * B], 7, 0, s == 0, False))

            te.wait_ge(ve["consts"], 1)
            te.wait_ge(ld_prm, 16)
            all_sum(bank[:, 0, 0:TOK], patch_part, ve["patch_part"], 1, "patch_mean")
            all_sum(bank[:, 2, 0:B], wsum, ve["win_sums"], 1, "win_mean")
            te.wait_ge(ve["win_sums"], 2)
            te.matmul(bank[:, 3, :], par("pool"), reg_g[:, 0:512], start=True, stop=True).then_inc(pe["pool"], 1)
            all_sum(bank[:, 1, 0:TOK], patch_part2, ve["patch_part"], 2, "patch_var")
            project_t(PREFIX.index("q"), 0)
            te.wait_ge(ve["patch_centred"], 1)
            all_sum(bank[:, 0, 0:B], wsq_sum, ve["win_sq_sums"], 1, "win_var")
            all_sum(bank[:, 1, 0:B], pl_sum, ve["pl_sums"], 1, "pl_mean")
            te.wait_ge(ve["xw"], 1)
            v_slot(0)
            v_slot(1)
            all_sum(bank[:, 2, 0:B], pl_sq_sum, ve["pl_sq_sums"], 1, "pl_var")
            project_t(PREFIX.index("k"), 4)
            for n in range(2, 5):
                v_slot(n)
            kv = PREFIX.index("v")
            slot_ready(te, kv)
            for n in range(4):
                t, half = n // 2, n % 2
                te.wait_ge(ac["qkv"], 8 + n - 1)
                for c in range(KC):
                    ins = te.matmul(bank[:, 4 + n % 2, :], fl[:, c, t * P:(t + 1) * P],
                                    slot[kv % NSLOT][:, c, half * 512:(half + 1) * 512], start=(c == 0), stop=(c == KC - 1))
                ins.then_inc(pe["qkv"], 1)
            te.wait_ge(ac["pl_std"], 1)
            te.wait_ge(ve["pln"], 1)
            te.wait_ge(ac["qkv"], 8)
            for i in range(NBLK):
                t, h = i // HEADS, i % HEADS
                ins = te.matmul(bank[:, i // 4, (i % 4) * P:(i % 4 + 1) * P], q_t[:, h, t * P:(t + 1) * P],
                                k_t[:, h, t * P:(t + 1) * P], start=True, stop=True, skip_group_check=True)
                if i % 4 == 3:
                    ins.then_inc(pe["scores"], 1)
            te.wait_ge(ac["qkv"], 12)
            for i in range(NBLK):
                t, h = i // HEADS, i % HEADS
                if i % 4 == 0 and i >= 8:
                    te.wait_ge(ac["vt"], i // 4 - 1)
                ins = te.transpose(bank[:, 4 + i // 4 % 2, (i % 4) * P:(i % 4 + 1) * P],
                                   v_tok[:, t, h * DH:(h + 1) * DH], ident)
                if i % 4 == 3:
                    ins.then_inc(pe["vt"], 1)
            v_slot(5)
            v_slot(6)
            te.wait_ge(ve["prob"], 1)
            te.wait_ge(ac["vt"], 4)
            for i in range(NBLK):
                if i % 4 == 0 and i >= 8:
                    te.wait_ge(ac["pt"], i // 4 - 1)
                ins = te.transpose(bank[:, 4 + i // 4 % 2, (i % 4) * P:(i % 4 + 1) * P], prob[:, i, :], ident)
                if i % 4 == 3:
                    ins.then_inc(pe["pt"], 1)
            v_slot(7)
            for i in range(NBLK):
                t, h = i // HEADS, i % HEADS
                if i % 4 == 0:
                    te.wait_ge(ac["pt"], i // 4 + 1)
                ins = te.matmul(bank[:, i // 4, (i % 4) * P:(i % 4 + 1) * P], v_tok[:, t, h * DH:(h + 1) * DH],
                                prob_t[:, i, :], start=True, stop=True, skip_group_check=True)
                if i % 4 == 3:
                    ins.then_inc(pe["attn"], 1)
            ko = PREFIX.index("o")
            slot_ready(te, ko)
            te.wait_ge(ve["pf"], 4)
            for n in range(4):
                t, half = n // 2, n % 2
                if n >= 2:
                    te.wait_ge(ac["rows"], n - 1)
                for c in range(HEADS):
                    ins = te.matmul(bank[:, 4 + n % 2, :], pf_t[:, t * HEADS + c, :],
                                    slot[ko % NSLOT][:, c, half * 512:(half + 1) * 512], start=(c == 0), stop=(c == HEADS - 1))
                ins.then_inc(pe["out"], 1)
            for k, n0 in ((PREFIX.index("wq"), 0), (PREFIX.index("wk"), 256)):
                slot_ready(te, k)
                used(thin(k, lambda c: pln[:, c * 2 * B:(c + 1) * 2 * B], 6, n0, True, True))
            te.wait_ge(ve["dsl"], 2)
            te.matmul(bank[:, 3, 0:64], reg_b[:, 0:P], ident.rearrange("p (g b) -> p g b", g=G)[:, :, 0:B],
                      start=True, stop=True).then_inc(pe["ds"], 1)
            with te.Fori(0, (NV - V_FIRST) // NSLOT) as i:
                for m in range(NSLOT):
                    te.wait_ge(ld_slot[(k0 + m) % NSLOT], i * 16 + 16 * ((k0 + m) // NSLOT + 1))
                    te.wait_ge(po["stat"], i * NSLOT + (m + 1))
                    used(thin(k0 + m, lambda c: stat_v[m][:, c * B:(c + 2) * B], 7, 0, False, False))
            with te.Fori(0, NO // NSLOT) as i:
                for m in range(NSLOT):
                    te.wait_ge(ld_slot[(k1 + m) % NSLOT], i * 16 + 16 * ((k1 + m) // NSLOT + 1))
                    te.wait_ge(ve["bank_turn"], i * NSLOT + (m + 1))
                    used(thin(k1 + m, lambda c: wft[:, c * 2 * B:(c + 1) * 2 * B], 4 + m, 0, True, True))
            te.wait_ge(ve["stage"], NO)
            te.wait_ge(ld_band, 16 * (RG + 2))
            for layer in range(NCONV):
                src, halo, hs = (xa4, halo_of[0], halo_x) if layer % 2 == 0 else (xb4, halo_of[1], halo_y)
                b0 = 4 * (layer % 2)
                for g in range(G):
                    if layer:
                        te.wait_ge(ve["conv"] if layer % 2 == 0 else ac["conv"],
                                   G * layer // 2 - G + g + 1 if layer % 2 == 0 else G * (layer // 2) + g + 1)
                    for dw in range(3):
                        te.matmul(bank[:, b0 + g, :], bands[:, layer * 3 + dw, C:C + P],
                                  src[:, g, dw:dw + S, :], start=(dw == 0), stop=False)
                te.wait_ge(hs, 96 * (layer // 2 + 1))
                for g in range(G):
                    te.matmul(bank[:, b0 + g, :], hmats[0:6 * C, layer, :], halo[0:6 * C, g, :],
                              start=False, stop=True).then_inc(pe["conv"], 1)

            def fields(k, c, first, wait):
                par_ = c % 2
                a3 = h_a[c].rearrange("p (w b) -> p w b", b=B)
                s3 = h_s[c].rearrange("p (w b) -> p w b", b=B)
                b1 = 5 * par_
                te.wait_ge(po["a"], k + 1)
                if wait:
                    te.wait_ge(ac["evac1"], k - 1)
                te.matmul(bank[:, b1, :], mat("SV", first), a3[:, 1:S + 1], start=True, stop=True)
                for n, (m, sh) in enumerate((("DS", 0), ("2DS", 1), ("DS", 2))):
                    te.matmul(bank[:, b1 + 2, :], mat(m, first), a3[:, sh:sh + S], start=(n == 0), stop=(n == 2))
                te.wait_ge(po["s"], k + 1)
                te.matmul(bank[:, b1 + 1, :], mat("DV", first), s3[:, 1:S + 1],
                          start=True, stop=True).then_inc(pe["fld1"], 1)
                if wait or c:
                    te.wait_ge(ac["evac2"], k)
                for n, (m, sh) in enumerate((("DD", 0), ("2DD", 1), ("DD", 2))):
                    te.matmul(bank[:, 3, :], mat(m, first), s3[:, sh:sh + S], start=(n == 0), stop=(n == 2))
                te.matmul(bank[:, 4, :], mat("SS", first), a3[:, 2:S + 2], start=True, stop=False)
                te.matmul(bank[:, 4, :], mat("-SS", first), a3[:, 0:S], start=False, stop=True).then_inc(pe["fld2"], 1)

            te.wait_ge(ld_vm, 32)
            te.wait_ge(ve["conv"], G * NCONV // 2)
            for k in range(4):
                fields(k, k, True, k >= 2)
            with te.Fori(1, STEPS) as i:
                for c in range(NCH):
                    fields(i * NCH + c, c, False, True)
            te.wait_ge(ac["evac2"], SLOTS)
            for x in range(NCH):
                te.wait_ge(ve["pad"], SLOTS - NCH + x + 1)
                te.matmul(bank[:, x, :], edge_m, u[:, x, 1:S + 1, :], start=True, stop=True).then_inc(pe["edge"], 1)

        @block.vector
        def _(v):
            n_order = [0]

            def then(ins):
                n_order[0] += 1
                ins.then_inc(ve["order"], 1)
                v.wait_ge(ve["order"], n_order[0])

            def kb(row, k):
                return row.unsqueeze(1).to_broadcast([P, k, row.shape[1]])

            then(v.memset(ones[:, :], 1.0))
            then(v.memset(eps_ln, LN_EPS))
            then(v.memset(d_eps, D_EPS))
            then(v.memset(ln2, 0.6931471805599453))
            then(v.memset(xw[:, P * B:], 0.0))
            v.memset(pln, 0.0).then_inc(ve["consts"], 1)
            v.wait_ge(ve["consts"], 1)
            v.wait_ge(ld_patch, 16)
            v.tensor_reduce(patch_part, fl.rearrange("p k t -> p t k"), AX.X, ALU.add).then_inc(ve["patch_part"], 1)
            v.wait_ge(ld_win, 16)
            v.tensor_reduce(wsum, xwk.rearrange("p k b -> p b k"), AX.X, ALU.add).then_inc(ve["win_sums"], 1)
            v.wait_ge(pe["patch_mean"], 1)
            mean = reg_c[:, 0:TOK]
            then(v.tensor_scalar(mean, bank[:, 0, 0:TOK], 1.0 / PD, None, ALU.mult))
            v.tensor_tensor(fl, fl, kb(mean, KC), ALU.subtract).then_inc(ve["patch_centred"], 1)
            for w2 in range(2):
                ins = v.tensor_reduce(reg_g[:, w2 * 256:(w2 + 1) * 256],
                                      xw[:, w2 * 1024:(w2 + 1) * 1024].rearrange("p (w n) -> p n w", w=4), AX.X, ALU.add)
                if w2 == 0:
                    then(ins)
            ins.then_inc(ve["win_sums"], 1)
            v.wait_ge(ac["patch_sq"], 1)
            v.tensor_reduce(patch_part2, sq.rearrange("p k t -> p t k"), AX.X, ALU.add).then_inc(ve["patch_part"], 1)
            v.wait_ge(ac["patch_std"], 1)
            v.wait_ge(ld_prm, 16)
            v.wait_ge(ve["patch_centred"], 1)
            then(v.reciprocal(rstd_p, rstd_p))
            for c in range(KC):
                v.scalar_tensor_tensor(fl[:, c, :], fl[:, c, :], par("pn_g")[:, c:c + 1], rstd_p,
                                       ALU.mult, ALU.mult).then_inc(ve["fl"], 1)
            v.wait_ge(pe["win_mean"], 1)
            v.wait_ge(ve["win_sums"], 2)
            then(v.tensor_scalar(wsum, bank[:, 2, 0:B], 1.0 / WD, None, ALU.mult))
            v.wait_ge(pe["pool"], 1)
            v.tensor_tensor(xwk, xwk, kb(wsum, P), ALU.subtract).then_inc(ve["win_centred"], 1)
            for q in range(4):
                then(v.tensor_copy(pl[32 * q:32 * q + 32, :], bank[32 * q:32 * q + 32, 3, q * P:(q + 1) * P]))
            pl3 = pl.rearrange("p (k b) -> p k b", b=B)
            plq3 = pl_sq.rearrange("p (k b) -> p k b", b=B)
            v.tensor_reduce(pl_sum, pl3.rearrange("p k b -> p b k"), AX.X, ALU.add).then_inc(ve["pl_sums"], 1)
            v.wait_ge(ac["win_sq"], 1)
            v.tensor_reduce(wsq_sum, wsq.rearrange("p k b -> p b k"), AX.X, ALU.add).then_inc(ve["win_sq_sums"], 1)
            v.wait_ge(pe["pl_mean"], 1)
            then(v.tensor_scalar(pl_sum, bank[:, 1, 0:B], 1.0 / PD, None, ALU.mult))
            then(v.tensor_tensor(pl3, pl3, kb(pl_sum, KC), ALU.subtract))
            then(v.tensor_tensor(pl_sq, pl, pl, ALU.mult))
            v.tensor_reduce(pl_sq_sum, plq3.rearrange("p k b -> p b k"), AX.X, ALU.add).then_inc(ve["pl_sq_sums"], 1)
            v.wait_ge(ac["win_std"], 1)
            v.wait_ge(ve["win_centred"], 1)
            then(v.reciprocal(wrstd, wrstd))
            then(v.tensor_tensor(xwk, xwk, kb(wrstd, P), ALU.mult))
            then(v.tensor_tensor(xwk, xwk, par("wn_g").unsqueeze(2).to_broadcast([P, P, B]), ALU.mult))
            v.tensor_tensor(xwk, xwk, par("wn_b").unsqueeze(2).to_broadcast([P, P, B]), ALU.add).then_inc(ve["xw"], 1)
            v.wait_ge(ac["pl_std"], 1)
            then(v.reciprocal(pl_rstd, pl_rstd))
            then(v.tensor_tensor(pl3, pl3, kb(pl_rstd, KC), ALU.mult))
            then(v.tensor_tensor(pl3, pl3, par("pln_g").unsqueeze(2).to_broadcast([P, KC, B]), ALU.mult))
            v.tensor_tensor(pln.rearrange("p (k b) -> p k b", b=2 * B)[:, :, 0:B], pl3,
                            par("pln_b").unsqueeze(2).to_broadcast([P, KC, B]), ALU.add).then_inc(ve["pln"], 1)
            for n in range(4):
                v.wait_ge(pe["scores"], n + 1)
                if n == 0:
                    v.wait_ge(ac["qkv"], 12)
                then(v.scalar_tensor_tensor(prob[:, 4 * n:4 * n + 4, :],
                                            bank[:, n, :].rearrange("p (i k) -> p i k", k=P), DH ** -0.5,
                                            kb(par("mask"), 4), ALU.mult, ALU.add))
            v.tensor_reduce(negmax, prob, AX.X, ALU.max, negate=True).then_inc(ve["negmax"], 1)
            v.wait_ge(ac["exp"], NBLK)
            then(v.reciprocal(pinv, psum_exp))
            v.tensor_tensor(prob, prob, pinv.unsqueeze(2).to_broadcast([P, NBLK, P]), ALU.mult).then_inc(ve["prob"], 1)
            v.wait_ge(ac["vt"], 4)
            then(v.tensor_scalar(reg_g[:, :], reg_f[:, :], par("cp_w")[:, 4:5], par("cp_b"), ALU.mult, ALU.add))

            def tap(kh_, kw_):
                w = par("cp_w")[:, kh_ * 3 + kw_:kh_ * 3 + kw_ + 1]
                dg, dj = kh_ - 1, kw_ - 1
                g0, g1 = max(0, -dg), G - max(0, dg)
                if dj == 0:
                    o = reg_g[:, :].rearrange("p (n r) -> p n r", r=G * BL)[:, :, g0 * BL:g1 * BL]
                    i_ = reg_f[:, :].rearrange("p (n r) -> p n r", r=G * BL)[:, :, (g0 + dg) * BL:(g1 + dg) * BL]
                    then(v.scalar_tensor_tensor(o, i_, w, o, ALU.mult, ALU.add))
                    return
                j0, j1 = max(0, -dj), PPW - max(0, dj)
                if dg == 0:
                    o, i_ = pf_t[:, :, j0 * 32:j1 * 32], v_t[:, :, (j0 + dj) * 32:(j1 + dj) * 32]
                    then(v.scalar_tensor_tensor(o, i_, w, o, ALU.mult, ALU.add))
                    return
                for j in range(j0, j1):
                    o = pf_t[:, :, j * 32 + g0 * BL:j * 32 + g1 * BL]
                    i_ = v_t[:, :, (j + dj) * 32 + (g0 + dg) * BL:(j + dj) * 32 + (g1 + dg) * BL]
                    ins = v.scalar_tensor_tensor(o, i_, w, o, ALU.mult, ALU.add)
                    if j < j1 - 1:
                        continue
                    then(ins)

            for kh_ in range(3):
                for kw_ in range(3):
                    if (kh_, kw_) != (1, 1):
                        tap(kh_, kw_)
            for n in range(4):
                v.wait_ge(pe["attn"], n + 1)
                v.tensor_tensor(pf_t[:, 4 * n:4 * n + 4, :], pf_t[:, 4 * n:4 * n + 4, :],
                                bank[:, n, :].rearrange("p (i k) -> p i k", k=P), ALU.add).then_inc(ve["pf"], 1)
            v.wait_ge(pe["slot_used"], U_PREFIX)
            v.wait_ge(ac["wwk"], 1)
            qk = reg_b[:, 256:512]
            then(v.tensor_tensor(qk, bank[:, 6, 0:256], reg_b[:, 0:256], ALU.mult))
            then(v.tensor_reduce(logit, qk.rearrange("p (h d) -> p h d", h=2), AX.X, ALU.add))
            then(v.tensor_scalar(logit, logit, DH ** -0.5, None, ALU.mult))
            then(v.tensor_reduce(lmax, logit.unsqueeze(2), AX.X, ALU.max))
            v.tensor_tensor(logit, logit, lmax, ALU.subtract).then_inc(ve["dsl"], 1)
            v.wait_ge(ac["wwk"], 2)
            then(v.tensor_reduce(lmax, wexp.unsqueeze(2), AX.X, ALU.add))
            then(v.reciprocal(lmax, lmax))
            then(v.tensor_tensor(wwt, wexp, lmax, ALU.mult))
            then(v.tensor_scalar(line, wwt, 0.5, None, ALU.is_lt))
            then(v.tensor_scalar(ds, wwt, 0.5, None, ALU.max))
            then(v.tensor_tensor(nds, wwt, wwt, ALU.subtract))
            then(v.tensor_scalar(omd, wwt, -1.0, 1.0, ALU.mult, ALU.add))
            then(v.tensor_scalar(omd, omd, 0.5, None, ALU.max))
            then(v.reciprocal(fct, omd))
            then(v.tensor_scalar(fct, fct, 0.5, -1.0, ALU.mult, ALU.add))
            then(v.tensor_tensor(fct, fct, line, ALU.mult))
            then(v.scalar_tensor_tensor(nds, fct, 1.0, nds, ALU.add, ALU.mult))
            then(v.tensor_scalar(reg_b[:, 0:64], ones[:, 0:64], ds[:, 0:1], None, ALU.mult))
            v.tensor_scalar(reg_b[:, 64:128], ones[:, 0:64], ds[:, 1:2], None, ALU.mult).then_inc(ve["dsl"], 1)
            v.wait_ge(pe["ds"], 1)
            for t in range(TT):
                then(v.tensor_copy(dst[:, t * 32:(t + 1) * 32].rearrange("p (g b) -> p g b", b=BL),
                                   bank[:, 3, 0:64].rearrange("p (g b) -> p g b", b=B)[:, :, t * BL:(t + 1) * BL]))
            v.wait_ge(ac["rows"], 4)
            v.wait_ge(ld_img, 16)
            v.wait_ge(po["zero"], 1)
            for t in range(TT):
                tr = reg_b[:, 1024 * (1 - t):1024 * (2 - t)].rearrange("p (w n) -> p w n", n=32)
                then(v.transpose(tr, rows[:, t, :].rearrange("p (r w c) -> p w r c", r=2, w=S)))
                then(v.tensor_tensor(tr, tr, kb(dst[:, t * 32:(t + 1) * 32], S), ALU.mult))
                xv = xa4[:, :, 1:S + 1, t * BL:(t + 1) * BL].rearrange("p g w b -> p w g b")
                v.tensor_tensor(xv, xv, tr.rearrange("p w (g b) -> p w g b", b=BL), ALU.add).then_inc(ve["img"], 1)
            v.wait_ge(ac["wv"], 1)
            wv_s, w0, t1, t2 = (reg_b[:, 256 * n:256 * n + 256] for n in range(4))
            for h in range(2):
                then(v.tensor_scalar(w0[:, h * P:(h + 1) * P], wv_s[:, h * P:(h + 1) * P], nds[:, h:h + 1], None, ALU.mult))
            then(v.transpose(t1, wv_s))
            then(v.transpose(t2, w0))
            r3 = lambda a: a.rearrange("p (k b) -> p k b", b=2 * B)
            cb = lambda n: par(n).unsqueeze(2).to_broadcast([P, KC, 2 * B])
            then(v.tensor_tensor(r3(t1), r3(t1), cb("cw_w"), ALU.mult))
            then(v.tensor_tensor(r3(t1), r3(t1), cb("cw_b"), ALU.add))
            v.wait_ge(ve["img"], TT)
            v.tensor_tensor(wft, t1, t2, ALU.add).then_inc(ve["bank_turn"], NSLOT)
            with v.Fori(0, NO // NSLOT) as i:
                for m in range(NSLOT):
                    v.wait_ge(pe["slot_used"], i * NSLOT + (U_V + m + 1))
                    tr = reg_b[:, 1024 + 256 * m:1024 + 256 * (m + 1)]
                    v.transpose(tr, bank[:, 4 + m, 0:256]).then_inc(ve["bank_turn"], 1)
                    v.wait_ge(ve["bank_turn"], i * NSLOT + (NSLOT + m + 1))
                    xv = xa4[:, bass.ds(i, 1), 1 + 8 * m:9 + 8 * m, :].rearrange("p g w b -> p (g w) b")
                    v.tensor_tensor(xv, xv, tr.rearrange("p (w b) -> p w b", b=2 * B)[:, :, 0:B],
                                    ALU.add).then_inc(ve["stage"], 1)
            for n in range(G * NCONV // 2):
                layer, g = 1 + 2 * (n // G), n % G
                v.wait_ge(pe["conv"], layer * G + g + 1)
                if n == 0:
                    v.wait_ge(ve["stage"], NO)
                    v.wait_ge(halo_x, 96)
                if n == G:
                    v.wait_ge(ve["conv"], G)
                    v.wait_ge(halo_x, 192)
                v.scalar_tensor_tensor(xa4[:, g, 1:S + 1, :], bank[:, 4 + g, :].rearrange("p (w b) -> p w b", b=B),
                                       par("conv_b")[:, layer:layer + 1], xa4[:, g, 1:S + 1, :],
                                       ALU.add, ALU.add).then_inc(ve["conv"], 1)

            def f(par_, n, m=1):
                return fld[par_][:, n * ROW:(n + m) * ROW]

            def slot_step(k, q, c, new, old):
                n, uc = 1 - q, u[:, c, 1:S + 1, :]
                if old:
                    v.wait_ge(po["nk"], k - 1)
                    v.wait_ge(ac["inv"], k - 1)
                    v.wait_ge(ve["hn"], k - 1)
                    v.tensor_tensor(kh[q], num[q], inv[q], ALU.mult).then_inc(ve["kh"], 1)
                if new:
                    v.wait_ge(ac["evac1"], k)
                    v.tensor_scalar(f(n, 0, 3), f(n, 0, 3), 10.0, -10.0, ALU.min, ALU.max).then_inc(ve["clip1"], 1)
                if old:
                    v.wait_ge(ve["kh"], k - 1)
                    v.tensor_scalar(kh[q], kh[q], 5.0, -5.0, ALU.min, ALU.max).then_inc(ve["cliph"], 1)
                if new:
                    v.wait_ge(ac["evac2"], k)
                    v.tensor_scalar(f(n, 3, 2), f(n, 3, 2), 10.0, -10.0, ALU.min, ALU.max).then_inc(ve["clip2"], 1)
                    v.wait_ge(ac["sqr"], k)
                    v.scalar_tensor_tensor(slope[n], sqs[n][:, 0:ROW], 1.0, sqs[n][:, ROW:2 * ROW],
                                           ALU.add, ALU.add).then_inc(ve["slope"], 1)
                    v.wait_ge(ve["clip2"], k)
                    v.scalar_tensor_tensor(ab[n], sqs[n][:, 0:2 * ROW], 1.0, f(n, 3, 2),
                                           ALU.add, ALU.mult).then_inc(ve["outer"], 1)
                if old:
                    v.wait_ge(ac["beta"], k - 1)
                    v.scalar_tensor_tensor(dif[q], kh[q][:, 0:ROW], par("alpha"), hb[q],
                                           ALU.mult, ALU.add).then_inc(ve["diff"], 1)
                if new:
                    v.wait_ge(po["cxy"], k)
                    v.scalar_tensor_tensor(cxy[n], cxy[n], -2.0, f(n, 2), ALU.mult, ALU.mult).then_inc(ve["cross"], 1)
                if old:
                    v.wait_ge(ve["diff"], k - 1)
                    v.tensor_scalar(dif[q], dif[q], 1.0, -1.0, ALU.min, ALU.max).then_inc(ve["clipd"], 1)
                if new:
                    v.wait_ge(ve["cross"], k)
                    v.wait_ge(po["absum"], k)
                    v.tensor_tensor(num[n][:, ROW:2 * ROW], abs_[n], cxy[n], ALU.add).then_inc(ve["hn"], 1)
                if old:
                    v.wait_ge(ve["clipd"], k - 1)
                    v.scalar_tensor_tensor(uc, dif[q].rearrange("p (w b) -> p w b", b=B), DT, uc,
                                           ALU.mult, ALU.add).then_inc(ve["u"], 1)
                    v.wait_ge(ve["u"], k - 1)
                    v.tensor_copy(u[:, c, 1:S + 1:S - 1, :], u[:, c, 2:S:S - 3, :]).then_inc(ve["pad"], 1)

            v.wait_ge(pe["slot_used"], U_ALL)
            v.wait_ge(po["padz"], 1)
            for n in ("alpha", "beta"):
                then(v.scalar_tensor_tensor(par(n), par(n), -1.0, par(n), ALU.mult, ALU.max))
            for x in range(NCH):
                v.wait_ge(ld_u[x], 16)
                v.tensor_copy(u[:, x, 1:S + 1, :], x3[:, x, :].rearrange("p (w b) -> p w b", b=B)).then_inc(ve["u0"], 1)
            slot_step(1, 1, 0, True, False)
            for k in range(2, 6):
                slot_step(k, k % 2, (k - 2) % NCH, True, True)
            with v.Fori(1, (SLOTS - 2) // NCH) as i:
                for m in range(NCH):
                    slot_step(i * NCH + (m + 2), m % 2, m, True, True)
            for k in range(NCH * ((SLOTS - 2) // NCH) + 2, SLOTS + 2):
                slot_step(k, k % 2, (k - 2) % NCH, k <= SLOTS, True)
            for x in range(NCH):
                v.wait_ge(pe["edge"], x + 1)
                v.wait_ge(ac["x3"], x + 1)
                if x == 0:
                    v.wait_ge(ve["diff"], SLOTS)
                v.scalar_tensor_tensor(result(x), bank[:, x, :], 0.7, x3[:, x, :], ALU.mult, ALU.add).then_inc(ve["fin"], 1)

        @block.scalar
        def _(a):
            a.dma_start(prm[:, :], params).then_inc(ld_prm, 16)
            nc.scalar.preload_act_table_set("sqrt_and_others")
            a.wait_ge(ve["consts"], 1)
            a.wait_ge(ve["patch_centred"], 1)
            a.activation(reg_b[:, :], reg_a[:, :], ACT.Square).then_inc(ac["patch_sq"], 1)
            a.wait_ge(pe["patch_var"], 1)
            a.activation(rstd_p, bank[:, 1, 0:TOK], ACT.Sqrt, bias=eps_ln, scale=1.0 / PD).then_inc(ac["patch_std"], 1)
            a.wait_ge(ld_prm, 16)
            for c in range(KC):
                a.wait_ge(ve["fl"], c + 1)
                a.activation(fl[:, c, :], fl[:, c, :], ACT.Identity, bias=par("pn_b")[:, c:c + 1]).then_inc(ac["fl"], 1)
            a.wait_ge(ve["win_centred"], 1)
            a.activation(reg_g[:, :], xw[:, 0:P * B], ACT.Square).then_inc(ac["win_sq"], 1)
            for n in range(4):
                a.wait_ge(pe["qkv"], n + 1)
                a.activation(reg_c[:, n * 512:(n + 1) * 512], bank[:, 4 + n % 2, :], ACT.Copy).then_inc(ac["qkv"], 1)
            a.wait_ge(po["zero"], 1)
            a.dma_start(xa4[:, :, 1:S + 1, :], x_conv.rearrange("p (g w b) -> p g w b", g=G, b=B)).then_inc(ld_img, 16)
            a.wait_ge(pe["win_var"], 1)
            a.activation(wrstd, bank[:, 0, 0:B], ACT.Sqrt, bias=eps_ln, scale=1.0 / WD).then_inc(ac["win_std"], 1)
            for n in range(4):
                a.wait_ge(pe["qkv"], 4 + n + 1)
                a.activation(reg_d[:, n * 512:(n + 1) * 512], bank[:, 4 + n % 2, :], ACT.Copy).then_inc(ac["qkv"], 1)
            a.wait_ge(pe["pl_var"], 1)
            a.activation(pl_rstd, bank[:, 2, 0:B], ACT.Sqrt, bias=eps_ln, scale=1.0 / PD).then_inc(ac["pl_std"], 1)
            for n in range(4):
                a.wait_ge(pe["qkv"], 8 + n + 1)
                a.activation(reg_e[:, n * 512:(n + 1) * 512], bank[:, 4 + n % 2, :], ACT.Copy).then_inc(ac["qkv"], 1)
            for n in range(4):
                a.wait_ge(pe["vt"], n + 1)
                a.activation(reg_f[:, n * 512:(n + 1) * 512], bank[:, 4 + n % 2, :], ACT.Copy).then_inc(ac["vt"], 1)
            a.wait_ge(ve["negmax"], 1)
            for i in range(NBLK):
                a.activation(prob[:, i, :], prob[:, i, :], ACT.Exp, bias=negmax[:, i:i + 1],
                             accum_out=psum_exp[:, i:i + 1]).then_inc(ac["exp"], 1)
            for n in range(4):
                a.wait_ge(pe["pt"], n + 1)
                a.activation(reg_b[:, n * 512:(n + 1) * 512], bank[:, 4 + n % 2, :], ACT.Copy).then_inc(ac["pt"], 1)
            for n in range(4):
                a.wait_ge(pe["out"], n + 1)
                a.activation(reg_c[:, n * 512:(n + 1) * 512], bank[:, 4 + n % 2, :], ACT.Copy).then_inc(ac["rows"], 1)
            a.wait_ge(pe["slot_used"], U_PREFIX)
            a.activation(reg_b[:, 0:256], bank[:, 6, 256:512], ACT.Copy).then_inc(ac["wwk"], 1)
            a.wait_ge(ve["dsl"], 1)
            a.activation(wexp, logit, ACT.Exp).then_inc(ac["wwk"], 1)
            a.wait_ge(pe["slot_used"], U_V)
            a.wait_ge(ve["img"], TT)
            a.activation(reg_b[:, 0:256], bank[:, 7, 0:256], ACT.Copy).then_inc(ac["wv"], 1)
            for n in range(G * NCONV // 2):
                layer, g = 2 * (n // G), n % G
                a.wait_ge(pe["conv"], layer * G + g + 1)
                if n == 0:
                    a.wait_ge(po["zero"], 2)
                if n == G:
                    a.wait_ge(halo_y, 96)
                a.activation(xb4[:, g, 1:S + 1, :], bank[:, g, :].rearrange("p (w b) -> p w b", b=B), ACT.Relu,
                             bias=par("conv_b")[:, layer:layer + 1]).then_inc(ac["conv"], 1)

            def slot_step(k, q, new, old):
                n = 1 - q
                if new:
                    a.wait_ge(pe["fld1"], k)
                    a.activation(fld[n][:, 0:3 * ROW], bank[:, 5 * n:5 * n + 3, :].rearrange("p x n -> p (x n)"),
                                 ACT.Copy).then_inc(ac["evac1"], 1)
                    a.wait_ge(pe["fld2"], k)
                    a.activation(fld[n][:, 3 * ROW:5 * ROW], bank[:, 3:5, :].rearrange("p x n -> p (x n)"),
                                 ACT.Copy).then_inc(ac["evac2"], 1)
                    a.wait_ge(ve["clip1"], k)
                    a.activation(sqs[n], fld[n][:, 0:3 * ROW], ACT.Square).then_inc(ac["sqr"], 1)
                if old:
                    a.wait_ge(ve["cliph"], k - 1)
                    a.activation(hb[q], kh[q][:, ROW:2 * ROW], ACT.Copy, scale=par("beta")).then_inc(ac["beta"], 1)
                if not new:
                    return
                q = n
                a.wait_ge(ve["slope"], k)
                a.activation(lnw[q], slope[q], ACT.Ln, bias=d_eps).then_inc(ac["lnw"], 1)
                a.activation(den[q][:, 0:ROW], slope[q], ACT.Square).then_inc(ac["psq"], 1)
                a.wait_ge(ac["lnw"], k)
                a.activation(den[q][:, ROW:2 * ROW], lnw[q], ACT.Exp, bias=ln2, scale=1.5).then_inc(ac["w15"], 1)
                a.wait_ge(ac["psq"], k)
                a.wait_ge(ac["w15"], k)
                a.activation(den[q], den[q], ACT.Ln, bias=d_eps).then_inc(ac["lnd"], 1)
                a.wait_ge(ac["lnd"], k)
                a.activation(inv[q], den[q], ACT.Exp, scale=-1.0).then_inc(ac["inv"], 1)

            nc.scalar.preload_act_table_set("natural_log_exp_and_others")
            a.wait_ge(ve["u0"], NCH)
            for x in range(NCH):
                a.activation(x3[:, x, :], x3[:, x, :], ACT.Copy, scale=0.3).then_inc(ac["x3"], 1)
            slot_step(1, 1, True, False)
            for k in range(2, 6):
                slot_step(k, k % 2, True, True)
            with a.Fori(1, (SLOTS - 2) // NCH) as i:
                for m in range(NCH):
                    slot_step(i * NCH + (m + 2), m % 2, True, True)
            for k in range(NCH * ((SLOTS - 2) // NCH) + 2, SLOTS + 2):
                slot_step(k, k % 2, k <= SLOTS, True)

        @block.gpsimd
        def _(p):
            p.memset(xa[:, :], 0.0).then_inc(po["zero"], 1)
            p.wait_ge(pe["scores"], 4)
            p.memset(reg_d[:, :], 0.0).then_inc(po["zero"], 1)
            p.wait_ge(pe["attn"], 4)
            p.wait_ge(ve["xw"], 1)
            for m in range(NSLOT):
                n = V_FIRST + m
                p.tensor_copy(stat_v[m], xw[:, n * KC * B:n * KC * B + STATF]).then_inc(po["stat"], 1)
            with p.Fori(1, (NV - V_FIRST) // NSLOT) as i:
                for m in range(NSLOT):
                    p.wait_ge(pe["slot_used"], i * NSLOT + (U_PREFIX + m - NSLOT + 1))
                    p.tensor_copy(stat_v[m], xw[:, bass.ds(i * (NSLOT * KC * B) + (V_FIRST + m) * KC * B, STATF)])\
                        .then_inc(po["stat"], 1)
            p.wait_ge(ve["img"], TT)
            p.memset(bands, 0.0).then_inc(po["bandz"], 1)
            p.wait_ge(po["bandz"], 1)
            for r in range(RG):
                p.dma_start(bands[r * C:(r + 1) * C, :, r * C:(r + 3) * C],
                            conv_band.rearrange("c (m n) -> c m n", n=3 * C)).then_inc(ld_band, 16)
            p.wait_ge(pe["slot_used"], U_V)
            p.memset(hmats, 0.0).then_inc(po["bandz"], 1)
            p.wait_ge(po["bandz"], 2)
            halo_src = conv_halo.rearrange("c (s m n) -> c s m n", s=2, n=C)
            p.dma_start(hmats[0:3 * C, :, 0:C], halo_src[:, 0]).then_inc(ld_band, 16)
            p.dma_start(hmats[3 * C:6 * C, :, P - C:P], halo_src[:, 1]).then_inc(ld_band, 16)
            p.memset(reg_e[:, :], 0.0).then_inc(po["zero"], 1)
            p.wait_ge(ve["pf"], 4)
            p.memset(reg_f[:, :], 0.0).then_inc(po["zero"], 1)
            p.wait_ge(pe["slot_used"], U_ALL)
            p.memset(u, 0.0).then_inc(po["padz"], 1)
            p.wait_ge(st_rows, 16 * G)

            def horizontal(k, c, later):
                if not later:
                    p.wait_ge(ve["u0"], k + 1)
                else:
                    p.wait_ge(ve["pad"], k - (NCH - 1))
                    p.wait_ge(pe["fld2"], k - (NCH - 1))
                uc = u[:, c].rearrange("p w b -> p (w b)")
                p.tensor_tensor(h_a[c][:, B:(S + 1) * B], uc[:, 2 * B:], uc[:, 0:S * B], ALU.subtract).then_inc(po["a"], 1)
                p.tensor_tensor(h_t[c % 2][:, 0:(S + 1) * B], uc[:, 0:(S + 1) * B], uc[:, B:], ALU.add).then_inc(po["t"], 1)
                p.wait_ge(po["t"], k + 1)
                p.tensor_tensor(h_s[c][:, B:(S + 1) * B], h_t[c % 2][:, 0:S * B], h_t[c % 2][:, B:(S + 1) * B],
                                ALU.add).then_inc(po["s"], 1)

            def products(k, q):
                p.wait_ge(ve["clip1"], k)
                p.tensor_tensor(cxy[q], fld[q][:, 0:ROW], fld[q][:, ROW:2 * ROW], ALU.mult).then_inc(po["cxy"], 1)
                p.wait_ge(ve["clip2"], k)
                p.tensor_tensor(mxy[q], fld[q][:, 3 * ROW:4 * ROW], fld[q][:, 4 * ROW:5 * ROW], ALU.mult).then_inc(po["m"], 1)
                p.wait_ge(ve["outer"], k)
                p.tensor_tensor(abs_[q], ab[q][:, 0:ROW], ab[q][:, ROW:2 * ROW], ALU.add).then_inc(po["absum"], 1)
                p.wait_ge(po["m"], k)
                p.wait_ge(ac["sqr"], k)
                p.tensor_tensor(num[q][:, 0:ROW], mxy[q], sqs[q][:, 2 * ROW:3 * ROW], ALU.subtract).then_inc(po["nk"], 1)

            horizontal(0, 0, False)
            horizontal(1, 1, False)
            for k in range(1, 6):
                horizontal(k + 1, (k + 1) % NCH, k + 1 >= NCH)
                products(k, (k - 1) % 2)
            with p.Fori(1, (SLOTS - 2) // NCH) as i:
                for m in range(NCH):
                    k = i * NCH + (m + 2)
                    horizontal(k + 1, (m + 3) % NCH, True)
                    products(k, (m + 1) % 2)
            for k in range(NCH * ((SLOTS - 2) // NCH) + 2, SLOTS + 1):
                if k + 1 < SLOTS:
                    horizontal(k + 1, (k + 1) % NCH, True)
                products(k, (k - 1) % 2)
    return nc


def vertical_operators(np):
    sv = np.eye(S) * 2 + np.eye(S, k=1) + np.eye(S, k=-1)
    dv = np.eye(S, k=1) - np.eye(S, k=-1)
    edge = np.eye(S)
    edge[0], edge[S - 1] = edge[1], edge[S - 2]
    ops = {"SV": sv / 8, "DV": dv / 8, "SS": sv @ sv / 64, "-SS": -sv @ sv / 64, "DS": dv @ sv / 64,
           "2DS": 2 * dv @ sv / 64, "DD": dv @ dv / 64, "2DD": 2 * dv @ dv / 64}
    four = lambda m: np.kron(np.eye(P // S), m.T)
    mats = [four(ops[n]) for n in MATS] + [four(ops[n] @ edge) for n in MATS]
    return (np.concatenate(mats, 1).astype(np.float32), four(edge).astype(np.float32))


def kernel(**inputs):
    import numpy as np
    import concourse.bacc as bacc
    from concourse.bass_utils import run_bass_kernel_spmd

    a = {k: np.asarray(v) for k, v in inputs.items()}
    x = a["x"]
    d = {}
    x8 = x.reshape(TT, BL, C, PPW, PS, PPW, PS)
    d["x_patch"] = x8.transpose(4, 6, 2, 0, 5, 3, 1).reshape(P, KC * TOK)
    d["x_window"] = x.transpose(2, 3, 1, 0).reshape(P, P * B)
    d["x_conv"] = x.reshape(B, C, G, RG, S).transpose(3, 1, 2, 4, 0).reshape(P, G * ROW)
    L0 = {k[len("L0_conv_"):]: v for k, v in a.items() if k.startswith("L0_conv_")}
    d["wqk_p"], d["wv_p"], d["wout_p"] = L0["Wqk_p"], L0["Wv_p"], L0["Wout_p"]
    d["wqk_w"] = L0["Wqk_w"].reshape(32, 4, KC, 2, PD).transpose(3, 1, 0, 2, 4).reshape(2, P, SLOTF)
    d["wv_w"] = L0["Wv_w"].reshape(P, NV, SLOTF).transpose(1, 0, 2)
    d["wout_w"] = L0["Wout_w"].reshape(4, KC, 32, G, 4, 2, 4, 8, C).transpose(3, 6, 0, 2, 1, 4, 7, 5, 8)\
        .reshape(NO, P, SLOTF)
    by_quadrant = lambda t: np.broadcast_to(t.reshape(1, 4, 32).transpose(0, 2, 1)[:, :, None, :], (4, 32, 2, 4)).reshape(P, KC)
    conv_w = np.stack([a[f"L{l}_conv_w{i}"] for l in (1, 2) for i in (1, 2)])
    conv_b = np.stack([a[f"L{l}_conv_b{i}"] for l in (1, 2) for i in (1, 2)])
    d["conv_band"] = conv_w[:, :, :, ::-1, :].transpose(2, 0, 4, 3, 1).reshape(C, 3 * NCONV * 3 * C)
    d["conv_halo"] = conv_w[:, :, :, 0::2, :].transpose(4, 2, 3, 0, 1).reshape(3 * C, 2 * NCONV * C)
    tok = np.arange(P)
    rows = tok // 4
    pooled_at = np.arange(P) % 32
    cols = {
        "pn_g": L0["pn_g"].reshape(P, KC), "pn_b": L0["pn_b"].reshape(P, KC),
        "pln_g": L0["pln_g"].reshape(32, 4, KC).transpose(1, 0, 2).reshape(P, KC),
        "pln_b": L0["pln_b"].reshape(32, 4, KC).transpose(1, 0, 2).reshape(P, KC),
        "wn_g": L0["wn_g"].reshape(P, P), "wn_b": L0["wn_b"].reshape(P, P),
        "cp_w": L0["conv_p_w"].reshape(DH, 9), "cp_b": L0["conv_p_b"].reshape(DH, 1),
        "cw_w": by_quadrant(L0["conv_w_w"][:, 0, 1, 1]), "cw_b": by_quadrant(L0["conv_w_b"]),
        "conv_b": np.tile(conv_b.T, (RG, 1)),
        "alpha": np.broadcast_to(a["L3_conv_alpha_param"].reshape(1, 1), (P, 1)),
        "beta": np.broadcast_to(a["L3_conv_beta_param"].reshape(1, 1), (P, 1)),
        "ident": np.eye(P, dtype=np.float32),
        "mask": np.where(tok[:, None] % BL == tok[None] % BL, 0.0, -1e30).astype(np.float32),
        "pool": (((rows // 4)[:, None] * 4 + (tok % 4)[:, None]) == pooled_at[None]).astype(np.float32) / 16,
    }
    d["params"] = np.concatenate([cols[n] for n, _ in PARAMS], 1)
    d["vmats"], d["edge"] = vertical_operators(np)

    nc = bacc.Bacc("TRN2", target_bir_lowering=False, num_devices=1)
    arrays, args = {}, []
    for n in ("x_patch", "x_window", "x_conv", "params", "wqk_p", "wv_p", "wout_p", "wqk_w", "wv_w", "wout_w",
              "conv_band", "conv_halo", "vmats", "edge"):
        arrays[n] = np.ascontiguousarray(d[n])
        assert arrays[n].dtype == np.float32, n
        args.append(nc.dram_tensor(n, arrays[n].shape, F32, kind="ExternalInput").ap())
    args.append(nc.dram_tensor("y_rows", (C, S, ROW), F32, kind="Internal").ap())
    args.append(nc.dram_tensor("out", (NCH * P, ROW), F32, kind="ExternalOutput").ap())
    build(nc, *args)
    r = run_bass_kernel_spmd(nc, [arrays], core_ids=[0])
    return r.results[0]["out"].reshape(C, S, S, B).transpose(3, 0, 1, 2)
```

```python
from contextlib import ExitStack

import concourse.bass as bass
from concourse import mybir

F32 = mybir.dt.float32
FR = mybir.dt.float32r
ALU = mybir.AluOpType
ACT = mybir.ActivationFunctionType
AX = mybir.AxisListType

P = 128
B, C, S = 16, 16, 32
HEADS = 8
PS = 8
PPW = S // PS
TOK = B * PPW * PPW
PD = PS * PS * C
WD = S * S * C
DH = PD // HEADS
KC = PD // P
TT = TOK // P
NBLK = TT * HEADS
BL = B // TT
G = 4
RG = S // G
WP = S + 2
ROWF = WP * B
ROW = S * B
NSLOT = 4
SLOTF = KC * 1024
PREFIX = ["q", "V0", "V1", "k", "V2", "V3", "V4", "v", "V5", "V6", "V7", "wq", "wk", "o"]
NV = WD // P // KC
NO = WD // 1024
V_FIRST = 8
STEPS = 10
NCH = 4
CC = C // NCH
HALF = ROW // 2
SLOTS = STEPS * NCH
LOOP_FROM = NCH + 3
LOOPS = (SLOTS + 1 - LOOP_FROM) // NCH
LOOP_END = LOOP_FROM + NCH * LOOPS
LN_EPS, D_EPS, DT = 1e-5, 1e-6, 0.01
NCONV = 4

WB = 8
WAVES = S // WB
NPIECE = 4
QUAD = 32


def columns(w, layer):
    return (0 if w == 0 else WB * w - 1 - layer), (S if w == WAVES - 1 else WB * (w + 1) - 1 - layer)


def convs_after(s):
    if s == NO - 1:
        return [(WAVES - 1, layer) for layer in range(NCONV)]
    return [(w, s - G + 1 - G * w) for w in range(WAVES - 1) if 0 <= s - G + 1 - G * w < NCONV]


def halo_rows(eng, copy, shifts, w, layer, source, waits, halo_sem):
    a_, b_ = columns(w, layer)
    src, halo = source
    at = slice(a_ * B, b_ * B)
    cols = lambda part, g0, g1, dw: src[part, g0:g1, a_ + dw:b_ + dw, :].rearrange("p g w b -> p g (w b)")
    for semaphore, count in waits:
        eng.wait_ge(semaphore, count)
    for dw in shifts:
        copy(halo[dw * QUAD:(dw + 1) * QUAD, 1:G, at], cols(slice(P - QUAD, P), 0, G - 1, dw)).then_inc(halo_sem, 1)
    for n, dw in enumerate(shifts):
        eng.wait_ge(halo_sem, (w * NCONV + layer) * 2 * len(shifts) + n + 1)
        copy(halo[dw * QUAD:dw * QUAD + C, 0:G - 1, at], cols(slice(0, C), 1, G, dw)).then_inc(halo_sem, 1)


def pairs_done(w, layer, h):
    return (w * NCONV // 2 + layer // 2) * 2 + h + 1


PARAMS = [("pn_g", KC), ("pn_b", KC), ("pln_g", KC), ("pln_b", KC), ("wn_g", P), ("wn_b", P),
          ("cp_w", 9), ("cp_b", 1), ("cw_w", KC), ("cw_b", KC), ("conv_b", NCONV), ("alpha", 1), ("beta", 1),
          ("ident", P), ("mask", P), ("pool", P)]
COL, _at = {}, 0
for _n, _w in PARAMS:
    COL[_n] = (_at, _at + _w)
    _at += _w
NPARAM = _at
UX = ((1, "SV"), (-1, "-SV"))
UY = ((0, "2DV"), (1, "DV"), (-1, "DV"))
UXY = ((2, "DS"), (1, "2DS"), (-1, "-2DS"), (-2, "-DS"))
UYY = ((0, "6DD"), (1, "4DD"), (-1, "4DD"), (2, "DD"), (-2, "DD"))
UXX = ((0, "-2SS"), (2, "SS"), (-2, "SS"))
MATS = ["SV", "-SV", "DV", "2DV", "SS", "-2SS", "DS", "2DS", "-2DS", "-DS", "DD", "4DD", "6DD"]
NF = (S - 2) * B
NVM = 2 * len(MATS) * P


def build(nc, x_patch, x_window, x_conv, params, wqk_p, wv_p, wout_p, wqk_w, wv_w, wout_w,
          conv_band, conv_halo, vmats, edge, out):
    with ExitStack() as ctx:
        def sb(name, cols):
            return ctx.enter_context(nc.sbuf_tensor(name, [P, cols], F32))

        def sem(name):
            return ctx.enter_context(nc.semaphore(name))

        with ExitStack() as shared:
            vmr = shared.enter_context(nc.sbuf_tensor("vmr", [P, NVM], FR))
            u_parts = shared.enter_context(nc.sbuf_tensor("u_parts", [P, 2 * NCH * ROWF], FR))
        ring = sb("ring", NSLOT * SLOTF)
        prm = sb("prm", NPARAM)
        ones = sb("ones", P)
        xw = sb("xw", P * B + B)
        xa = sb("xa", G * ROWF)
        reg_a = sb("reg_a", 2048)
        reg_b = sb("reg_b", 2048)
        reg_c = sb("reg_c", 2048)
        reg_d = sb("reg_d", G * ROWF)
        reg_e = sb("reg_e", 2048)
        reg_f = sb("reg_f", 2048)
        reg_g = sb("reg_g", 2048)
        small = sb("small", 896)
        bank = ctx.enter_context(nc.psum_tensor("bank", [P, 8, 512], F32))

        def par(name):
            a, b = COL[name]
            return prm[:, a:b]

        ident = par("ident")
        pick = par("mask")

        slot = [ring[:, r * SLOTF:(r + 1) * SLOTF].rearrange("p (k n) -> p k n", k=KC) for r in range(NSLOT)]
        fl = reg_a[:, :].rearrange("p (k t) -> p k t", k=KC)
        prob = reg_a[:, :].rearrange("p (i k) -> p i k", i=NBLK)
        sq = reg_b[:, :].rearrange("p (k t) -> p k t", k=KC)
        prob_t = reg_b[:, :].rearrange("p (i q) -> p i q", i=NBLK)
        q_t = reg_c[:, :].rearrange("p (h t) -> p h t", h=HEADS)
        rows = reg_c[:, :].rearrange("p (t e) -> p t e", t=TT)
        k_t = reg_d[:, 0:2048].rearrange("p (h t) -> p h t", h=HEADS)
        v_tok = reg_e[:, :].rearrange("p (t e) -> p t e", t=TT)
        v_t = reg_f[:, :].rearrange("p (i t) -> p i t", i=NBLK)
        wsq = reg_g[:, :].rearrange("p (k b) -> p k b", b=B)
        pf_t = reg_g[:, :].rearrange("p (i t) -> p i t", i=NBLK)
        xwk = xw[:, 0:P * B].rearrange("p (k b) -> p k b", b=B)
        xa4 = xa[:, :].rearrange("p (g w b) -> p g w b", g=G, b=B)
        xb4 = reg_d[:, :].rearrange("p (g w b) -> p g w b", g=G, b=B)

        at = [0]

        def sm(cols):
            at[0] += cols
            return small[:, at[0] - cols:at[0]]

        rstd_p, patch_part, patch_part2 = (reg_c[:, n * TOK:(n + 1) * TOK] for n in range(1, 4))
        wsum, wsq_sum, wrstd, pl_sum, pl_sq_sum, pl_rstd = (sm(B) for _ in range(6))
        pl = sm(KC * B)
        pl_sq = reg_f[:, 0:KC * B]
        pln = sm(KC * 2 * B)
        negmax, psum_exp, pinv = sm(NBLK), sm(NBLK), sm(NBLK)
        logit, lmax, wexp, wwt, omd, fct, line, ds, nds = (sm(2) for _ in range(9))
        eps_ln = sm(1)
        dst = sm(TOK // 4)
        d_eps, ln2 = sm(1), sm(1)
        wft = sm(KC * 2 * B)

        ld_patch, ld_prm, ld_win, ld_img = sem("ld_patch"), sem("ld_prm"), sem("ld_win"), sem("ld_img")
        ld_slot = [sem(f"ld_slot{r}") for r in range(NSLOT)]
        ld_band, ld_vm = sem("ld_band"), sem("ld_vm")
        pe = {n: sem("pe_" + n) for n in (
            "slot_used", "patch_mean", "patch_var", "win_mean", "pool", "win_var", "pl_mean", "pl_var", "qkv",
            "scores", "vt", "pt", "attn", "out", "ds", "conv", "fld1", "fld2", "edge", "chunk")}
        ve = {n: sem("ve_" + n) for n in (
            "order", "consts", "patch_part", "patch_centred", "fl", "win_sums", "win_centred", "win_sq_sums", "xw", "pl_sums",
            "pl_sq_sums", "pln", "negmax", "prob", "pf", "dsl", "stage", "conv", "bank_turn", "img",
            "clip1", "clip2", "slope", "outer", "cross", "kh", "cliph", "diff", "clipd", "u", "pad", "fin", "halo", "u_in")}
        ac = {n: sem("ac_" + n) for n in (
            "patch_sq", "patch_std", "fl", "win_sq", "win_std", "pl_std", "qkv", "vt", "exp", "pt", "rows",
            "wwk", "wv", "conv", "evac1", "sqr", "lnw", "psq", "w15", "lnd", "inv", "beta", "x3", "hi", "halo", "u_in")}
        po = {n: sem("po_" + n) for n in ("zero", "stat", "bandz", "pick", "vm", "padz", "lo", "cxy", "m", "absum", "hn", "nk")}
        ld_last, st_out = [sem(f"ld_last{n}") for n in range(NPIECE)], sem("st_out")

        block = ctx.enter_context(nc.Block())

        STATF = KC * B + B
        stat_v = [reg_e[:, 1024 + m * STATF:1024 + (m + 1) * STATF] for m in range(4)]

        CB = (RG + 2) * C
        bands = reg_c[:, 0:3 * NCONV * CB].rearrange("p (m n) -> p m n", n=CB)
        hmats = xw[:, 0:2 * NCONV * P].rearrange("p (m n) -> p m n", n=P)
        halo_of = {0: reg_e[:, :].rearrange("p (g n) -> p g n", g=G), 1: reg_f[:, :].rearrange("p (g n) -> p g n", g=G)}

        def halo_source(layer):
            return (xa4, halo_of[0]) if layer % 2 == 0 else (xb4, halo_of[1])

        def halo_waits(w, layer):
            if layer == 0:
                return [(ve["stage"], G * (w + 1)), (po["zero"], 4)]
            before = ve if layer % 2 == 0 else ac
            return [(before["conv"], pairs_done(w, layer - 1, 1))]

        la = [NVM + 2 * NCH * ROWF]

        def arena(cols):
            la[0] += cols
            return ring[:, la[0] - cols:la[0]]

        u = [reg_a[:, x * ROWF:(x + 1) * ROWF] for x in range(3)] + [reg_g[:, 0:ROWF]]
        u3 = lambda c: u[c].rearrange("p (w b) -> p w b", b=B)
        x3 = arena(NCH * ROW).rearrange("p (x n) -> p x n", x=NCH)
        edge_m = arena(P)
        dual = lambda cols: [arena(cols) for _ in range(2)]
        u_hi = [u_parts[:, c * ROWF:(c + 1) * ROWF] for c in range(NCH)]
        u_lo = [u_parts[:, (NCH + c) * ROWF:(NCH + c + 1) * ROWF] for c in range(NCH)]
        u_in = lambda c: u[c][:, B:(S + 1) * B]
        u_half = lambda c, half: u[c][:, B + half * HALF:B + (half + 1) * HALF]
        vm = ring[:, la[0]:la[0] + NVM]
        fld = dual(5 * NF)
        sqs = dual(3 * NF)
        cxy, mxy, slope = dual(NF), dual(NF), dual(NF)
        ab, abs_ = dual(2 * NF), dual(NF)
        num = dual(2 * NF)
        lnw = [arena(NF)] * 2
        den, inv = dual(2 * NF), dual(2 * NF)
        kh = num
        hb, dif = ([reg_b[:, n * NF:(n + 1) * NF] for n in ns] for ns in ((0, 1), (2, 3)))
        assert la[0] <= NSLOT * SLOTF

        def mat(name, first):
            n = MATS.index(name) + (0 if first else len(MATS))
            return vmr[:, n * P:(n + 1) * P]

        def slot_ready(eng, k):
            eng.wait_ge(ld_slot[k % NSLOT], 16 * (k // NSLOT + 1))

        k0 = len(PREFIX)
        k1 = k0 + NV - V_FIRST
        U_PREFIX = V_FIRST + 2
        U_V = U_PREFIX + NV - V_FIRST
        U_ALL = U_V + NO
        released, n_v = [], 0
        for kind in PREFIX:
            if kind in ("q", "k", "v"):
                released.append((pe["qkv"], 4 * (("q", "k", "v").index(kind) + 1)))
            elif kind == "o":
                released.append((pe["out"], 4))
            else:
                n_v += 1
                released.append((pe["slot_used"], n_v))

        @block.sync
        def _(sp):
            sp.dma_start(reg_a[:, :], x_patch).then_inc(ld_patch, 16)
            sp.dma_start(xw[:, 0:P * B], x_window).then_inc(ld_win, 16)
            vslot = 0
            for k, kind in enumerate(PREFIX + ["V"] * NSLOT):
                if k >= NSLOT:
                    sp.wait_ge(*released[k - NSLOT])
                if kind in ("q", "k"):
                    n0 = 0 if kind == "q" else PD
                    src = wqk_p.rearrange("(p k) n -> p k n", k=KC)[:, :, n0:n0 + PD]
                elif kind == "v":
                    src = wv_p.rearrange("(p k) n -> p k n", k=KC)
                elif kind == "o":
                    src = wout_p.rearrange("(h d) n -> d h n", d=DH)
                elif kind in ("wq", "wk"):
                    src = wqk_w[("wq", "wk").index(kind)].rearrange("p (k n) -> p k n", k=KC)
                else:
                    src = wv_w[vslot].rearrange("p (k n) -> p k n", k=KC)
                    vslot += 1
                sp.dma_start(slot[k % NSLOT], src).then_inc(ld_slot[k % NSLOT], 16)
            with sp.Fori(1, (NV - V_FIRST) // NSLOT) as i:
                for m in range(NSLOT):
                    sp.wait_ge(pe["slot_used"], i * NSLOT + (U_PREFIX + m - NSLOT + 1))
                    r = (k0 + m) % NSLOT
                    sp.dma_start(ring[:, r * SLOTF:(r + 1) * SLOTF], wv_w[i * NSLOT + (V_FIRST + m)]).then_inc(ld_slot[r], 16)
            with sp.Fori(0, NO // NSLOT - 1) as i:
                for m in range(NSLOT):
                    sp.wait_ge(pe["slot_used"], i * NSLOT + (U_V + m - NSLOT + 1))
                    r = (k1 + m) % NSLOT
                    sp.dma_start(ring[:, r * SLOTF:(r + 1) * SLOTF], wout_w[i * NSLOT + m]).then_inc(ld_slot[r], 16)
            for s_ in range(NO - NSLOT, NO - 1):
                sp.wait_ge(pe["slot_used"], U_V + s_ - NSLOT + 1)
                r = (k1 + s_) % NSLOT
                sp.dma_start(ring[:, r * SLOTF:(r + 1) * SLOTF], wout_w[s_]).then_inc(ld_slot[r], 16)
            sp.wait_ge(pe["slot_used"], U_ALL - NSLOT)
            r, piece = (k1 + NO - 1) % NSLOT, SLOTF // NPIECE
            for n in range(NPIECE):
                sp.dma_start(ring[:, r * SLOTF + n * piece:r * SLOTF + (n + 1) * piece],
                             wout_w[NO - 1, :, n * piece:(n + 1) * piece]).then_inc(ld_last[n], 16)
            sp.wait_ge(pe["slot_used"], U_ALL)
            sp.dma_start(vm, vmats).then_inc(ld_vm, 16)
            sp.dma_start(edge_m, edge).then_inc(ld_vm, 16)
            for x in range(NCH):
                sp.wait_ge(ve["fin"], x + 1)
                sp.dma_start(out[x * P:(x + 1) * P, :], x3[:, x, :]).then_inc(st_out, 16)
            sp.wait_ge(st_out, 16 * NCH)

        @block.tensor
        def _(te):
            def used(ins):
                ins.then_inc(pe["slot_used"], 1)

            def all_sum(dst, src, ready, value, signal):
                te.wait_ge(ready, value)
                te.matmul(dst, ones[:, :], src, start=True, stop=True).then_inc(pe[signal], 1)

            def project_t(k, first, between=None):
                slot_ready(te, k)
                for h in range(HEADS):
                    if h == HEADS // 2 and between:
                        between()
                    n = first + h // 2
                    if h % 2 == 0 and n >= 2:
                        te.wait_ge(ac["qkv"], n - 1)
                    for c in range(KC):
                        if first == 0 and h == 0:
                            te.wait_ge(ac["fl"], c + 1)
                        ins = te.matmul(bank[:, 4 + n % 2, (h % 2) * TOK:(h % 2 + 1) * TOK],
                                        slot[k % NSLOT][:, c, h * DH:(h + 1) * DH], fl[:, c, :],
                                        start=(c == 0), stop=(c == KC - 1))
                    if h % 2 == 1:
                        ins.then_inc(pe["qkv"], 1)

            def thin(k, lhs, b_, n0, start, stop, pieces=False):
                for c in range(KC):
                    if pieces and c % (KC // NPIECE) == 0:
                        te.wait_ge(ld_last[c // (KC // NPIECE)], 16)
                    for j in range(4):
                        ins = te.matmul(bank[32 * j:32 * j + 32, b_, n0:n0 + 256], lhs(c),
                                        slot[k % NSLOT][:, c, 256 * j:256 * j + 256],
                                        start=start and c == 0, stop=stop and c == KC - 1, skip_group_check=True)
                return ins

            def v_slot(s):
                k = PREFIX.index(f"V{s}")
                slot_ready(te, k)
                used(thin(k, lambda c: xw[:, (s * KC + c) * B:(s * KC + c) * B + 2 * B], 7, 0, s == 0, False))

            te.wait_ge(ve["consts"], 1)
            te.wait_ge(ld_prm, 16)
            all_sum(bank[:, 0, 0:TOK], patch_part, ve["patch_part"], 1, "patch_mean")
            all_sum(bank[:, 2, 0:B], wsum, ve["win_sums"], 1, "win_mean")
            te.wait_ge(ve["win_sums"], 2)
            te.matmul(bank[:, 3, :], par("pool"), reg_g[:, 0:512], start=True, stop=True).then_inc(pe["pool"], 1)
            all_sum(bank[:, 1, 0:TOK], patch_part2, ve["patch_part"], 2, "patch_var")

            def window_sums():
                te.wait_ge(ve["patch_centred"], 1)
                all_sum(bank[:, 0, 0:B], wsq_sum, ve["win_sq_sums"], 1, "win_var")
                all_sum(bank[:, 1, 0:B], pl_sum, ve["pl_sums"], 1, "pl_mean")

            project_t(PREFIX.index("q"), 0, window_sums)
            te.wait_ge(ve["xw"], 1)
            v_slot(0)
            v_slot(1)
            all_sum(bank[:, 2, 0:B], pl_sq_sum, ve["pl_sq_sums"], 1, "pl_var")
            project_t(PREFIX.index("k"), 4)
            for n in range(2, 5):
                v_slot(n)
            kv = PREFIX.index("v")
            slot_ready(te, kv)
            for n in range(4):
                t, half = n // 2, n % 2
                te.wait_ge(ac["qkv"], 8 + n - 1)
                for c in range(KC):
                    ins = te.matmul(bank[:, 4 + n % 2, :], fl[:, c, t * P:(t + 1) * P],
                                    slot[kv % NSLOT][:, c, half * 512:(half + 1) * 512], start=(c == 0), stop=(c == KC - 1))
                ins.then_inc(pe["qkv"], 1)
            te.wait_ge(ac["pl_std"], 1)
            te.wait_ge(ve["pln"], 1)
            te.wait_ge(ac["qkv"], 8)
            for i in range(NBLK):
                t, h = i // HEADS, i % HEADS
                ins = te.matmul(bank[:, i // 4, (i % 4) * P:(i % 4 + 1) * P], q_t[:, h, t * P:(t + 1) * P],
                                k_t[:, h, t * P:(t + 1) * P], start=True, stop=True, skip_group_check=True)
                if i % 4 == 3:
                    ins.then_inc(pe["scores"], 1)
            te.wait_ge(ac["qkv"], 12)
            for i in range(NBLK):
                t, h = i // HEADS, i % HEADS
                if i % 4 == 0 and i >= 8:
                    te.wait_ge(ac["vt"], i // 4 - 1)
                ins = te.transpose(bank[:, 4 + i // 4 % 2, (i % 4) * P:(i % 4 + 1) * P],
                                   v_tok[:, t, h * DH:(h + 1) * DH], ident)
                if i % 4 == 3:
                    ins.then_inc(pe["vt"], 1)
            v_slot(5)
            v_slot(6)
            te.wait_ge(ve["prob"], 1)
            te.wait_ge(ac["vt"], 4)
            for i in range(NBLK):
                if i % 4 == 0 and i >= 8:
                    te.wait_ge(ac["pt"], i // 4 - 1)
                ins = te.transpose(bank[:, 4 + i // 4 % 2, (i % 4) * P:(i % 4 + 1) * P], prob[:, i, :], ident)
                if i % 4 == 3:
                    ins.then_inc(pe["pt"], 1)
            v_slot(7)
            for i in range(NBLK):
                t, h = i // HEADS, i % HEADS
                if i % 4 == 0:
                    te.wait_ge(ac["pt"], i // 4 + 1)
                ins = te.matmul(bank[:, i // 4, (i % 4) * P:(i % 4 + 1) * P], v_tok[:, t, h * DH:(h + 1) * DH],
                                prob_t[:, i, :], start=True, stop=True, skip_group_check=True)
                if i % 4 == 3:
                    ins.then_inc(pe["attn"], 1)
            for k, n0 in ((PREFIX.index("wq"), 0), (PREFIX.index("wk"), 256)):
                slot_ready(te, k)
                used(thin(k, lambda c: pln[:, c * 2 * B:(c + 1) * 2 * B], 6, n0, True, True))
            ko = PREFIX.index("o")
            slot_ready(te, ko)
            te.wait_ge(ve["pf"], 4)
            for n in range(4):
                t, half = n // 2, n % 2
                if n >= 2:
                    te.wait_ge(ac["rows"], n - 1)
                for c in range(HEADS):
                    ins = te.matmul(bank[:, 4 + n % 2, :], pf_t[:, t * HEADS + c, :],
                                    slot[ko % NSLOT][:, c, half * 512:(half + 1) * 512], start=(c == 0), stop=(c == HEADS - 1))
                ins.then_inc(pe["out"], 1)
            te.wait_ge(ve["dsl"], 2)
            te.matmul(bank[:, 3, 0:64], reg_b[:, 0:P], ident.rearrange("p (g b) -> p g b", g=G)[:, :, 0:B],
                      start=True, stop=True).then_inc(pe["ds"], 1)
            with te.Fori(0, (NV - V_FIRST) // NSLOT) as i:
                for m in range(NSLOT):
                    te.wait_ge(ld_slot[(k0 + m) % NSLOT], i * 16 + 16 * ((k0 + m) // NSLOT + 1))
                    te.wait_ge(po["stat"], i * NSLOT + (m + 1))
                    used(thin(k0 + m, lambda c: stat_v[m][:, c * B:(c + 2) * B], 7, 0, False, False))

            def conv(w, layer):
                a_, b_ = columns(w, layer)
                src, halo = halo_source(layer)
                out_ = lambda g: bank[:, g, 0:(b_ - a_) * B]
                for g in range(G):
                    if layer % 2:
                        te.wait_ge(ac["conv"], pairs_done(w, layer - 1, g // 2))
                    elif layer:
                        te.wait_ge(ve["conv"], pairs_done(w, layer - 1, g // 2))
                    elif w:
                        te.wait_ge(ve["conv"], pairs_done(w - 1, NCONV - 1, g // 2))
                    for dw in range(3):
                        te.matmul(out_(g), bands[:, layer * 3 + dw, C:C + P],
                                  src[:, g, a_ + dw:b_ + dw, :], start=(dw == 0), stop=False)
                te.wait_ge(ac["halo"], 2 * (w * NCONV + layer + 1))
                te.wait_ge(ve["halo"], 4 * (w * NCONV + layer + 1))
                for g in range(G):
                    te.matmul(out_(g), hmats[0:6 * C, layer + (NCONV if g == G - 1 else 0), :], halo[0:6 * C, g, a_ * B:b_ * B],
                              start=False, stop=True).then_inc(pe["conv"], 1)

            def chunk_rows(x, g, half):
                w0 = half * S // 2
                return te.matmul(bank[QUAD * g:QUAD * (g + 1), 4 + x, (1 - half) * HALF:(2 - half) * HALF],
                                 pick[:, x * QUAD:(x + 1) * QUAD],
                                 xa4[:, g, 1 + w0:1 + w0 + S // 2, :], start=True, stop=True, skip_group_check=True)

            for s_ in range(NO):
                i, m = s_ // NSLOT, s_ % NSLOT
                if s_ < NO - 1:
                    te.wait_ge(ld_slot[(k1 + m) % NSLOT], 16 * i + 16 * ((k1 + m) // NSLOT + 1))
                te.wait_ge(ve["bank_turn"], s_ + 1)
                used(thin(k1 + m, lambda c: wft[:, c * 2 * B:(c + 1) * 2 * B], 4 + m, 0, True, True, s_ == NO - 1))
                if s_ == NO - 1:
                    te.wait_ge(po["pick"], 1)
                    te.wait_ge(ve["conv"], pairs_done(WAVES - 2, NCONV - 1, 1))
                    for x in range(NCH):
                        te.wait_ge(ve["bank_turn"], NO + x + 1)
                        for g in range(G):
                            ins = chunk_rows(x, g, 0)
                        ins.then_inc(pe["chunk"], 1)
                for w, layer in convs_after(s_):
                    if layer == 0:
                        te.wait_ge(ve["stage"], G * (w + 1))
                    if (w, layer) == (0, 0):
                        te.wait_ge(ld_band, 16 * (RG + 9))
                    conv(w, layer)

            te.wait_ge(ac["u_in"], NCH)
            for h in range(2):
                te.wait_ge(ve["conv"], pairs_done(WAVES - 1, NCONV - 1, h))
                for x in range(NCH):
                    for g in (2 * h, 2 * h + 1):
                        ins = chunk_rows(x, g, 1)
                    if h:
                        ins.then_inc(pe["chunk"], 1)

            def stencil(dst, c, first, terms):
                for part in (u_hi[c], u_lo[c]):
                    p3 = part.rearrange("p (w b) -> p w b", b=B)
                    for n, (off, m) in enumerate(terms):
                        last = te.matmul(dst[:, 0:NF], mat(m, first), p3[:, 2 + off:S + off, :],
                                         start=(part is u_hi[c] and n == 0),
                                         stop=(part is u_lo[c] and n == len(terms) - 1))
                return last

            def fields(k, c, first, wait):
                b1 = 5 * (c % 2)
                if first and c == 0:
                    te.wait_ge(ac["u_in"], NCH + 2)
                    te.wait_ge(ve["u_in"], 2)
                te.wait_ge(po["lo"], k + 1)
                if wait:
                    te.wait_ge(ac["evac1"], k - 1)
                stencil(bank[:, b1, :], c, first, UX)
                stencil(bank[:, b1 + 1, :], c, first, UY)
                stencil(bank[:, b1 + 2, :], c, first, UXY).then_inc(pe["fld1"], 1)
                if wait or c:
                    te.wait_ge(ve["clip2"], k)
                stencil(bank[:, 3, :], c, first, UYY)
                stencil(bank[:, 4, :], c, first, UXX).then_inc(pe["fld2"], 1)

            te.wait_ge(po["vm"], 1)
            te.wait_ge(ld_vm, 32)
            for k in range(4):
                fields(k, k, True, k >= 2)
            with te.Fori(1, STEPS) as i:
                for c in range(NCH):
                    fields(i * NCH + c, c, False, True)
            te.wait_ge(ac["evac1"], SLOTS - 1)
            for x in range(NCH):
                if x == 3:
                    te.wait_ge(ve["clip2"], SLOTS)
                te.wait_ge(ve["pad"], SLOTS - NCH + x + 1)
                te.matmul(bank[:, x, :], edge_m, u_in(x), start=True, stop=True).then_inc(pe["edge"], 1)

        @block.vector
        def _(v):
            n_order = [0]

            def then(ins):
                n_order[0] += 1
                ins.then_inc(ve["order"], 1)
                v.wait_ge(ve["order"], n_order[0])

            def kb(row, k):
                return row.unsqueeze(1).to_broadcast([P, k, row.shape[1]])

            then(v.memset(ones[:, :], 1.0))
            then(v.memset(eps_ln, LN_EPS))
            then(v.memset(d_eps, D_EPS))
            then(v.memset(ln2, 0.6931471805599453))
            then(v.memset(xw[:, P * B:], 0.0))
            v.memset(pln, 0.0).then_inc(ve["consts"], 1)
            v.wait_ge(ve["consts"], 1)
            v.wait_ge(ld_patch, 16)
            v.tensor_reduce(patch_part, fl.rearrange("p k t -> p t k"), AX.X, ALU.add).then_inc(ve["patch_part"], 1)
            v.wait_ge(ld_win, 16)
            v.tensor_reduce(wsum, xwk.rearrange("p k b -> p b k"), AX.X, ALU.add).then_inc(ve["win_sums"], 1)
            v.wait_ge(pe["patch_mean"], 1)
            mean = reg_c[:, 0:TOK]
            then(v.tensor_scalar(mean, bank[:, 0, 0:TOK], 1.0 / PD, None, ALU.mult))
            v.tensor_tensor(fl, fl, kb(mean, KC), ALU.subtract).then_inc(ve["patch_centred"], 1)
            for w2 in range(2):
                ins = v.tensor_reduce(reg_g[:, w2 * 256:(w2 + 1) * 256],
                                      xw[:, w2 * 1024:(w2 + 1) * 1024].rearrange("p (w n) -> p n w", w=4), AX.X, ALU.add)
                if w2 == 0:
                    then(ins)
            ins.then_inc(ve["win_sums"], 1)
            v.wait_ge(ac["patch_sq"], 1)
            v.tensor_reduce(patch_part2, sq.rearrange("p k t -> p t k"), AX.X, ALU.add).then_inc(ve["patch_part"], 1)
            v.wait_ge(ac["patch_std"], 1)
            v.wait_ge(ld_prm, 16)
            v.wait_ge(ve["patch_centred"], 1)
            then(v.reciprocal(rstd_p, rstd_p))
            for c in range(KC):
                v.scalar_tensor_tensor(fl[:, c, :], fl[:, c, :], par("pn_g")[:, c:c + 1], rstd_p,
                                       ALU.mult, ALU.mult).then_inc(ve["fl"], 1)
            v.wait_ge(pe["win_mean"], 1)
            v.wait_ge(ve["win_sums"], 2)
            then(v.tensor_scalar(wsum, bank[:, 2, 0:B], 1.0 / WD, None, ALU.mult))
            v.wait_ge(pe["pool"], 1)
            v.tensor_tensor(xwk, xwk, kb(wsum, P), ALU.subtract).then_inc(ve["win_centred"], 1)
            for q in range(4):
                then(v.tensor_copy(pl[32 * q:32 * q + 32, :], bank[32 * q:32 * q + 32, 3, q * P:(q + 1) * P]))
            pl3 = pl.rearrange("p (k b) -> p k b", b=B)
            plq3 = pl_sq.rearrange("p (k b) -> p k b", b=B)
            v.tensor_reduce(pl_sum, pl3.rearrange("p k b -> p b k"), AX.X, ALU.add).then_inc(ve["pl_sums"], 1)
            v.wait_ge(ac["win_sq"], 1)
            v.tensor_reduce(wsq_sum, wsq.rearrange("p k b -> p b k"), AX.X, ALU.add).then_inc(ve["win_sq_sums"], 1)
            v.wait_ge(pe["pl_mean"], 1)
            then(v.tensor_scalar(pl_sum, bank[:, 1, 0:B], 1.0 / PD, None, ALU.mult))
            then(v.tensor_tensor(pl3, pl3, kb(pl_sum, KC), ALU.subtract))
            then(v.tensor_tensor(pl_sq, pl, pl, ALU.mult))
            v.tensor_reduce(pl_sq_sum, plq3.rearrange("p k b -> p b k"), AX.X, ALU.add).then_inc(ve["pl_sq_sums"], 1)
            v.wait_ge(ac["win_std"], 1)
            v.wait_ge(ve["win_centred"], 1)
            then(v.reciprocal(wrstd, wrstd))
            then(v.tensor_tensor(xwk, xwk, kb(wrstd, P), ALU.mult))
            then(v.tensor_tensor(xwk, xwk, par("wn_g").unsqueeze(2).to_broadcast([P, P, B]), ALU.mult))
            v.tensor_tensor(xwk, xwk, par("wn_b").unsqueeze(2).to_broadcast([P, P, B]), ALU.add).then_inc(ve["xw"], 1)
            v.wait_ge(ac["pl_std"], 1)
            then(v.reciprocal(pl_rstd, pl_rstd))
            then(v.tensor_tensor(pl3, pl3, kb(pl_rstd, KC), ALU.mult))
            then(v.tensor_tensor(pl3, pl3, par("pln_g").unsqueeze(2).to_broadcast([P, KC, B]), ALU.mult))
            v.tensor_tensor(pln.rearrange("p (k b) -> p k b", b=2 * B)[:, :, 0:B], pl3,
                            par("pln_b").unsqueeze(2).to_broadcast([P, KC, B]), ALU.add).then_inc(ve["pln"], 1)
            for n in range(4):
                v.wait_ge(pe["scores"], n + 1)
                if n == 0:
                    v.wait_ge(ac["qkv"], 12)
                then(v.scalar_tensor_tensor(prob[:, 4 * n:4 * n + 4, :],
                                            bank[:, n, :].rearrange("p (i k) -> p i k", k=P), DH ** -0.5,
                                            kb(par("mask"), 4), ALU.mult, ALU.add))
            v.tensor_reduce(negmax, prob, AX.X, ALU.max, negate=True).then_inc(ve["negmax"], 1)
            v.wait_ge(ac["vt"], 4)
            then(v.tensor_scalar(reg_g[:, :], reg_f[:, :], par("cp_w")[:, 4:5], par("cp_b"), ALU.mult, ALU.add))

            def tap(kh_, kw_):
                w = par("cp_w")[:, kh_ * 3 + kw_:kh_ * 3 + kw_ + 1]
                dg, dj = kh_ - 1, kw_ - 1
                g0, g1 = max(0, -dg), G - max(0, dg)
                if dj == 0:
                    o = reg_g[:, :].rearrange("p (n r) -> p n r", r=G * BL)[:, :, g0 * BL:g1 * BL]
                    i_ = reg_f[:, :].rearrange("p (n r) -> p n r", r=G * BL)[:, :, (g0 + dg) * BL:(g1 + dg) * BL]
                    then(v.scalar_tensor_tensor(o, i_, w, o, ALU.mult, ALU.add))
                    return
                j0, j1 = max(0, -dj), PPW - max(0, dj)
                if dg == 0:
                    o, i_ = pf_t[:, :, j0 * 32:j1 * 32], v_t[:, :, (j0 + dj) * 32:(j1 + dj) * 32]
                    then(v.scalar_tensor_tensor(o, i_, w, o, ALU.mult, ALU.add))
                    return
                for j in range(j0, j1):
                    o = pf_t[:, :, j * 32 + g0 * BL:j * 32 + g1 * BL]
                    i_ = v_t[:, :, (j + dj) * 32 + (g0 + dg) * BL:(j + dj) * 32 + (g1 + dg) * BL]
                    ins = v.scalar_tensor_tensor(o, i_, w, o, ALU.mult, ALU.add)
                    if j < j1 - 1:
                        continue
                    then(ins)

            for kh_ in range(3):
                for kw_ in range(3):
                    if (kh_, kw_) != (1, 1):
                        tap(kh_, kw_)
                if kh_ == 0:
                    v.wait_ge(ac["exp"], NBLK)
                    then(v.reciprocal(pinv, psum_exp))
                    v.tensor_tensor(prob, prob, pinv.unsqueeze(2).to_broadcast([P, NBLK, P]),
                                    ALU.mult).then_inc(ve["prob"], 1)
            for n in range(4):
                v.wait_ge(pe["attn"], n + 1)
                v.tensor_tensor(pf_t[:, 4 * n:4 * n + 4, :], pf_t[:, 4 * n:4 * n + 4, :],
                                bank[:, n, :].rearrange("p (i k) -> p i k", k=P), ALU.add).then_inc(ve["pf"], 1)
            v.wait_ge(pe["slot_used"], U_PREFIX)
            v.wait_ge(ac["wwk"], 1)
            qk = reg_b[:, 256:512]
            then(v.tensor_tensor(qk, bank[:, 6, 0:256], reg_b[:, 0:256], ALU.mult))
            then(v.tensor_reduce(logit, qk.rearrange("p (h d) -> p h d", h=2), AX.X, ALU.add))
            then(v.tensor_scalar(logit, logit, DH ** -0.5, None, ALU.mult))
            then(v.tensor_reduce(lmax, logit.unsqueeze(2), AX.X, ALU.max))
            v.tensor_tensor(logit, logit, lmax, ALU.subtract).then_inc(ve["dsl"], 1)
            v.wait_ge(ac["wwk"], 2)
            then(v.tensor_reduce(lmax, wexp.unsqueeze(2), AX.X, ALU.add))
            then(v.reciprocal(lmax, lmax))
            then(v.tensor_tensor(wwt, wexp, lmax, ALU.mult))
            then(v.tensor_scalar(line, wwt, 0.5, None, ALU.is_lt))
            then(v.tensor_scalar(ds, wwt, 0.5, None, ALU.max))
            then(v.tensor_tensor(nds, wwt, wwt, ALU.subtract))
            then(v.tensor_scalar(omd, wwt, -1.0, 1.0, ALU.mult, ALU.add))
            then(v.tensor_scalar(omd, omd, 0.5, None, ALU.max))
            then(v.reciprocal(fct, omd))
            then(v.tensor_scalar(fct, fct, 0.5, -1.0, ALU.mult, ALU.add))
            then(v.tensor_tensor(fct, fct, line, ALU.mult))
            then(v.scalar_tensor_tensor(nds, fct, 1.0, nds, ALU.add, ALU.mult))
            then(v.tensor_scalar(reg_b[:, 0:64], ones[:, 0:64], ds[:, 0:1], None, ALU.mult))
            v.tensor_scalar(reg_b[:, 64:128], ones[:, 0:64], ds[:, 1:2], None, ALU.mult).then_inc(ve["dsl"], 1)
            v.wait_ge(pe["ds"], 1)
            for t in range(TT):
                then(v.tensor_copy(dst[:, t * 32:(t + 1) * 32].rearrange("p (g b) -> p g b", b=BL),
                                   bank[:, 3, 0:64].rearrange("p (g b) -> p g b", b=B)[:, :, t * BL:(t + 1) * BL]))
            v.wait_ge(ac["rows"], 4)
            v.wait_ge(ld_img, 16)
            v.wait_ge(po["zero"], 1)
            for t in range(TT):
                tr = reg_b[:, 1024 * (1 - t):1024 * (2 - t)].rearrange("p (w n) -> p w n", n=32)
                then(v.transpose(tr, rows[:, t, :].rearrange("p (r w c) -> p w r c", r=2, w=S)))
                then(v.tensor_tensor(tr, tr, kb(dst[:, t * 32:(t + 1) * 32], S), ALU.mult))
                xv = xa4[:, :, 1:S + 1, t * BL:(t + 1) * BL].rearrange("p g w b -> p w g b")
                v.tensor_tensor(xv, xv, tr.rearrange("p w (g b) -> p w g b", b=BL), ALU.add).then_inc(ve["img"], 1)
            v.wait_ge(ac["wv"], 1)
            wv_s, w0, t1, t2 = (reg_b[:, 256 * n:256 * n + 256] for n in range(4))
            for h in range(2):
                then(v.tensor_scalar(w0[:, h * P:(h + 1) * P], wv_s[:, h * P:(h + 1) * P], nds[:, h:h + 1], None, ALU.mult))
            then(v.transpose(t1, wv_s))
            then(v.transpose(t2, w0))
            r3 = lambda a: a.rearrange("p (k b) -> p k b", b=2 * B)
            cb = lambda n: par(n).unsqueeze(2).to_broadcast([P, KC, 2 * B])
            then(v.tensor_tensor(r3(t1), r3(t1), cb("cw_w"), ALU.mult))
            then(v.tensor_tensor(r3(t1), r3(t1), cb("cw_b"), ALU.add))
            v.wait_ge(ve["img"], TT)
            v.tensor_tensor(wft, t1, t2, ALU.add).then_inc(ve["bank_turn"], NSLOT)

            def conv(w, layer):
                a_, b_ = columns(w, layer)
                for h in range(2):
                    v.wait_ge(pe["conv"], (w * NCONV + layer) * G + 2 * h + 2)
                    xv = xa4[:, 2 * h:2 * h + 2, 1 + a_:1 + b_, :]
                    v.scalar_tensor_tensor(
                        xv, bank[:, 2 * h:2 * h + 2, 0:(b_ - a_) * B].rearrange("p g (w b) -> p g w b", b=B),
                        par("conv_b")[:, layer:layer + 1], xv, ALU.add, ALU.add).then_inc(ve["conv"], 1)

            for s_ in range(NO):
                i, m = s_ // NSLOT, s_ % NSLOT
                v.wait_ge(pe["slot_used"], U_V + s_ + 1)
                tr = reg_b[:, 1024 + 256 * m:1024 + 256 * (m + 1)]
                v.transpose(tr, bank[:, 4 + m, 0:256]).then_inc(ve["bank_turn"], 1)
                v.wait_ge(ve["bank_turn"], s_ + NSLOT + 1)
                xv = xa4[:, m, 1 + WB * i:1 + WB * (i + 1), :]
                v.tensor_tensor(xv, xv, tr.rearrange("p (w b) -> p w b", b=2 * B)[:, :, 0:B],
                                ALU.add).then_inc(ve["stage"], 1)
                for w, layer in convs_after(s_):
                    halo_rows(v, v.tensor_copy, (1, 2), w, layer, halo_source(layer), halo_waits(w, layer), ve["halo"])
                    if layer % 2:
                        conv(w, layer)

            def f(par_, n, m=1):
                return fld[par_][:, n * NF:(n + m) * NF]

            def slot_step(k, q, c, new, old, end, first=False):
                n = 1 - q
                if new:
                    v.wait_ge(ac["evac1"], k)
                    v.tensor_scalar(f(n, 0, 3), f(n, 0, 3), 10.0, -10.0, ALU.min, ALU.max).then_inc(ve["clip1"], 1)
                if end:
                    v.wait_ge(ac["beta"], k - 2)
                    v.scalar_tensor_tensor(dif[n], kh[n][:, 0:NF], par("alpha"), hb[n],
                                           ALU.mult, ALU.add).then_inc(ve["diff"], 1)
                if new:
                    v.wait_ge(pe["fld2"], k)
                    v.tensor_scalar(f(n, 3, 2).rearrange("p (x n) -> p x n", x=2), bank[:, 3:5, 0:NF], 10.0, -10.0,
                                    ALU.min, ALU.max).then_inc(ve["clip2"], 1)
                if end:
                    v.wait_ge(ve["diff"], k - 2)
                    v.tensor_scalar(dif[n], dif[n], 1.0, -1.0, ALU.min, ALU.max).then_inc(ve["clipd"], 1)
                if new:
                    v.wait_ge(ac["sqr"], k)
                    v.scalar_tensor_tensor(slope[n], sqs[n][:, 0:NF], 1.0, sqs[n][:, NF:2 * NF],
                                           ALU.add, ALU.add).then_inc(ve["slope"], 1)
                if end:
                    v.wait_ge(ve["clipd"], k - 2)
                    if first:
                        v.wait_ge(ac["x3"], k - 2)
                    inner = u[c][:, 2 * B:S * B]
                    v.scalar_tensor_tensor(inner, dif[n], DT, inner,
                                           ALU.mult, ALU.add).then_inc(ve["u"], 1)
                if old:
                    v.wait_ge(po["nk"], k - 1)
                    v.wait_ge(po["hn"], k - 1)
                    v.wait_ge(ac["inv"], k - 1)
                    v.tensor_tensor(kh[q], num[q], inv[q], ALU.mult).then_inc(ve["kh"], 1)
                if end:
                    v.wait_ge(ve["u"], k - 2)
                    v.tensor_copy(u3(c)[:, 1:S + 1:S - 1, :], u3(c)[:, 2:S:S - 3, :]).then_inc(ve["pad"], 1)
                if new:
                    v.wait_ge(ve["clip2"], k)
                    v.scalar_tensor_tensor(ab[n], sqs[n][:, 0:2 * NF], 1.0, f(n, 3, 2),
                                           ALU.add, ALU.mult).then_inc(ve["outer"], 1)
                if old:
                    v.wait_ge(ve["kh"], k - 1)
                    v.tensor_scalar(kh[q], kh[q], 5.0, -5.0, ALU.min, ALU.max).then_inc(ve["cliph"], 1)
                if new:
                    v.wait_ge(po["cxy"], k)
                    v.scalar_tensor_tensor(cxy[n], cxy[n], -2.0, f(n, 2), ALU.mult, ALU.mult).then_inc(ve["cross"], 1)

            for n in ("alpha", "beta"):
                then(v.scalar_tensor_tensor(par(n), par(n), -1.0, par(n), ALU.mult, ALU.max))
            for x in range(1, NCH, 2):
                v.wait_ge(pe["chunk"], NCH + x + 1)
                v.tensor_copy(u_half(x, 1), bank[:, 4 + x, 0:HALF]).then_inc(ve["u_in"], 1)
            finished = ((0,), (1,), (2, 3))
            for k in range(1, LOOP_FROM):
                slot_step(k, k % 2, (k - 3) % NCH, True, k > 1, k > 2, True)
            with v.Fori(1, LOOPS + 1) as i:
                for m in range(NCH):
                    slot_step(i * NCH + (m + 3), (m + 3) % 2, m, True, True, True)
            for k in range(LOOP_END, SLOTS + 3):
                slot_step(k, k % 2, (k - 3) % NCH, k <= SLOTS, k <= SLOTS + 1, True)
                for x in finished[k - SLOTS] if k >= SLOTS else ():
                    v.wait_ge(pe["edge"], x + 1)
                    v.wait_ge(ac["x3"], x + 1)
                    v.scalar_tensor_tensor(x3[:, x, :], bank[:, x, :], 0.7, x3[:, x, :],
                                           ALU.mult, ALU.add).then_inc(ve["fin"], 1)

        @block.scalar
        def _(a):
            a.dma_start(prm[:, :], params).then_inc(ld_prm, 16)
            nc.scalar.preload_act_table_set("sqrt_and_others")
            a.wait_ge(ve["consts"], 1)
            a.wait_ge(ve["patch_centred"], 1)
            a.activation(reg_b[:, :], reg_a[:, :], ACT.Square).then_inc(ac["patch_sq"], 1)
            a.wait_ge(pe["patch_var"], 1)
            a.activation(rstd_p, bank[:, 1, 0:TOK], ACT.Sqrt, bias=eps_ln, scale=1.0 / PD).then_inc(ac["patch_std"], 1)
            a.wait_ge(ld_prm, 16)
            for c in range(KC):
                a.wait_ge(ve["fl"], c + 1)
                a.activation(fl[:, c, :], fl[:, c, :], ACT.Identity, bias=par("pn_b")[:, c:c + 1]).then_inc(ac["fl"], 1)
            a.wait_ge(ve["win_centred"], 1)
            a.activation(reg_g[:, :], xw[:, 0:P * B], ACT.Square).then_inc(ac["win_sq"], 1)
            for n in range(4):
                if n == 2:
                    a.wait_ge(pe["win_var"], 1)
                    a.activation(wrstd, bank[:, 0, 0:B], ACT.Sqrt, bias=eps_ln, scale=1.0 / WD).then_inc(ac["win_std"], 1)
                a.wait_ge(pe["qkv"], n + 1)
                a.activation(reg_c[:, n * 512:(n + 1) * 512], bank[:, 4 + n % 2, :], ACT.Copy).then_inc(ac["qkv"], 1)
            a.wait_ge(po["zero"], 1)
            a.dma_start(xa4[:, :, 1:S + 1, :], x_conv.rearrange("p (g w b) -> p g w b", g=G, b=B)).then_inc(ld_img, 16)
            for n in range(4):
                a.wait_ge(pe["qkv"], 4 + n + 1)
                a.activation(reg_d[:, n * 512:(n + 1) * 512], bank[:, 4 + n % 2, :], ACT.Copy).then_inc(ac["qkv"], 1)
            a.wait_ge(pe["pl_var"], 1)
            a.activation(pl_rstd, bank[:, 2, 0:B], ACT.Sqrt, bias=eps_ln, scale=1.0 / PD).then_inc(ac["pl_std"], 1)
            for n in range(4):
                a.wait_ge(pe["qkv"], 8 + n + 1)
                a.activation(reg_e[:, n * 512:(n + 1) * 512], bank[:, 4 + n % 2, :], ACT.Copy).then_inc(ac["qkv"], 1)
            for n in range(4):
                a.wait_ge(pe["vt"], n + 1)
                a.activation(reg_f[:, n * 512:(n + 1) * 512], bank[:, 4 + n % 2, :], ACT.Copy).then_inc(ac["vt"], 1)
            a.wait_ge(ve["negmax"], 1)
            for i in range(NBLK):
                a.activation(prob[:, i, :], prob[:, i, :], ACT.Exp, bias=negmax[:, i:i + 1],
                             accum_out=psum_exp[:, i:i + 1]).then_inc(ac["exp"], 1)
            for n in range(4):
                a.wait_ge(pe["pt"], n + 1)
                a.activation(reg_b[:, n * 512:(n + 1) * 512], bank[:, 4 + n % 2, :], ACT.Copy).then_inc(ac["pt"], 1)
            a.wait_ge(pe["slot_used"], U_PREFIX)
            a.activation(reg_b[:, 0:256], bank[:, 6, 256:512], ACT.Copy).then_inc(ac["wwk"], 1)
            a.wait_ge(ve["dsl"], 1)
            a.activation(wexp, logit, ACT.Exp).then_inc(ac["wwk"], 1)
            for n in range(4):
                a.wait_ge(pe["out"], n + 1)
                a.activation(reg_c[:, n * 512:(n + 1) * 512], bank[:, 4 + n % 2, :], ACT.Copy).then_inc(ac["rows"], 1)
            a.wait_ge(pe["slot_used"], U_V)
            a.wait_ge(ve["img"], TT)
            a.activation(reg_b[:, 0:256], bank[:, 7, 0:256], ACT.Copy).then_inc(ac["wv"], 1)
            nc.scalar.preload_act_table_set("natural_log_exp_and_others")
            for w, layer in [c for s_ in range(NO) for c in convs_after(s_)]:
                a_, b_ = columns(w, layer)
                halo_rows(a, lambda o, i: a.activation(o, i, ACT.Copy), (0,), w, layer, halo_source(layer),
                          halo_waits(w, layer), ac["halo"])
                if (w, layer) == (WAVES - 1, 0):
                    a.wait_ge(po["padz"], 2)
                    for x in range(NCH):
                        a.wait_ge(pe["chunk"], x + 1)
                        a.activation(u_half(x, 0), bank[:, 4 + x, HALF:2 * HALF], ACT.Copy).then_inc(ac["u_in"], 1)
                if layer % 2:
                    continue
                for h in range(2):
                    a.wait_ge(pe["conv"], (w * NCONV + layer) * G + 2 * h + 2)
                    a.activation(xb4[:, 2 * h:2 * h + 2, 1 + a_:1 + b_, :],
                                 bank[:, 2 * h:2 * h + 2, 0:(b_ - a_) * B].rearrange("p g (w b) -> p g w b", b=B),
                                 ACT.Relu, bias=par("conv_b")[:, layer:layer + 1]).then_inc(ac["conv"], 1)

            def u_there(c):
                a.wait_ge(ac["u_in"], NCH + c // 2 + 1)
                if c % 2:
                    a.wait_ge(ve["u_in"], c // 2 + 1)

            def high(k, c, later):
                if not later:
                    u_there(c)
                    a.activation(u_hi[c], u[c], ACT.Copy).then_inc(ac["hi"], 1)
                    return
                a.wait_ge(ve["pad"], k - (NCH - 1))
                a.wait_ge(pe["fld2"], k - (NCH - 1))
                a.activation(u_hi[c][:, B:(S + 1) * B], u_in(c), ACT.Copy).then_inc(ac["hi"], 1)

            def evac1(k, n):
                a.wait_ge(pe["fld1"], k)
                a.activation(fld[n][:, 0:3 * NF].rearrange("p (x n) -> p x n", x=3), bank[:, 5 * n:5 * n + 3, 0:NF],
                             ACT.Copy).then_inc(ac["evac1"], 1)

            def slot_step(k, q, new, old, c, ahead):
                n = 1 - q
                if old:
                    a.wait_ge(ac["psq"], k - 1)
                    a.wait_ge(ac["w15"], k - 1)
                    a.activation(den[q], den[q], ACT.Ln, bias=d_eps).then_inc(ac["lnd"], 1)
                if new:
                    a.wait_ge(ve["clip1"], k)
                    a.activation(sqs[n], fld[n][:, 0:3 * NF], ACT.Square).then_inc(ac["sqr"], 1)
                if old:
                    a.wait_ge(ac["lnd"], k - 1)
                    a.activation(inv[q], den[q], ACT.Exp, scale=-1.0).then_inc(ac["inv"], 1)
                if new:
                    a.wait_ge(ve["slope"], k)
                    a.activation(lnw[n], slope[n], ACT.Ln, bias=d_eps).then_inc(ac["lnw"], 1)
                    a.activation(den[n][:, 0:NF], slope[n], ACT.Square).then_inc(ac["psq"], 1)
                    a.wait_ge(ac["lnw"], k)
                    a.activation(den[n][:, NF:2 * NF], lnw[n], ACT.Exp, bias=ln2, scale=1.5).then_inc(ac["w15"], 1)
                if c is not None:
                    high(k + 1, c, k + 1 >= NCH)
                if ahead:
                    evac1(k + 1, q)
                if old:
                    a.wait_ge(ve["cliph"], k - 1)
                    a.activation(hb[q], kh[q][:, NF:2 * NF], ACT.Copy, scale=par("beta")).then_inc(ac["beta"], 1)

            for x in (0, 2):
                a.wait_ge(pe["chunk"], NCH + x + 1)
                a.activation(u_half(x, 1), bank[:, 4 + x, 0:HALF], ACT.Copy).then_inc(ac["u_in"], 1)
            high(0, 0, False)
            high(1, 1, False)
            for x in range(NCH):
                u_there(x)
                a.activation(x3[:, x, :], u_in(x), ACT.Copy, scale=0.3).then_inc(ac["x3"], 1)
            evac1(1, 0)
            for k in range(1, LOOP_FROM):
                slot_step(k, k % 2, True, k > 1, (k + 1) % NCH, True)
            with a.Fori(1, LOOPS + 1) as i:
                for m in range(NCH):
                    slot_step(i * NCH + (m + 3), (m + 3) % 2, True, True, m, True)
            for k in range(LOOP_END, SLOTS + 2):
                slot_step(k, k % 2, k <= SLOTS, True, (k + 1) % NCH if k + 1 < SLOTS else None, k < SLOTS)

        @block.gpsimd
        def _(p):
            p.memset(xa[:, :], 0.0).then_inc(po["zero"], 1)
            p.wait_ge(pe["scores"], 4)
            p.memset(reg_d[:, :], 0.0).then_inc(po["zero"], 1)
            p.wait_ge(pe["attn"], 4)
            p.wait_ge(ve["xw"], 1)
            for m in range(NSLOT):
                n = V_FIRST + m
                p.tensor_copy(stat_v[m], xw[:, n * KC * B:n * KC * B + STATF]).then_inc(po["stat"], 1)
            with p.Fori(1, (NV - V_FIRST) // NSLOT) as i:
                for m in range(NSLOT):
                    p.wait_ge(pe["slot_used"], i * NSLOT + (U_PREFIX + m - NSLOT + 1))
                    p.tensor_copy(stat_v[m], xw[:, bass.ds(i * (NSLOT * KC * B) + (V_FIRST + m) * KC * B, STATF)])\
                        .then_inc(po["stat"], 1)
            p.wait_ge(ve["img"], TT)
            p.memset(bands, 0.0).then_inc(po["bandz"], 1)
            p.wait_ge(po["bandz"], 1)
            for r in range(RG):
                p.dma_start(bands[r * C:(r + 1) * C, :, r * C:(r + 3) * C],
                            conv_band.rearrange("c (m n) -> c m n", n=3 * C)).then_inc(ld_band, 16)
            p.wait_ge(pe["slot_used"], U_V)
            p.memset(hmats, 0.0).then_inc(po["bandz"], 1)
            p.wait_ge(po["bandz"], 2)
            halo_src = conv_halo.rearrange("c (s m n) -> c s m n", s=2, n=C)
            for dw in range(3):
                q0, shift = dw * QUAD, slice(dw * C, (dw + 1) * C)
                p.dma_start(hmats[q0 + C:q0 + 2 * C, 0:NCONV, 0:C], halo_src[shift, 0]).then_inc(ld_band, 16)
                p.dma_start(hmats[q0 + C:q0 + 2 * C, NCONV:, 0:C], halo_src[shift, 0]).then_inc(ld_band, 16)
                p.dma_start(hmats[q0:q0 + C, 0:NCONV, P - C:P], halo_src[shift, 1]).then_inc(ld_band, 16)
            p.memset(reg_e[:, :], 0.0).then_inc(po["zero"], 1)
            p.wait_ge(ve["pf"], 4)
            p.memset(reg_f[:, :], 0.0).then_inc(po["zero"], 1)
            p.tensor_copy(pick.rearrange("p (x r c) -> p x r c", x=NCH, c=CC),
                          ident.rearrange("p (r x c) -> p x r c", x=NCH, c=CC)).then_inc(po["pick"], 1)
            p.memset(reg_a[:, :], 0.0).then_inc(po["padz"], 1)
            p.memset(reg_g[:, :], 0.0).then_inc(po["padz"], 1)
            p.wait_ge(ld_vm, 32)
            p.tensor_copy(vmr[:, :], vm).then_inc(po["vm"], 1)

            def low(k, c, later=True):
                p.wait_ge(ac["hi"], k + 1)
                at = slice(B, (S + 1) * B) if later else slice(0, ROWF)
                p.tensor_tensor(u_lo[c][:, at], u[c][:, at], u_hi[c][:, at].bitcast(F32),
                                ALU.subtract).then_inc(po["lo"], 1)

            def slot_step(k, q, c, later=True):
                p.wait_ge(ve["clip1"], k)
                p.tensor_tensor(cxy[q], fld[q][:, 0:NF], fld[q][:, NF:2 * NF], ALU.mult).then_inc(po["cxy"], 1)
                p.wait_ge(ve["clip2"], k)
                p.tensor_tensor(mxy[q], fld[q][:, 3 * NF:4 * NF], fld[q][:, 4 * NF:5 * NF], ALU.mult).then_inc(po["m"], 1)
                p.wait_ge(po["m"], k)
                p.wait_ge(ac["sqr"], k)
                p.tensor_tensor(num[q][:, 0:NF], mxy[q], sqs[q][:, 2 * NF:3 * NF], ALU.subtract).then_inc(po["nk"], 1)
                p.wait_ge(ve["outer"], k)
                p.tensor_tensor(abs_[q], ab[q][:, 0:NF], ab[q][:, NF:2 * NF], ALU.add).then_inc(po["absum"], 1)
                if c is not None:
                    low(k + 1, c, later)
                p.wait_ge(ve["cross"], k)
                p.wait_ge(po["absum"], k)
                p.tensor_tensor(num[q][:, NF:2 * NF], abs_[q], cxy[q], ALU.add).then_inc(po["hn"], 1)

            low(0, 0, False)
            low(1, 1, False)
            for k in range(1, LOOP_FROM):
                slot_step(k, (k - 1) % 2, (k + 1) % NCH, k + 1 >= NCH)
            with p.Fori(1, LOOPS + 1) as i:
                for m in range(NCH):
                    slot_step(i * NCH + (m + 3), m % 2, m)
            for k in range(LOOP_END, SLOTS + 1):
                slot_step(k, (k - 1) % 2, (k + 1) % NCH if k + 1 < SLOTS else None)
    return nc


def vertical_operators(np):
    sv = np.eye(S) * 2 + np.eye(S, k=1) + np.eye(S, k=-1)
    dv = np.eye(S, k=1) - np.eye(S, k=-1)
    edge = np.eye(S)
    edge[0], edge[S - 1] = edge[1], edge[S - 2]
    ops = {"SV": sv / 8, "DV": dv / 8, "SS": sv @ sv / 64, "DS": dv @ sv / 64, "DD": dv @ dv / 64}

    def op(name):
        factor = name[:-2]
        return {"": 1, "-": -1}.get(factor) or int(factor), ops[name[-2:]]

    four = lambda m: np.kron(m.T, np.eye(CC))
    mats = [four(op(n)[0] * op(n)[1]) for n in MATS] + [four(op(n)[0] * op(n)[1] @ edge) for n in MATS]
    return (np.concatenate(mats, 1).astype(np.float32), four(edge).astype(np.float32))


def kernel(**inputs):
    import numpy as np
    import concourse.bacc as bacc
    from concourse.bass_utils import run_bass_kernel_spmd

    a = {k: np.asarray(v) for k, v in inputs.items()}
    x = a["x"]
    d = {}
    x8 = x.reshape(TT, BL, C, PPW, PS, PPW, PS)
    d["x_patch"] = x8.transpose(4, 6, 2, 0, 5, 3, 1).reshape(P, KC * TOK)
    d["x_window"] = x.transpose(2, 3, 1, 0).reshape(P, P * B)
    d["x_conv"] = x.reshape(B, C, G, RG, S).transpose(3, 1, 2, 4, 0).reshape(P, G * ROW)
    L0 = {k[len("L0_conv_"):]: v for k, v in a.items() if k.startswith("L0_conv_")}
    d["wqk_p"], d["wv_p"], d["wout_p"] = L0["Wqk_p"], L0["Wv_p"], L0["Wout_p"]
    d["wqk_w"] = L0["Wqk_w"].reshape(32, 4, KC, 2, PD).transpose(3, 1, 0, 2, 4).reshape(2, P, SLOTF)
    d["wv_w"] = L0["Wv_w"].reshape(P, NV, SLOTF).transpose(1, 0, 2)
    d["wout_w"] = L0["Wout_w"].reshape(4, KC, 32, G, 4, 2, 4, 8, C).transpose(6, 3, 0, 2, 1, 4, 7, 5, 8)\
        .reshape(NO, P, SLOTF)
    by_quadrant = lambda t: np.broadcast_to(t.reshape(1, 4, 32).transpose(0, 2, 1)[:, :, None, :], (4, 32, 2, 4)).reshape(P, KC)
    conv_w = np.stack([a[f"L{l}_conv_w{i}"] for l in (1, 2) for i in (1, 2)])
    conv_b = np.stack([a[f"L{l}_conv_b{i}"] for l in (1, 2) for i in (1, 2)])
    d["conv_band"] = conv_w[:, :, :, ::-1, :].transpose(2, 0, 4, 3, 1).reshape(C, 3 * NCONV * 3 * C)
    d["conv_halo"] = conv_w[:, :, :, 0::2, :].transpose(4, 2, 3, 0, 1).reshape(3 * C, 2 * NCONV * C)
    tok = np.arange(P)
    rows = tok // 4
    pooled_at = np.arange(P) % 32
    cols = {
        "pn_g": L0["pn_g"].reshape(P, KC), "pn_b": L0["pn_b"].reshape(P, KC),
        "pln_g": L0["pln_g"].reshape(32, 4, KC).transpose(1, 0, 2).reshape(P, KC),
        "pln_b": L0["pln_b"].reshape(32, 4, KC).transpose(1, 0, 2).reshape(P, KC),
        "wn_g": L0["wn_g"].reshape(P, P), "wn_b": L0["wn_b"].reshape(P, P),
        "cp_w": L0["conv_p_w"].reshape(DH, 9), "cp_b": L0["conv_p_b"].reshape(DH, 1),
        "cw_w": by_quadrant(L0["conv_w_w"][:, 0, 1, 1]), "cw_b": by_quadrant(L0["conv_w_b"]),
        "conv_b": np.tile(conv_b.T, (RG, 1)),
        "alpha": np.broadcast_to(a["L3_conv_alpha_param"].reshape(1, 1), (P, 1)),
        "beta": np.broadcast_to(a["L3_conv_beta_param"].reshape(1, 1), (P, 1)),
        "ident": np.eye(P, dtype=np.float32),
        "mask": np.where(tok[:, None] % BL == tok[None] % BL, 0.0, -1e30).astype(np.float32),
        "pool": (((rows // 4)[:, None] * 4 + (tok % 4)[:, None]) == pooled_at[None]).astype(np.float32) / 16,
    }
    d["params"] = np.concatenate([cols[n] for n, _ in PARAMS], 1)
    d["vmats"], d["edge"] = vertical_operators(np)

    nc = bacc.Bacc("TRN2", target_bir_lowering=False, num_devices=1)
    arrays, args = {}, []
    for n in ("x_patch", "x_window", "x_conv", "params", "wqk_p", "wv_p", "wout_p", "wqk_w", "wv_w", "wout_w",
              "conv_band", "conv_halo", "vmats", "edge"):
        arrays[n] = np.ascontiguousarray(d[n])
        assert arrays[n].dtype == np.float32, n
        args.append(nc.dram_tensor(n, arrays[n].shape, F32, kind="ExternalInput").ap())
    args.append(nc.dram_tensor("out", (NCH * P, ROW), F32, kind="ExternalOutput").ap())
    build(nc, *args)
    r = run_bass_kernel_spmd(nc, [arrays], core_ids=[0])
    y = r.results[0]["out"].reshape(NCH, G, RG, CC, S, B)
    return y.transpose(5, 0, 3, 1, 2, 4).reshape(B, C, S, S)
```
